# Optimizing a Trainium2 kernel written in Bass

```python
import numpy as np
import jax
import jax.numpy as jnp

def _softmax(x, axis=-1):
    return jax.nn.softmax(x, axis=axis)

def _gelu(x):
    return jax.nn.gelu(x, approximate=True)

def _silu(x):
    return jax.nn.silu(x)

def _sigmoid(x):
    return jax.nn.sigmoid(x)

def _layernorm(x, axis=-1, eps=1e-05):
    m = jnp.mean(x, axis=axis, keepdims=True)
    v = jnp.var(x, axis=axis, keepdims=True)
    return (x - m) / jnp.sqrt(v + eps)

def _scatter_add(tgt, idx, src, axis=0):
    return tgt.at[idx].add(src)

def _segment_sum(src, seg, n):
    return jax.ops.segment_sum(src, seg, n)
kernel_name = 'mk_early_fusion_embed_d1_tok_img768_r4_5ec75c'

def setup_inputs(seed: int=0):
    np.random.seed(seed)
    _w = jnp.asarray

    def _rec_inputs():
        import jax
        import jax.numpy as jnp
        _rk = jax.random.key(seed)
        x = -0.000348323 + 0.999952 * jax.random.normal(jax.random.fold_in(_rk, 1), (32, 3, 96, 96), jnp.float32)
        x_txt = jax.random.randint(jax.random.fold_in(_rk, 51), (32, 128), 0, 31993, jnp.int32)
        mask_BS_i1_0 = jnp.where(jnp.ones((32, 128), dtype=bool), 1, 0).astype(jnp.int32)
        return (x, x_txt, mask_BS_i1_0)
    x, x_txt, mask_BS_i1_0 = _rec_inputs()

    def _L0_tok_setup():
        import jax, jax.numpy as jnp
        import numpy as np
        PATCH = 16

        def _shifted_concat(x):
            B, C, H, W = x.shape
            xp = jnp.pad(x, ((0, 0), (0, 0), (1, 1), (1, 1)))
            right = xp[:, :, 1:1 + H, 0:W]
            left = xp[:, :, 1:1 + H, 2:2 + W]
            down = xp[:, :, 0:H, 1:1 + W]
            up = xp[:, :, 2:2 + H, 1:1 + W]
            return jnp.concatenate([x, right, left, down, up], axis=1)

        def _patchify(x, p):
            B, C, H, W = x.shape
            h, w = (H // p, W // p)
            x = x.reshape(B, C, h, p, w, p)
            x = x.transpose(0, 2, 4, 3, 5, 1)
            return x.reshape(B, h * w, p * p * C)

        def _layernorm(x, gamma, beta, eps=1e-05):
            mu = jnp.mean(x, axis=-1, keepdims=True)
            var = jnp.var(x, axis=-1, keepdims=True)
            return (x - mu) * jax.lax.rsqrt(var + eps) * gamma + beta
        key = jax.random.key(seed)
        k1, k2 = jax.random.split(key)
        B, H, W = (32, 96, 96)
        patch_dim = PATCH * PATCH * 15
        d_hidn = 192
        x = jax.random.normal(k1, (B, 3, H, W), dtype=jnp.float32)
        gamma = jnp.ones((patch_dim,), dtype=jnp.float32)
        beta = jnp.zeros((patch_dim,), dtype=jnp.float32)
        W_ = jax.random.normal(k2, (patch_dim, d_hidn), dtype=jnp.float32) * patch_dim ** (-0.5)
        b = jnp.zeros((d_hidn,), dtype=jnp.float32)
        return {'x': x, 'gamma': gamma, 'beta': beta, 'W': W_, 'b': b}
    _L0_tok_all = _L0_tok_setup()
    _L0_tok_in = {k: v for k, v in _L0_tok_all.items() if k in ('gamma', 'beta', 'W', 'b')}
    del _L0_tok_all

    def _L0_txt_setup():
        import jax, jax.numpy as jnp
        import numpy as np
        NH = 12
        W = 64
        EPS = 1e-12

        def layer_norm(x, s, b):
            mu = x.mean(-1, keepdims=True)
            var = ((x - mu) ** 2).mean(-1, keepdims=True)
            return (x - mu) / jnp.sqrt(var + EPS) * s + b

        def band_attention(q, k, v, mask):
            B, H, S, d = q.shape
            nc = S // W
            kp = jnp.pad(k, ((0, 0), (0, 0), (W, W), (0, 0)))
            vp = jnp.pad(v, ((0, 0), (0, 0), (W, W), (0, 0)))
            idx = jnp.arange(nc)[:, None] * W + jnp.arange(3 * W)[None, :]
            kb = kp[:, :, idx]
            vb = vp[:, :, idx]
            qc = q.reshape(B, H, nc, W, d)
            scores = jnp.einsum('bhcqd,bhckd->bhcqk', qc, kb) / jnp.sqrt(jnp.asarray(d, q.dtype))
            rel = jnp.arange(3 * W)[None, :] - W - jnp.arange(W)[:, None]
            band_ok = jnp.abs(rel) <= W
            key_abs = idx - W
            pos_ok = (key_abs >= 0) & (key_abs < S)
            mp = jnp.pad(mask, ((0, 0), (W, W)))
            mb = mp[:, idx] > 0
            allowed = mb[:, None, :, None, :] & pos_ok[None, None, :, None, :] & band_ok[None, None, None, :, :]
            scores = jnp.where(allowed, scores, jnp.asarray(-1000000000.0, scores.dtype))
            probs = jax.nn.softmax(scores, axis=-1)
            out = jnp.einsum('bhcqk,bhckd->bhcqd', probs, vb)
            return out.reshape(B, H, S, d)

        def _forward(input_ids, attention_mask, emb_word, emb_pos, emb_ln_s, emb_ln_b, Wq, bq, Wk, bk, Wv, bv, Wo, bo, ln1_s, ln1_b, W1, b1, W2, b2, ln2_s, ln2_b):
            B, S = input_ids.shape
            Hd = emb_word.shape[1]
            dh = Hd // NH
            mask = attention_mask.astype(emb_word.dtype)
            h = layer_norm(emb_word[input_ids] + emb_pos[:S][None], emb_ln_s, emb_ln_b)
            L = Wq.shape[0]
            for l in range(L):

                def heads(x):
                    return x.reshape(B, S, NH, dh).transpose(0, 2, 1, 3)
                q = heads(h @ Wq[l] + bq[l])
                k = heads(h @ Wk[l] + bk[l])
                v = heads(h @ Wv[l] + bv[l])
                a = band_attention(q, k, v, mask)
                a = a.transpose(0, 2, 1, 3).reshape(B, S, Hd)
                h = layer_norm(h + a @ Wo[l] + bo[l], ln1_s[l], ln1_b[l])
                f = jax.nn.gelu(h @ W1[l] + b1[l], approximate=False)
                h = layer_norm(h + f @ W2[l] + b2[l], ln2_s[l], ln2_b[l])
            return h
        key = jax.random.key(seed)
        B, S, Hd, L, V, FF = (2, 1024, 192, 4, 8000, 4 * 192)
        ks = jax.random.split(key, 16)
        std = 0.02
        inp = {'input_ids': jax.random.randint(ks[0], (B, S), 0, V, dtype=jnp.int64) if jax.config.jax_enable_x64 else jax.random.randint(ks[0], (B, S), 0, V, dtype=jnp.int32), 'attention_mask': jnp.ones((B, S), dtype=jnp.int32), 'emb_word': jax.random.normal(ks[1], (V, Hd), jnp.float32) * std, 'emb_pos': jax.random.normal(ks[2], (S, Hd), jnp.float32) * std, 'emb_ln_s': jnp.ones((Hd,), jnp.float32), 'emb_ln_b': jnp.zeros((Hd,), jnp.float32), 'Wq': jax.random.normal(ks[3], (L, Hd, Hd), jnp.float32) * std, 'bq': jnp.zeros((L, Hd), jnp.float32), 'Wk': jax.random.normal(ks[4], (L, Hd, Hd), jnp.float32) * std, 'bk': jnp.zeros((L, Hd), jnp.float32), 'Wv': jax.random.normal(ks[5], (L, Hd, Hd), jnp.float32) * std, 'bv': jnp.zeros((L, Hd), jnp.float32), 'Wo': jax.random.normal(ks[6], (L, Hd, Hd), jnp.float32) * std, 'bo': jnp.zeros((L, Hd), jnp.float32), 'ln1_s': jnp.ones((L, Hd), jnp.float32), 'ln1_b': jnp.zeros((L, Hd), jnp.float32), 'W1': jax.random.normal(ks[7], (L, Hd, FF), jnp.float32) * std, 'b1': jnp.zeros((L, FF), jnp.float32), 'W2': jax.random.normal(ks[8], (L, FF, Hd), jnp.float32) * std, 'b2': jnp.zeros((L, Hd), jnp.float32), 'ln2_s': jnp.ones((L, Hd), jnp.float32), 'ln2_b': jnp.zeros((L, Hd), jnp.float32)}
        return inp
    _L0_txt_all = _L0_txt_setup()
    _L0_txt_in = {k: v for k, v in _L0_txt_all.items() if k in ('emb_word', 'emb_pos', 'emb_ln_s', 'emb_ln_b', 'Wq', 'bq', 'Wk', 'bk', 'Wv', 'bv', 'Wo', 'bo', 'ln1_s', 'ln1_b', 'W1', 'b1', 'W2', 'b2', 'ln2_s', 'ln2_b')}
    del _L0_txt_all

    def _L0_attn_setup():
        import jax, jax.numpy as jnp
        import numpy as np
        D_MODEL = 192
        D_STATE = 16
        K_CONV = 4
        BATCH = 2
        SEQ = 512

        def _forward(x, Wi, bi, Wconv, bconv, Wdt, bdt, WB, bB, WC, bC, A_log, D, Wo, bo):
            B, L, dm = x.shape
            ds = A_log.shape[1]
            K = Wconv.shape[1]
            uv = x @ Wi + bi
            u, v = (uv[..., :dm], uv[..., dm:])
            u_pad = jnp.pad(u, ((0, 0), (K - 1, 0), (0, 0)))
            u_conv = bconv + sum((u_pad[:, k:k + L, :] * Wconv[:, k] for k in range(K)))
            dt = jax.nn.softplus(u_conv @ Wdt + bdt)
            Bt = (u_conv @ WB + bB).reshape(B, L, dm, ds)
            Ct = (u_conv @ WC + bC).reshape(B, L, dm, ds)
            A = -jnp.exp(A_log)

            def step(s, inputs):
                dt_t, u_t, B_tt, C_tt = inputs
                dt_e = dt_t[..., None]
                s = s * jnp.exp(dt_e * A) + dt_e * B_tt * u_t[..., None]
                y = jnp.sum(C_tt * s, axis=-1) + D * u_t
                return (s, y)
            s0 = jnp.zeros((B, dm, ds), x.dtype)
            xs = (dt.transpose(1, 0, 2), u_conv.transpose(1, 0, 2), Bt.transpose(1, 0, 2, 3), Ct.transpose(1, 0, 2, 3))
            _, ys = jax.lax.scan(step, s0, xs)
            y = ys.transpose(1, 0, 2)
            y = y * jax.nn.sigmoid(v)
            return y @ Wo + bo
        key = jax.random.key(seed)
        ks = jax.random.split(key, 16)
        dm, ds, K = (D_MODEL, D_STATE, K_CONV)
        s = 0.02
        inp = {'x': jax.random.normal(ks[0], (BATCH, SEQ, dm), dtype=jnp.float32), 'Wi': jax.random.normal(ks[1], (dm, 2 * dm), dtype=jnp.float32) * s, 'bi': jnp.zeros((2 * dm,), jnp.float32), 'Wconv': jax.random.normal(ks[2], (dm, K), dtype=jnp.float32) * s, 'bconv': jnp.zeros((dm,), jnp.float32), 'Wdt': jax.random.normal(ks[3], (dm, dm), dtype=jnp.float32) * s, 'bdt': jnp.zeros((dm,), jnp.float32), 'WB': jax.random.normal(ks[4], (dm, dm * ds), dtype=jnp.float32) * s, 'bB': jnp.zeros((dm * ds,), jnp.float32), 'WC': jax.random.normal(ks[5], (dm, dm * ds), dtype=jnp.float32) * s, 'bC': jnp.zeros((dm * ds,), jnp.float32), 'A_log': jnp.zeros((dm, ds), jnp.float32), 'D': jnp.ones((dm,), jnp.float32), 'Wo': jax.random.normal(ks[6], (dm, dm), dtype=jnp.float32) * s, 'bo': jnp.zeros((dm,), jnp.float32)}
        return inp
    _L0_attn_all = _L0_attn_setup()
    _L0_attn_in = {k: v for k, v in _L0_attn_all.items() if k in ('Wi', 'bi', 'Wconv', 'bconv', 'Wdt', 'bdt', 'WB', 'bB', 'WC', 'bC', 'A_log', 'D', 'Wo', 'bo')}
    del _L0_attn_all

    def _L0_ffn_setup():
        import jax, jax.numpy as jnp
        import numpy as np
        EPS = 1e-06

        def l2_normalize(x, axis):
            norm = jnp.sqrt(jnp.square(x).sum(axis=axis, keepdims=True))
            return x * (1.0 / (norm + EPS))
        key = jax.random.key(seed)
        ks = jax.random.split(key, 8)
        b, m, d = (32, 256, 192)
        n, p = (8, 4)
        h = d // 8
        X = jax.random.normal(ks[0], (b, m, d), dtype=jnp.float32)
        std_slot = float(np.sqrt(2.0 / (d + n * p)))
        slot_params = jax.random.normal(ks[1], (d, n, p), dtype=jnp.float32) * std_slot
        scale = jnp.ones((), dtype=jnp.float32)
        W_down = jax.random.normal(ks[2], (n, d, h), dtype=jnp.float32) * float(np.sqrt(1.0 / d))
        b_down = jnp.zeros((n, h), dtype=jnp.float32)
        W_up = jax.random.normal(ks[3], (n, h, d), dtype=jnp.float32) * float(np.sqrt(1.0 / h))
        b_up = jnp.zeros((n, d), dtype=jnp.float32)
        return {'X': X, 'slot_params': slot_params, 'scale': scale, 'W_down': W_down, 'b_down': b_down, 'W_up': W_up, 'b_up': b_up}
    _L0_ffn_all = _L0_ffn_setup()
    _L0_ffn_in = {k: v for k, v in _L0_ffn_all.items() if k in ('slot_params', 'scale', 'W_down', 'b_down', 'W_up', 'b_up')}
    del _L0_ffn_all
    return {'x': x, 'x_txt': x_txt, 'mask_BS_i1_0': mask_BS_i1_0, 'L0_tok_gamma': _L0_tok_in['gamma'], 'L0_tok_beta': _L0_tok_in['beta'], 'L0_tok_W': _L0_tok_in['W'], 'L0_tok_b': _L0_tok_in['b'], 'L0_txt_emb_word': _L0_txt_in['emb_word'], 'L0_txt_emb_pos': _L0_txt_in['emb_pos'], 'L0_txt_emb_ln_s': _L0_txt_in['emb_ln_s'], 'L0_txt_emb_ln_b': _L0_txt_in['emb_ln_b'], 'L0_txt_Wq': _L0_txt_in['Wq'], 'L0_txt_bq': _L0_txt_in['bq'], 'L0_txt_Wk': _L0_txt_in['Wk'], 'L0_txt_bk': _L0_txt_in['bk'], 'L0_txt_Wv': _L0_txt_in['Wv'], 'L0_txt_bv': _L0_txt_in['bv'], 'L0_txt_Wo': _L0_txt_in['Wo'], 'L0_txt_bo': _L0_txt_in['bo'], 'L0_txt_ln1_s': _L0_txt_in['ln1_s'], 'L0_txt_ln1_b': _L0_txt_in['ln1_b'], 'L0_txt_W1': _L0_txt_in['W1'], 'L0_txt_b1': _L0_txt_in['b1'], 'L0_txt_W2': _L0_txt_in['W2'], 'L0_txt_b2': _L0_txt_in['b2'], 'L0_txt_ln2_s': _L0_txt_in['ln2_s'], 'L0_txt_ln2_b': _L0_txt_in['ln2_b'], 'L0_attn_Wi': _L0_attn_in['Wi'], 'L0_attn_bi': _L0_attn_in['bi'], 'L0_attn_Wconv': _L0_attn_in['Wconv'], 'L0_attn_bconv': _L0_attn_in['bconv'], 'L0_attn_Wdt': _L0_attn_in['Wdt'], 'L0_attn_bdt': _L0_attn_in['bdt'], 'L0_attn_WB': _L0_attn_in['WB'], 'L0_attn_bB': _L0_attn_in['bB'], 'L0_attn_WC': _L0_attn_in['WC'], 'L0_attn_bC': _L0_attn_in['bC'], 'L0_attn_A_log': _L0_attn_in['A_log'], 'L0_attn_D': _L0_attn_in['D'], 'L0_attn_Wo': _L0_attn_in['Wo'], 'L0_attn_bo': _L0_attn_in['bo'], 'L0_ffn_slot_params': _L0_ffn_in['slot_params'], 'L0_ffn_scale': _L0_ffn_in['scale'], 'L0_ffn_W_down': _L0_ffn_in['W_down'], 'L0_ffn_b_down': _L0_ffn_in['b_down'], 'L0_ffn_W_up': _L0_ffn_in['W_up'], 'L0_ffn_b_up': _L0_ffn_in['b_up']}

def reference(x, x_txt, mask_BS_i1_0, L0_tok_gamma, L0_tok_beta, L0_tok_W, L0_tok_b, L0_txt_emb_word, L0_txt_emb_pos, L0_txt_emb_ln_s, L0_txt_emb_ln_b, L0_txt_Wq, L0_txt_bq, L0_txt_Wk, L0_txt_bk, L0_txt_Wv, L0_txt_bv, L0_txt_Wo, L0_txt_bo, L0_txt_ln1_s, L0_txt_ln1_b, L0_txt_W1, L0_txt_b1, L0_txt_W2, L0_txt_b2, L0_txt_ln2_s, L0_txt_ln2_b, L0_attn_Wi, L0_attn_bi, L0_attn_Wconv, L0_attn_bconv, L0_attn_Wdt, L0_attn_bdt, L0_attn_WB, L0_attn_bB, L0_attn_WC, L0_attn_bC, L0_attn_A_log, L0_attn_D, L0_attn_Wo, L0_attn_bo, L0_ffn_slot_params, L0_ffn_scale, L0_ffn_W_down, L0_ffn_b_down, L0_ffn_W_up, L0_ffn_b_up):
    import jax
    import jax.numpy as jnp

    def _L0_tok_ref(x, gamma, beta, W, b):
        import jax, jax.numpy as jnp
        import numpy as np
        PATCH = 16

        def _shifted_concat(x):
            B, C, H, W = x.shape
            xp = jnp.pad(x, ((0, 0), (0, 0), (1, 1), (1, 1)))
            right = xp[:, :, 1:1 + H, 0:W]
            left = xp[:, :, 1:1 + H, 2:2 + W]
            down = xp[:, :, 0:H, 1:1 + W]
            up = xp[:, :, 2:2 + H, 1:1 + W]
            return jnp.concatenate([x, right, left, down, up], axis=1)

        def _patchify(x, p):
            B, C, H, W = x.shape
            h, w = (H // p, W // p)
            x = x.reshape(B, C, h, p, w, p)
            x = x.transpose(0, 2, 4, 3, 5, 1)
            return x.reshape(B, h * w, p * p * C)

        def _layernorm(x, gamma, beta, eps=1e-05):
            mu = jnp.mean(x, axis=-1, keepdims=True)
            var = jnp.var(x, axis=-1, keepdims=True)
            return (x - mu) * jax.lax.rsqrt(var + eps) * gamma + beta
        xs = _shifted_concat(x)
        tokens = _patchify(xs, PATCH)
        normed = _layernorm(tokens, gamma, beta)
        return jnp.einsum('bnd,de->bne', normed, W) + b

    def _L0_txt_ref(input_ids, attention_mask, emb_word, emb_pos, emb_ln_s, emb_ln_b, Wq, bq, Wk, bk, Wv, bv, Wo, bo, ln1_s, ln1_b, W1, b1, W2, b2, ln2_s, ln2_b):
        import jax, jax.numpy as jnp
        import numpy as np
        NH = 12
        W = 64
        EPS = 1e-12

        def layer_norm(x, s, b):
            mu = x.mean(-1, keepdims=True)
            var = ((x - mu) ** 2).mean(-1, keepdims=True)
            return (x - mu) / jnp.sqrt(var + EPS) * s + b

        def band_attention(q, k, v, mask):
            B, H, S, d = q.shape
            nc = S // W
            kp = jnp.pad(k, ((0, 0), (0, 0), (W, W), (0, 0)))
            vp = jnp.pad(v, ((0, 0), (0, 0), (W, W), (0, 0)))
            idx = jnp.arange(nc)[:, None] * W + jnp.arange(3 * W)[None, :]
            kb = kp[:, :, idx]
            vb = vp[:, :, idx]
            qc = q.reshape(B, H, nc, W, d)
            scores = jnp.einsum('bhcqd,bhckd->bhcqk', qc, kb) / jnp.sqrt(jnp.asarray(d, q.dtype))
            rel = jnp.arange(3 * W)[None, :] - W - jnp.arange(W)[:, None]
            band_ok = jnp.abs(rel) <= W
            key_abs = idx - W
            pos_ok = (key_abs >= 0) & (key_abs < S)
            mp = jnp.pad(mask, ((0, 0), (W, W)))
            mb = mp[:, idx] > 0
            allowed = mb[:, None, :, None, :] & pos_ok[None, None, :, None, :] & band_ok[None, None, None, :, :]
            scores = jnp.where(allowed, scores, jnp.asarray(-1000000000.0, scores.dtype))
            probs = jax.nn.softmax(scores, axis=-1)
            out = jnp.einsum('bhcqk,bhckd->bhcqd', probs, vb)
            return out.reshape(B, H, S, d)

        def _forward(input_ids, attention_mask, emb_word, emb_pos, emb_ln_s, emb_ln_b, Wq, bq, Wk, bk, Wv, bv, Wo, bo, ln1_s, ln1_b, W1, b1, W2, b2, ln2_s, ln2_b):
            B, S = input_ids.shape
            Hd = emb_word.shape[1]
            dh = Hd // NH
            mask = attention_mask.astype(emb_word.dtype)
            h = layer_norm(emb_word[input_ids] + emb_pos[:S][None], emb_ln_s, emb_ln_b)
            L = Wq.shape[0]
            for l in range(L):

                def heads(x):
                    return x.reshape(B, S, NH, dh).transpose(0, 2, 1, 3)
                q = heads(h @ Wq[l] + bq[l])
                k = heads(h @ Wk[l] + bk[l])
                v = heads(h @ Wv[l] + bv[l])
                a = band_attention(q, k, v, mask)
                a = a.transpose(0, 2, 1, 3).reshape(B, S, Hd)
                h = layer_norm(h + a @ Wo[l] + bo[l], ln1_s[l], ln1_b[l])
                f = jax.nn.gelu(h @ W1[l] + b1[l], approximate=False)
                h = layer_norm(h + f @ W2[l] + b2[l], ln2_s[l], ln2_b[l])
            return h
        return _forward(input_ids, attention_mask, emb_word, emb_pos, emb_ln_s, emb_ln_b, Wq, bq, Wk, bk, Wv, bv, Wo, bo, ln1_s, ln1_b, W1, b1, W2, b2, ln2_s, ln2_b)

    def _L0_attn_ref(x, Wi, bi, Wconv, bconv, Wdt, bdt, WB, bB, WC, bC, A_log, D, Wo, bo):
        import jax, jax.numpy as jnp
        import numpy as np
        D_MODEL = 192
        D_STATE = 16
        K_CONV = 4
        BATCH = 2
        SEQ = 512

        def _forward(x, Wi, bi, Wconv, bconv, Wdt, bdt, WB, bB, WC, bC, A_log, D, Wo, bo):
            B, L, dm = x.shape
            ds = A_log.shape[1]
            K = Wconv.shape[1]
            uv = x @ Wi + bi
            u, v = (uv[..., :dm], uv[..., dm:])
            u_pad = jnp.pad(u, ((0, 0), (K - 1, 0), (0, 0)))
            u_conv = bconv + sum((u_pad[:, k:k + L, :] * Wconv[:, k] for k in range(K)))
            dt = jax.nn.softplus(u_conv @ Wdt + bdt)
            Bt = (u_conv @ WB + bB).reshape(B, L, dm, ds)
            Ct = (u_conv @ WC + bC).reshape(B, L, dm, ds)
            A = -jnp.exp(A_log)

            def step(s, inputs):
                dt_t, u_t, B_tt, C_tt = inputs
                dt_e = dt_t[..., None]
                s = s * jnp.exp(dt_e * A) + dt_e * B_tt * u_t[..., None]
                y = jnp.sum(C_tt * s, axis=-1) + D * u_t
                return (s, y)
            s0 = jnp.zeros((B, dm, ds), x.dtype)
            xs = (dt.transpose(1, 0, 2), u_conv.transpose(1, 0, 2), Bt.transpose(1, 0, 2, 3), Ct.transpose(1, 0, 2, 3))
            _, ys = jax.lax.scan(step, s0, xs)
            y = ys.transpose(1, 0, 2)
            y = y * jax.nn.sigmoid(v)
            return y @ Wo + bo
        return _forward(x, Wi, bi, Wconv, bconv, Wdt, bdt, WB, bB, WC, bC, A_log, D, Wo, bo)

    def _L0_ffn_ref(X, slot_params, scale, W_down, b_down, W_up, b_up):
        import jax, jax.numpy as jnp
        import numpy as np
        EPS = 1e-06

        def l2_normalize(x, axis):
            norm = jnp.sqrt(jnp.square(x).sum(axis=axis, keepdims=True))
            return x * (1.0 / (norm + EPS))
        b, m, d = X.shape
        _, n, p = slot_params.shape
        Xn = l2_normalize(X, axis=-1)
        sp = l2_normalize(slot_params, axis=1) * scale
        logits = jnp.einsum('bmd,dnp->bmnp', Xn, sp)
        D = jax.nn.softmax(logits, axis=1)
        C = jax.nn.softmax(logits.reshape(b, m, n * p), axis=2).reshape(b, m, n, p)
        X_tilde = jnp.einsum('bmd,bmnp->bnpd', Xn, D)
        H = jax.nn.gelu(jnp.einsum('bnpd,ndh->bnph', X_tilde, W_down) + b_down[None, :, None, :], approximate=False)
        Y_tilde = jnp.einsum('bnph,nhd->bnpd', H, W_up) + b_up[None, :, None, :]
        Y = jnp.einsum('bnpd,bmnp->bmd', Y_tilde, C)
        return Y
    h = _L0_tok_ref(x, L0_tok_gamma, L0_tok_beta, L0_tok_W, L0_tok_b)
    h = jnp.concatenate([h, _L0_txt_ref(x_txt, mask_BS_i1_0, L0_txt_emb_word, L0_txt_emb_pos, L0_txt_emb_ln_s, L0_txt_emb_ln_b, L0_txt_Wq, L0_txt_bq, L0_txt_Wk, L0_txt_bk, L0_txt_Wv, L0_txt_bv, L0_txt_Wo, L0_txt_bo, L0_txt_ln1_s, L0_txt_ln1_b, L0_txt_W1, L0_txt_b1, L0_txt_W2, L0_txt_b2, L0_txt_ln2_s, L0_txt_ln2_b)], axis=1)
    h = h + _L0_attn_ref(_layernorm(h, axis=-1), L0_attn_Wi, L0_attn_bi, L0_attn_Wconv, L0_attn_bconv, L0_attn_Wdt, L0_attn_bdt, L0_attn_WB, L0_attn_bB, L0_attn_WC, L0_attn_bC, L0_attn_A_log, L0_attn_D, L0_attn_Wo, L0_attn_bo)
    h = h + _L0_ffn_ref(_layernorm(h, axis=-1), L0_ffn_slot_params, L0_ffn_scale, L0_ffn_W_down, L0_ffn_b_down, L0_ffn_W_up, L0_ffn_b_up)
    return h

_drawn_inputs = setup_inputs


def setup_inputs(seed=0):
    import zlib

    import numpy as np

    out = dict(_drawn_inputs(seed))
    spreads = {'L0_tok_gamma': (1.0, 0.2),
     'L0_tok_beta': (0.0, 0.1),
     'L0_tok_b': (0.0, 0.1),
     'L0_txt_emb_ln_s': (1.0, 0.2),
     'L0_txt_emb_ln_b': (0.0, 0.1),
     'L0_txt_bq': (0.0, 0.8),
     'L0_txt_bk': (0.0, 2.0),
     'L0_txt_bv': (0.0, 0.1),
     'L0_txt_bo': (0.0, 0.1),
     'L0_txt_ln1_s': (1.0, 0.2),
     'L0_txt_ln1_b': (0.0, 0.1),
     'L0_txt_b1': (0.0, 0.1),
     'L0_txt_b2': (0.0, 0.1),
     'L0_txt_ln2_s': (1.0, 0.2),
     'L0_txt_ln2_b': (0.0, 0.1),
     'L0_attn_bi': (0.0, 0.8),
     'L0_attn_bconv': (0.0, 0.583),
     'L0_attn_bdt': (0.0, 0.8),
     'L0_attn_bB': (0.0, 0.8),
     'L0_attn_bC': (0.0, 0.8),
     'L0_attn_A_log': (0.0, 0.8),
     'L0_attn_D': (1.0, 0.6),
     'L0_attn_bo': (0.0, 2.0),
     'L0_ffn_b_down': (0.0, 2.0),
     'L0_ffn_b_up': (0.0, 2.0)}
    factors = {'L0_txt_Wq': 8.0,
     'L0_txt_Wk': 8.0,
     'L0_attn_Wi': 8.0,
     'L0_attn_Wconv': 8.0,
     'L0_attn_Wdt': 8.0,
     'L0_attn_WB': 8.0,
     'L0_attn_WC': 8.0,
     'L0_attn_Wo': 4.621,
     'L0_ffn_slot_params': 64.0,
     'L0_ffn_W_down': 64.0,
     'L0_ffn_W_up': 14.308}
    for name, (base, spread) in spreads.items():
        noise = np.random.default_rng([zlib.crc32(name.encode()), seed]).standard_normal(out[name].shape)
        drawn = base * np.exp(spread * noise) if base else spread * noise
        out[name] = jnp.asarray(drawn.astype(out[name].dtype))
    for name, factor in factors.items():
        out[name] = (out[name] * factor).astype(out[name].dtype)
    return out
```

```python
from contextlib import ExitStack

import numpy as np

import concourse.bass as bass
from concourse import mybir

ALU = mybir.AluOpType
ACT = mybir.ActivationFunctionType
AX = mybir.AxisListType
F32 = mybir.dt.float32
BF16 = mybir.dt.bfloat16
F16 = mybir.dt.float16
I32 = mybir.dt.int32

P = 128
D = 192
D1 = D - P
B = 32
S = 128
N_IMG = 36
T = N_IMG + S
L = 4
NH = 12
DH = D // NH
FF = 4 * D
NF = FF // P
WIN = 64
N_PAD = WIN
EPS_TXT = 1e-12
EPS = 1e-5
MASKED = -999292928.0
NS = 16
KC = 4
W_SCALE = 64.0
SLOTS = 32
NE = 8
NP_ = 4
HID = 24


HEADS_OF_GROUP = [(0, 1, 8), (2, 3, 10), (4, 5, 9), (6, 7, 11)]


def text_encoder(nc, io, sem, H, consts):
    ident, ident_bf, band, half = (consts[k] for k in ("ident", "ident_bf", "band", "half"))
    with ExitStack() as ctx:
        def sb(name, shape, dt=F32):
            return ctx.enter_context(nc.sbuf_tensor(name, shape, dt))

        def psum(name, shape, dt=F32):
            return ctx.enter_context(nc.psum_tensor(name, shape, dt))

        key_bias = sb("key_bias", [P, B, S], BF16)
        wq0, wq1 = sb("wq0", [P, 3 * P]), sb("wq1", [D1 + 1, 3 * P])
        wk0, wk1 = sb("wk0", [P, 2 * P]), sb("wk1", [D1 + 1, 2 * P])
        wv0, wv1 = sb("wv0", [P, D]), sb("wv1", [D1 + 1, D])
        wo0, wo1 = sb("wo0", [P, D]), sb("wo1", [D1 + 1, D])
        w10, w11 = sb("w10", [P, FF]), sb("w11", [D1 + 1, FF])
        w2 = sb("w2", [P, NF, D])
        b2_rows = sb("b2_rows", [P, D])
        ln1_s, ln1_b = sb("ln1_s", [P, D]), sb("ln1_b", [P, D])
        ln2_s, ln2_b = sb("ln2_s", [P, D]), sb("ln2_b", [P, D])
        xin = sb("xin", [P, D])
        hT0, hT1 = sb("hT0", [P, 2, S]), sb("hT1", [D1 + 1, 2, S])
        v_sb = sb("v_sb", [P, NH, DH + 1])
        oT0, oT1 = sb("oT0", [P, S]), sb("oT1", [D1 + 1, S])
        xres = sb("xres", [P, 2, D])
        stats = sb("stats", [P, 6])
        mv = sb("mv", [P, 2, 2])
        rstd = sb("rstd", [P, 1])
        var_eps = sb("var_eps", [P, 2])
        ln_y = sb("ln_y", [P, 3, D])
        bank = [psum(f"txt_bank{i}", [P, 512]) for i in range(8)]

        def norm_rows(pool, chain, n, x, mean, var_eps, scale, shift, out):
            nc.gpsimd.tensor_tensor(rstd[:], var_eps, half[:], ALU.pow).then_inc(chain, 1)
            nc.gpsimd.tensor_tensor(ln_y[:, 0, :], x, mean.to_broadcast([P, D]), ALU.subtract).then_inc(chain, 1)
            pool.wait_ge(chain, n + 2)
            nc.gpsimd.tensor_tensor(ln_y[:, 1, :], ln_y[:, 0, :], rstd[:].to_broadcast([P, D]), ALU.mult).then_inc(chain, 1)
            pool.wait_ge(chain, n + 3)
            nc.gpsimd.tensor_tensor(ln_y[:, 2, :], ln_y[:, 1, :], scale, ALU.mult).then_inc(chain, 1)
            pool.wait_ge(chain, n + 4)
            return nc.gpsimd.tensor_tensor(out, ln_y[:, 2, :], shift, ALU.add)

        s_const = sem("txt_constants_set")
        with ExitStack() as emb_ctx:
            def tmp(name, shape, dt=F32):
                return emb_ctx.enter_context(nc.sbuf_tensor(name, shape, dt))
            ids = tmp("ids", [P, B], I32)
            ids_f = tmp("ids_f", [P, 3, B])
            rows_of = tmp("rows_of", [P, B], I32)
            pos = tmp("pos", [P, D])
            mask_i = tmp("mask_i", [P, B * S], I32)
            emb_s, emb_b = tmp("emb_s", [P, D]), tmp("emb_b", [P, D])
            s_ids = sem("txt_ids_loaded")
            s_rows = sem("txt_rows_known")
            s_gath = sem("txt_rows_gathered")
            s_loads = sem("txt_small_loads")
            s_dve = sem("txt_dve_steps")
            s_pool = sem("txt_pool_steps")
            s_stat = sem("txt_emb_stats")
            s_emb = sem("txt_embedded")
            with nc.Block() as block:
                @block.sync
                def _(sp):
                    sp.dma_start(ids[:], io["ids"]).then_inc(s_ids, 16)
                    sp.dma_start(pos[:], io["pos"]).then_inc(s_loads, 16)
                    sp.dma_start(emb_s[:], io["emb_ln_s"].partition_broadcast(P)).then_inc(s_loads, 16)
                    sp.dma_start(emb_b[:], io["emb_ln_b"].partition_broadcast(P)).then_inc(s_loads, 16)
                    sp.dma_start(mask_i[:], io["mask"].partition_broadcast(P)).then_inc(s_loads, 16)

                @block.vector
                def _(dve):
                    V = io["emb"].shape[0]
                    dve.wait_ge(s_ids, 16)
                    nc.vector.tensor_copy(ids_f[:, 0, :], ids[:]).then_inc(s_dve, 1)
                    dve.wait_ge(s_dve, 1)
                    nc.vector.tensor_scalar(ids_f[:, 1, :], ids_f[:, 0, :], 0.0, float(V),
                                            ALU.is_lt, ALU.mult).then_inc(s_dve, 1)
                    dve.wait_ge(s_dve, 2)
                    nc.vector.tensor_tensor(ids_f[:, 2, :], ids_f[:, 0, :], ids_f[:, 1, :], ALU.add).then_inc(s_dve, 1)
                    dve.wait_ge(s_dve, 3)
                    nc.vector.tensor_scalar(rows_of[:], ids_f[:, 2, :], 0.0, float(V - 1), ALU.max, ALU.min).then_inc(s_rows, 1)
                    nc.vector.memset(v_sb[:], 1.0)
                    nc.vector.memset(hT1[:], 1.0)
                    nc.vector.memset(oT1[:], 1.0).then_inc(s_const, 1)
                    dve.wait_ge(s_loads, 64)
                    nc.vector.tensor_scalar(key_bias[:].rearrange("p b s -> p (b s)"), mask_i[:], 0.0, MASKED,
                                            ALU.is_le, ALU.mult).then_inc(s_dve, 1)
                    dve.wait_ge(s_dve, 4)
                    nc.vector.tensor_tensor(key_bias[:], key_bias[:], band[:].unsqueeze(1).to_broadcast([P, B, S]),
                                            ALU.min).then_inc(s_dve, 1)
                    dve.wait_ge(s_gath, 16 * B)
                    for b in range(B):
                        if b >= 2:
                            dve.wait_ge(s_emb, b - 1)
                        nc.vector.tensor_tensor(xres[:, b % 2, :], H[:, b, :], pos[:], ALU.add).then_inc(s_dve, 1)
                        dve.wait_ge(s_dve, 6 + 3 * b)
                        nc.vector.bn_stats(stats[:], xres[:, b % 2, :]).then_inc(s_dve, 1)
                        dve.wait_ge(s_dve, 7 + 3 * b)
                        nc.vector.bn_aggr(mv[:, b % 2, :], stats[:]).then_inc(s_dve, 1)
                        dve.wait_ge(s_dve, 8 + 3 * b)
                        nc.vector.tensor_scalar(var_eps[:, b % 2:b % 2 + 1], mv[:, b % 2, 1:2], EPS_TXT, None, ALU.add).then_inc(s_stat, 1)

                @block.gpsimd
                def _(pool):
                    pool.wait_ge(s_rows, 1)
                    for b in range(B):
                        nc.gpsimd.indirect_dma_start(
                            out=H[:, b, :], out_offset=None, in_=io["emb"],
                            in_offset=bass.IndirectOffsetOnAxis(ap=rows_of[:, b:b + 1], axis=0)).then_inc(s_gath, 16)
                    pool.wait_ge(s_loads, 64)
                    for b in range(B):
                        pool.wait_ge(s_stat, b + 1)
                        norm_rows(pool, s_pool, 4 * b, xres[:, b % 2, :], mv[:, b % 2, 0:1], var_eps[:, b % 2:b % 2 + 1],
                                  emb_s[:], emb_b[:], H[:, b, :]).then_inc(s_emb, 1)

        q_sb, k_sb = sb("q_sb", [P, 3, S]), sb("k_sb", [P, 2, S])
        neg_max = sb("neg_max", [P, 4, 3])
        pad_exp = sb("pad_exp", [P, NH])
        den = sb("den", [P, 2, NH])
        probs = sb("probs", [P, 4, 3, S])
        pT = sb("pT", [P, 2, 3 * S])
        o_sb = sb("o_sb", [P, NH, DH])
        fT = sb("fT", [P, 2, NF * S])

        w_attn, w_ffn = sem("attn_weights"), sem("ffn_weights")
        s_xin, s_hTp, s_hT = sem("attn_x_copied"), sem("attn_xT_done"), sem("attn_xT_copied")
        s_sc, s_max, s_exp, s_pad = sem("scores_done"), sem("max_done"), sem("exp_done"), sem("pad_exp_done")
        s_q, s_k, s_v = sem("q_done"), sem("k_done"), sem("v_done")
        s_qe, s_ke, s_ve = sem("q_copied"), sem("k_copied"), sem("v_copied")
        s_pTp, s_pTe, s_pv = sem("probsT_done"), sem("probsT_copied"), sem("pv_done")
        s_nc, s_norm, s_oTp, s_oTe = sem("norm_steps"), sem("o_ready"), sem("oT_done"), sem("oT_copied")
        s_wo, s_xadd, s_st, s_stat = sem("wo_done"), sem("attn_added"), sem("attn_bn"), sem("attn_stats")
        s_h, s_pc = sem("attn_h_written"), sem("attn_pool_steps")
        s_ag, f_ag = sem("attn_aggr"), sem("ffn_aggr")
        f_xin, f_T, f_hT = sem("ffn_x_copied"), sem("ffn_xT_done"), sem("ffn_xT_copied")
        f_1, f_g, f_2 = sem("ffn1_done"), sem("gelu_done"), sem("ffn2_done")
        f_c, f_st, f_stat = sem("ffn_added"), sem("ffn_bn"), sem("ffn_stats")
        f_h, f_pc = sem("ffn_h_written"), sem("ffn_pool_steps")
        N_WA = 10
        N_WF = 6
        O_BANK = bank[5][:, 0:NH * (DH + 1)].rearrange("p (h e) -> p h e", e=DH + 1)

        with nc.Block() as block:
            @block.sync
            def _(sp):
                def load_attn(l):
                    for dst, src in ((wq0[:], io["wq"][l, 0:P]), (wq1[:], io["wq"][l, P:D + 1]),
                                     (wk0[:], io["wk"][l, 0:P]), (wk1[:], io["wk"][l, P:D + 1]),
                                     (wv0[:], io["wv"][l, 0:P]), (wv1[:], io["wv"][l, P:D + 1]),
                                     (wo0[:], io["wo"][l, 0:P]), (wo1[:], io["wo"][l, P:D + 1]),
                                     (ln1_s[:], io["ln1_s"][l].partition_broadcast(P)),
                                     (ln1_b[:], io["ln1_b"][l].partition_broadcast(P))):
                        sp.dma_start(dst, src).then_inc(w_attn, 16)

                def load_ffn(l):
                    for dst, src in ((w10[:], io["w1"][l, 0:P]), (w11[:], io["w1"][l, P:D + 1]),
                                     (w2[:], io["w2"][l].rearrange("(c p) n -> p c n", p=P)),
                                     (b2_rows[:], io["b2"][l].partition_broadcast(P)),
                                     (ln2_s[:], io["ln2_s"][l].partition_broadcast(P)),
                                     (ln2_b[:], io["ln2_b"][l].partition_broadcast(P))):
                        sp.dma_start(dst, src).then_inc(w_ffn, 16)

                load_attn(0)
                load_ffn(0)
                with sp.Fori(1, L) as l:
                    sp.wait_ge(s_h, B * l)
                    load_attn(l)
                    sp.wait_ge(f_h, B * l)
                    load_ffn(l)

            @block.tensor
            def _(pe):
                def x_transposed(g):
                    pe.wait_ge(s_xin, g + 1)
                    nc.tensor.transpose(bank[6][:, 0:S], xin[:, 0:P], ident[:])
                    nc.tensor.transpose(bank[6][0:D1, S:2 * S], xin[:, P:D], ident[:]).then_inc(s_hTp, 1)

                def project_qk(g, first):
                    pe.wait_ge(s_hT, g + 1)
                    if not first:
                        pe.wait_ge(s_ve, g)
                        pe.wait_ge(s_norm, g - 1)
                    for t in range(3):
                        nc.tensor.matmul(bank[4][:, t * S:(t + 1) * S], wq0[:, t * P:(t + 1) * P], hT0[:, 0, :], start=True, stop=False)
                        last = nc.tensor.matmul(bank[4][:, t * S:(t + 1) * S], wq1[:, t * P:(t + 1) * P], hT1[:, 0, :], start=False, stop=True)
                    last.then_inc(s_q, 1)
                    for t in range(2):
                        nc.tensor.matmul(bank[5][:, t * S:(t + 1) * S], wk0[:, t * P:(t + 1) * P], hT0[:, 0, :], start=True, stop=False)
                        last = nc.tensor.matmul(bank[5][:, t * S:(t + 1) * S], wk1[:, t * P:(t + 1) * P], hT1[:, 0, :], start=False, stop=True)
                    last.then_inc(s_k, 1)

                def project_v(g):
                    pe.wait_ge(s_qe, g + 1)
                    nc.tensor.matmul(bank[4][:, 0:D], hT0[:, 0, :], wv0[:], start=True, stop=False)
                    nc.tensor.matmul(bank[4][:, 0:D], hT1[:, 0, :], wv1[:], start=False, stop=True).then_inc(s_v, 1)

                def o_transposed(g):
                    pe.wait_ge(s_norm, g + 1)
                    flat = o_sb[:].rearrange("p h e -> p (h e)")
                    nc.tensor.transpose(bank[7][:, 0:S], flat[:, 0:P], ident[:])
                    nc.tensor.transpose(bank[7][0:D1, S:2 * S], flat[:, P:D], ident[:]).then_inc(s_oTp, 1)

                def project_o(g):
                    pe.wait_ge(s_oTe, g + 1)
                    nc.tensor.matmul(bank[6][:, 256:256 + D], oT0[:], wo0[:], start=True, stop=False)
                    nc.tensor.matmul(bank[6][:, 256:256 + D], oT1[:], wo1[:], start=False, stop=True).then_inc(s_wo, 1)

                def attention_unit(l, u, first, last_unit):
                    g = l * B + u
                    if not last_unit:
                        if not first:
                            pe.wait_ge(s_pTe, 4 * g - 1)
                        x_transposed(g + 1)
                    if not first:
                        pe.wait_ge(s_pTe, 4 * g)
                        o_transposed(g - 1)
                    pe.wait_ge(s_qe, g + 1)
                    pe.wait_ge(s_ke, g + 1)
                    for r in range(4):
                        pe.wait_ge(s_exp, 4 * g if first else 4 * g - 3 + r)
                        nc.tensor.matmul(bank[r][:, 0:3 * S].rearrange("p (i s) -> p i s", i=3), ident_bf[:],
                                         key_bias[:, bass.ds(u, 1), :].to_broadcast([P, 3, S]),
                                         start=True, stop=True)
                    for r in range(4):
                        at = slice(32 * r, 32 * r + 32)
                        for i, (qt, kt) in enumerate(((0, 0), (1, 0), (2, 1))):
                            last = nc.tensor.matmul(bank[r][:, i * S:(i + 1) * S], q_sb[at, qt, :], k_sb[at, kt, :],
                                                    start=False, stop=True, skip_group_check=True)
                        last.then_inc(s_sc, 1)
                    if not first:
                        if not last_unit:
                            pe.wait_ge(s_hT, g + 2)
                        project_o(g - 1)
                    if not last_unit:
                        project_qk(g + 1, False)
                    for r in range(5):
                        if r < 4:
                            pe.wait_ge(s_exp, 4 * g + r + 1)
                            if r == 0 and not first:
                                pe.wait_ge(s_xadd, g)
                            if r == 0 and first:
                                pe.wait_ge(s_hT, g + 2)
                            if r >= 2:
                                pe.wait_ge(s_pTe, 4 * g + r - 1)
                            for i in range(3):
                                last = nc.tensor.transpose(bank[6 + r % 2][:, i * S:(i + 1) * S], probs[:, r, i, :], ident[:])
                            last.then_inc(s_pTp, 1)
                        if r >= 1:
                            pe.wait_ge(s_pTe, 4 * g + r)
                            if r == 1:
                                pe.wait_ge(s_ve, g + 1)
                            if r == 1 and not last_unit:
                                pe.wait_ge(s_ke, g + 2)
                            for i in range(3):
                                h = 3 * (r - 1) + i
                                last = nc.tensor.matmul(O_BANK[:, h, :], pT[:, (r - 1) % 2, i * S:(i + 1) * S], v_sb[:, h, :],
                                                        start=True, stop=True)
                            last.then_inc(s_pv, 1)
                    if not last_unit:
                        project_v(g + 1)

                def ffn_unit(l, u, par, first, last_unit):
                    w = l * B + u
                    if not last_unit:
                        pe.wait_ge(f_xin, w + 2)
                        pe.wait_ge(f_hT, w + 1)
                        nc.tensor.transpose(bank[0][:, 0:S], xin[:, 0:P], ident[:])
                        nc.tensor.transpose(bank[0][0:D1, S:2 * S], xin[:, P:D], ident[:]).then_inc(f_T, 1)
                    pe.wait_ge(f_hT, w + 1)
                    for c in range(NF):
                        if c == 0:
                            pe.wait_ge(f_g, 2 * w if first else 2 * w - 1)
                        if c == 4:
                            pe.wait_ge(f_g, 2 * w)
                        out = bank[1 + c // 4][:, (c % 4) * S:(c % 4 + 1) * S]
                        nc.tensor.matmul(out, w10[:, c * P:(c + 1) * P], hT0[:, par, :], start=True, stop=False)
                        last = nc.tensor.matmul(out, w11[:, c * P:(c + 1) * P], hT1[:, par, :], start=False, stop=True)
                        if c in (3, NF - 1):
                            last.then_inc(f_1, 1)
                    if not first:
                        ffn2(w - 1, 1 - par)

                def ffn2(w, par):
                    pe.wait_ge(f_g, 2 * w + 2)
                    pe.wait_ge(f_c, 2 * w)
                    for c in range(NF):
                        last = nc.tensor.matmul(bank[3][:, 0:D], fT[:, par, c * S:(c + 1) * S], w2[:, c, :], start=(c == 0), stop=(c == NF - 1))
                    last.then_inc(f_2, 1)

                with pe.Fori(0, L) as l:
                    pe.wait_ge(w_attn, 16 * N_WA * l + 16 * N_WA)
                    pe.wait_ge(f_h, B * l)
                    x_transposed(l * B)
                    project_qk(l * B, True)
                    project_v(l * B)
                    attention_unit(l, 0, True, False)
                    with pe.Fori(1, B - 1) as u:
                        attention_unit(l, u, False, False)
                    attention_unit(l, B - 1, False, True)
                    pe.wait_ge(s_pTe, 4 * B * l + 4 * B)
                    o_transposed(l * B + B - 1)
                    project_o(l * B + B - 1)
                    pe.wait_ge(w_ffn, 16 * N_WF * l + 16 * N_WF)
                    pe.wait_ge(s_h, B * l + B)
                    pe.wait_ge(f_xin, l * B + 1)
                    nc.tensor.transpose(bank[0][:, 0:S], xin[:, 0:P], ident[:])
                    nc.tensor.transpose(bank[0][0:D1, S:2 * S], xin[:, P:D], ident[:]).then_inc(f_T, 1)
                    ffn_unit(l, 0, 0, True, False)
                    with pe.Fori(0, B // 2 - 1) as j:
                        ffn_unit(l, 2 * j + 1, 1, False, False)
                        ffn_unit(l, 2 * j + 2, 0, False, False)
                    ffn_unit(l, B - 1, 1, False, True)
                    ffn2(l * B + B - 1, 1)

            @block.scalar
            def _(act):
                def copy_xT(g):
                    act.wait_ge(s_hTp, g + 1)
                    act.wait_ge(s_v, g)
                    nc.scalar.copy(hT0[:, 0, :], bank[6][:, 0:S])
                    nc.scalar.copy(hT1[0:D1, 0, :], bank[6][0:D1, S:2 * S]).then_inc(s_hT, 1)

                def copy_q(g):
                    act.wait_ge(s_q, g + 1)
                    nc.scalar.mul(q_sb[:].rearrange("p t s -> p (t s)"), bank[4][:, 0:3 * S], DH ** -0.5).then_inc(s_qe, 1)

                def copy_oT(g):
                    act.wait_ge(s_oTp, g + 1)
                    nc.scalar.copy(oT0[:], bank[7][:, 0:S])
                    nc.scalar.copy(oT1[0:D1, :], bank[7][0:D1, S:2 * S]).then_inc(s_oTe, 1)

                def attention_unit(l, u, first, last_unit):
                    g = l * B + u
                    if not last_unit:
                        copy_xT(g + 1)
                    if not first:
                        copy_oT(g - 1)
                    for r in range(4):
                        act.wait_ge(s_max, 4 * g + r + 1)
                        act.wait_ge(s_pTp, 4 * g if first else 4 * g - 3 + r)
                        for i in range(3):
                            last = nc.scalar.activation(probs[:, r, i, :], bank[r][:, i * S:(i + 1) * S], ACT.Exp,
                                                        bias=neg_max[:, r, i:i + 1])
                        last.then_inc(s_exp, 1)
                    act.wait_ge(s_norm, g)
                    nc.scalar.activation(pad_exp[:], neg_max[:].rearrange("p r i -> p (r i)"), ACT.Exp,
                                         bias=MASKED).then_inc(s_pad, 1)
                    if not last_unit:
                        copy_q(g + 1)

                def ffn_copy(w, par):
                    act.wait_ge(f_T, w + 1)
                    nc.scalar.copy(hT0[:, par, :], bank[0][:, 0:S])
                    nc.scalar.copy(hT1[0:D1, par, :], bank[0][0:D1, S:2 * S]).then_inc(f_hT, 1)

                def ffn_unit(l, u, par, first, last_unit):
                    w = l * B + u
                    if not last_unit:
                        act.wait_ge(f_1, 2 * w)
                        ffn_copy(w + 1, 1 - par)
                    act.wait_ge(f_1, 2 * w + 1)
                    act.wait_ge(f_2, w if first else w - 1)
                    nc.scalar.activation(fT[:, par, 0:512], bank[1][:, :], ACT.Gelu).then_inc(f_g, 1)
                    act.wait_ge(f_1, 2 * w + 2)
                    nc.scalar.activation(fT[:, par, 512:NF * S], bank[2][:, 0:NF * S - 512], ACT.Gelu).then_inc(f_g, 1)

                with act.Fori(0, L) as l:
                    copy_xT(l * B)
                    copy_q(l * B)
                    attention_unit(l, 0, True, False)
                    with act.Fori(1, B - 1) as u:
                        attention_unit(l, u, False, False)
                    attention_unit(l, B - 1, False, True)
                    copy_oT(l * B + B - 1)
                    ffn_copy(l * B, 0)
                    ffn_unit(l, 0, 0, True, False)
                    with act.Fori(0, B // 2 - 1) as j:
                        ffn_unit(l, 2 * j + 1, 1, False, False)
                        ffn_unit(l, 2 * j + 2, 0, False, False)
                    ffn_unit(l, B - 1, 1, False, True)

            @block.vector
            def _(dve):
                def copy_x(u, done):
                    nc.vector.tensor_copy(xin[:], H[:, u, :]).then_inc(done, 1)

                def copy_k(g):
                    dve.wait_ge(s_k, g + 1)
                    nc.vector.tensor_copy(k_sb[:].rearrange("p t s -> p (t s)"), bank[5][:, 0:2 * S]).then_inc(s_ke, 1)

                def copy_v(g):
                    dve.wait_ge(s_v, g + 1)
                    nc.vector.tensor_copy(v_sb[:, :, 0:DH], bank[4][:, 0:D].rearrange("p (h e) -> p h e", e=DH)).then_inc(s_ve, 1)

                def residual(g, u):
                    dve.wait_ge(s_wo, g + 1)
                    dve.wait_ge(s_h, g)
                    nc.vector.tensor_tensor(xres[:, 0, :], bank[6][:, 256:256 + D], H[:, u, :], ALU.add).then_inc(s_xadd, 1)
                    dve.wait_ge(s_xadd, g + 1)
                    nc.vector.bn_stats(stats[:], xres[:, 0, :]).then_inc(s_st, 1)
                    dve.wait_ge(s_const, 1)
                    dve.wait_ge(s_st, g + 1)
                    nc.vector.bn_aggr(mv[:, 0, :], stats[:]).then_inc(s_ag, 1)
                    dve.wait_ge(s_ag, g + 1)
                    nc.vector.tensor_scalar(var_eps[:, 0:1], mv[:, 0, 1:2], EPS_TXT, None, ALU.add).then_inc(s_stat, 1)

                def attention_unit(l, u, first, last_unit, more_x):
                    g = l * B + u
                    if more_x:
                        dve.wait_ge(s_hTp, g + 2)
                        copy_x(u + 2, s_xin)
                    dve.wait_ge(s_pad, g)
                    for r in range(4):
                        dve.wait_ge(s_sc, 4 * g + r + 1)
                        nc.vector.tensor_reduce(neg_max[:, r, :], bank[r][:, 0:3 * S].rearrange("p (i s) -> p i s", i=3),
                                                AX.X, ALU.max, negate=True).then_inc(s_max, 1)
                    if not first:
                        residual(g - 1, u - 1)
                    if not last_unit:
                        copy_k(g + 1)
                    for r in range(4):
                        dve.wait_ge(s_pTp, 4 * g + r + 1)
                        dve.wait_ge(s_pv, 4 * g if first and r < 2 else 4 * g + r - 1)
                        nc.vector.tensor_copy(pT[:, r % 2, :], bank[6 + r % 2][:, 0:3 * S]).then_inc(s_pTe, 1)
                    dve.wait_ge(s_pv, 4 * g + 4)
                    dve.wait_ge(s_pad, g + 1)
                    nc.vector.scalar_tensor_tensor(den[:, 0, :], pad_exp[:], float(N_PAD), O_BANK[:, :, DH], ALU.mult, ALU.add).then_inc(s_nc, 1)
                    dve.wait_ge(s_nc, 2 * g + 1)
                    nc.vector.reciprocal(den[:, 1, :], den[:, 0, :]).then_inc(s_nc, 1)
                    dve.wait_ge(s_nc, 2 * g + 2)
                    dve.wait_ge(s_oTp, g)
                    nc.vector.tensor_tensor(o_sb[:], O_BANK[:, :, 0:DH], den[:, 1, :].unsqueeze(2).to_broadcast([P, NH, DH]),
                                            ALU.mult).then_inc(s_norm, 1)
                    if not last_unit:
                        copy_v(g + 1)

                def ffn_residual(w, u, par, few):
                    dve.wait_ge(f_2, w + 1)
                    if not few:
                        dve.wait_ge(f_h, w - 1)
                    nc.vector.tensor_tensor(xres[:, par, :], bank[3][:, 0:D], H[:, u, :], ALU.add).then_inc(f_c, 1)
                    dve.wait_ge(f_c, 2 * w + 1)
                    nc.vector.tensor_tensor(xres[:, par, :], xres[:, par, :], b2_rows[:], ALU.add).then_inc(f_c, 1)
                    dve.wait_ge(f_c, 2 * w + 2)
                    nc.vector.bn_stats(stats[:], xres[:, par, :]).then_inc(f_st, 1)
                    dve.wait_ge(s_const, 1)
                    dve.wait_ge(f_st, w + 1)
                    nc.vector.bn_aggr(mv[:, par, :], stats[:]).then_inc(f_ag, 1)
                    dve.wait_ge(f_ag, w + 1)
                    nc.vector.tensor_scalar(var_eps[:, par:par + 1], mv[:, par, 1:2], EPS_TXT, None, ALU.add).then_inc(f_stat, 1)

                with dve.Fori(0, L) as l:
                    dve.wait_ge(f_h, B * l)
                    dve.wait_ge(w_attn, 16 * N_WA * l + 16 * N_WA)
                    copy_x(0, s_xin)
                    dve.wait_ge(s_hTp, B * l + 1)
                    copy_x(1, s_xin)
                    copy_k(l * B)
                    copy_v(l * B)
                    attention_unit(l, 0, True, False, True)
                    with dve.Fori(1, B - 2) as u:
                        attention_unit(l, u, False, False, True)
                    attention_unit(l, B - 2, False, False, False)
                    attention_unit(l, B - 1, False, True, False)
                    residual(l * B + B - 1, B - 1)
                    dve.wait_ge(w_ffn, 16 * N_WF * l + 16 * N_WF)
                    dve.wait_ge(s_h, B * l + B)
                    copy_x(0, f_xin)
                    dve.wait_ge(f_T, B * l + 1)
                    copy_x(1, f_xin)
                    dve.wait_ge(f_T, B * l + 2)
                    copy_x(2, f_xin)
                    ffn_residual(l * B, 0, 0, True)
                    with dve.Fori(0, B // 2 - 2) as j:
                        for c in range(2):
                            dve.wait_ge(f_T, l * B + 2 * j + c + 3)
                            copy_x(2 * j + c + 3, f_xin)
                            ffn_residual(l * B + 2 * j + c + 1, 2 * j + c + 1, 1 - c, False)
                    dve.wait_ge(f_T, l * B + B - 1)
                    copy_x(B - 1, f_xin)
                    for u in range(B - 3, B):
                        ffn_residual(l * B + u, u, u % 2, False)

            @block.gpsimd
            def _(pool):
                def attention_norm(g, u):
                    pool.wait_ge(s_stat, g + 1)
                    norm_rows(pool, s_pc, 4 * g, xres[:, 0, :], mv[:, 0, 0:1], var_eps[:, 0:1], ln1_s[:], ln1_b[:], H[:, u, :]).then_inc(s_h, 1)

                def ffn_norm(w, u, par):
                    pool.wait_ge(f_stat, w + 1)
                    norm_rows(pool, f_pc, 4 * w, xres[:, par, :], mv[:, par, 0:1], var_eps[:, par:par + 1], ln2_s[:], ln2_b[:], H[:, u, :]).then_inc(f_h, 1)

                with pool.Fori(0, L) as l:
                    with pool.Fori(0, B) as u:
                        attention_norm(l * B + u, u)
                    with pool.Fori(0, B // 2) as j:
                        ffn_norm(l * B + 2 * j, 2 * j, 0)
                        ffn_norm(l * B + 2 * j + 1, 2 * j + 1, 1)


def text_layout(x):
    order = [h for group in HEADS_OF_GROUP for h in group]
    cols = np.concatenate([np.arange(DH) + DH * h for h in order])

    def with_bias(w, b):
        return np.concatenate([w, b[:, None, :]], axis=1)

    wq = with_bias(x["L0_txt_Wq"], x["L0_txt_bq"])
    wk = with_bias(x["L0_txt_Wk"], x["L0_txt_bk"])
    wv = with_bias(x["L0_txt_Wv"], x["L0_txt_bv"])
    wq_tiles = np.zeros((L, D + 1, 3 * P), np.float32)
    wk_tiles = np.zeros((L, D + 1, 2 * P), np.float32)
    for r in range(4):
        for i, (qt, kt) in enumerate(((0, 0), (1, 0), (2, 1))):
            h = HEADS_OF_GROUP[r][i]
            a = qt * P + 32 * r + DH * (h % 2)
            wq_tiles[:, :, a:a + DH] = wq[:, :, DH * h:DH * h + DH]
            pair = h // 2
            wk_tiles[:, :, kt * P + 32 * r:kt * P + 32 * r + 2 * DH] = wk[:, :, 2 * DH * pair:2 * DH * pair + 2 * DH]
    wo = with_bias(x["L0_txt_Wo"][:, cols, :], x["L0_txt_bo"])
    return dict(
        ids=np.ascontiguousarray(x["x_txt"].T), mask=x["mask_BS_i1_0"].reshape(-1),
        emb=x["L0_txt_emb_word"], pos=x["L0_txt_emb_pos"][:S],
        emb_ln_s=x["L0_txt_emb_ln_s"], emb_ln_b=x["L0_txt_emb_ln_b"],
        wq=wq_tiles, wk=wk_tiles, wv=wv[:, :, cols], wo=wo,
        w1=with_bias(x["L0_txt_W1"], x["L0_txt_b1"]), w2=x["L0_txt_W2"], b2=x["L0_txt_b2"],
        ln1_s=x["L0_txt_ln1_s"], ln1_b=x["L0_txt_ln1_b"], ln2_s=x["L0_txt_ln2_s"], ln2_b=x["L0_txt_ln2_b"],
    )


def patch_embedding(nc, io, sem, H_img, consts):
    ident, half = consts["ident"], consts["half"]
    NP, WF, CH = 6, 3 * 18 * 18, 108
    NCH = WF // CH
    PD = 16 * 16 * 15
    with ExitStack() as ctx:
        def sb(name, shape, dt=F32):
            return ctx.enter_context(nc.sbuf_tensor(name, shape, dt))

        rows = [P, 6 * B - P]
        xw = [sb(f"tok_x{i}", [P, 3, 18, 98]) for i in range(2)]
        w5 = sb("tok_w5", [CH, 5, NCH, D])
        g5 = sb("tok_g5", [CH, 5, NCH])
        b5 = sb("tok_b5", [CH, 5, NCH])
        w_eff = sb("tok_w_eff", [CH, NCH, D])
        mult = sb("tok_mult", [P, WF])
        ones = sb("tok_ones", [CH, P])
        b_row = sb("tok_b", [1, D])
        beta_cols = sb("tok_beta_cols", [CH, 5 * NCH, P])
        const_rows = sb("tok_const", [P, D])
        xc = sb("tok_xc", [P, 2, WF])
        xm = sb("tok_xm", [P, 2, WF])
        junk = sb("tok_junk", [P, WF])
        xT = sb("tok_xT", [CH, NCH, P])
        neg_mean = sb("tok_neg_mean", [P, 12])
        var = sb("tok_var", [P, 12])
        var_eps = sb("tok_var_eps", [P, 12])
        rstd = sb("tok_rstd", [P, 12])
        tok_out = sb("tok_out", [P, 2, NP, D])
        tb = [ctx.enter_context(nc.psum_tensor(f"tok_bank{i}", [P, 512], F32)) for i in range(5)]

        s_x, s_w, s_one = sem("tok_x_loaded"), sem("tok_w_loaded"), sem("tok_ones_set")
        s_bcol, s_gw, s_const = sem("tok_beta_cols"), sem("tok_w_steps"), sem("tok_const_ready")
        s_cp = sem("tok_const_product")
        s_mean, s_xc, s_xm, s_var, s_rs = sem("tok_mean"), sem("tok_centred"), sem("tok_weighted"), sem("tok_var"), sem("tok_rstd")
        s_vp = sem("tok_var_sum")
        s_T, s_xT, s_mm, s_out = sem("tok_T"), sem("tok_xT"), sem("tok_mm"), sem("tok_out")
        s_junk = sem("tok_junk")
        s_scr, s_back = sem("tok_scratch_written"), sem("tok_scratch_read")
        steps = [(t, w) for t in range(2) for w in range(NP)]

        def window(t, w):
            return xw[t][0:rows[t], :, :, 16 * w:16 * w + 18]

        def v3(ap):
            return ap.rearrange("p (c y x) -> p c y x", c=3, y=18)

        with nc.Block() as block:
            @block.sync
            def _(sp):
                sp.dma_start(xw[0][:], io["tok_x"][0:P]).then_inc(s_x, 16)
                sp.dma_start(mult[:], io["tok_mult"].partition_broadcast(P)).then_inc(s_x, 16)
                sp.dma_start(g5[:], io["tok_g5"]).then_inc(s_w, 16)
                sp.dma_start(b5[:], io["tok_b5"]).then_inc(s_w, 16)
                sp.dma_start(b_row[:], io["tok_b"]).then_inc(s_w, 16)
                sp.dma_start(w5[:], io["tok_w5"]).then_inc(s_w, 16)
                sp.dma_start(xw[1][0:rows[1]], io["tok_x"][P:6 * B]).then_inc(s_x, 16)
                for t in range(2):
                    sp.wait_ge(s_out, NP * (t + 1))
                    sp.dma_start(io["scratch_tok"][t * P:t * P + rows[t]],
                                 tok_out[0:rows[t], t].rearrange("p w e -> p (w e)")).then_inc(s_scr, 16)
                sp.wait_ge(s_scr, 32)
                sp.dma_start(H_img[:], io["scratch_tok"].rearrange("(b h) n -> b (h n)", h=NP).rearrange(
                    "b (t e) -> t b e", e=D)).then_inc(s_back, 16)
                sp.wait_ge(s_back, 16)

            @block.vector
            def _(dve):
                nc.vector.memset(ones[:], 1.0).then_inc(s_one, 1)
                dve.wait_ge(s_w, 64)
                dve.wait_ge(s_one, 1)
                nc.vector.tensor_tensor(beta_cols[:], b5[:].rearrange("p s c -> p (s c)").unsqueeze(2).to_broadcast([CH, 5 * NCH, P]),
                                        ones[:].unsqueeze(1).to_broadcast([CH, 5 * NCH, P]), ALU.mult).then_inc(s_bcol, 1)
                dve.wait_ge(s_x, 48)
                for k, (t, w) in enumerate(steps):
                    if k:
                        dve.wait_ge(s_junk, k)
                    nc.vector.tensor_tensor_reduce(v3(junk[0:rows[t]]), window(t, w), v3(mult[0:rows[t]]), -1.0 / PD, 0.0,
                                                   ALU.mult, ALU.add, neg_mean[0:rows[t], k:k + 1]).then_inc(s_junk, 1)
                dve.wait_ge(s_junk, 12)
                for s in range(5):
                    if s:
                        dve.wait_ge(s_gw, s)
                    for c in range(NCH):
                        if s == 0:
                            last = nc.vector.tensor_scalar(w_eff[:, c, :], w5[:, 0, c, :], g5[:, 0, c:c + 1], None, ALU.mult)
                        else:
                            last = nc.vector.scalar_tensor_tensor(w_eff[:, c, :], w5[:, s, c, :], g5[:, s, c:c + 1], w_eff[:, c, :], ALU.mult, ALU.add)
                    last.then_inc(s_gw, 1)
                dve.wait_ge(s_cp, 1)
                nc.vector.tensor_copy(const_rows[:], tb[4][:, 0:D]).then_inc(s_const, 1)
                for k, (t, w) in enumerate(steps):
                    r = rows[t]
                    dve.wait_ge(s_xm, k + 1)
                    if k:
                        dve.wait_ge(s_vp, k)
                    nc.vector.tensor_tensor_reduce(junk[0:r], xc[0:r, k % 2], xm[0:r, k % 2], 1.0 / PD, 0.0,
                                                   ALU.mult, ALU.add, var[0:r, k:k + 1]).then_inc(s_vp, 1)
                    dve.wait_ge(s_vp, k + 1)
                    nc.vector.tensor_scalar(var_eps[0:r, k:k + 1], var[0:r, k:k + 1], EPS, None, ALU.add).then_inc(s_var, 1)
                    for q in range(2):
                        dve.wait_ge(s_T, 3 * k + q + 1)
                        if q == 0 and k:
                            dve.wait_ge(s_mm, k)
                        nc.vector.tensor_copy(xT[:, 4 * q:4 * q + 4, 0:r], tb[q][0:CH, :].rearrange("p (c n) -> p c n", c=4)[:, :, 0:r]).then_inc(s_xT, 1)
                    dve.wait_ge(s_T, 3 * k + 3)
                    nc.vector.tensor_copy(xT[:, 8, 0:r], tb[2][0:CH, 0:r]).then_inc(s_xT, 1)
                    dve.wait_ge(s_mm, k + 1)
                    dve.wait_ge(s_rs, k + 1)
                    dve.wait_ge(s_const, 1)
                    nc.vector.scalar_tensor_tensor(tok_out[0:r, t, w, :], tb[3][0:r, 0:D], rstd[0:r, k:k + 1], const_rows[0:r],
                                                   ALU.mult, ALU.add).then_inc(s_out, 1)

            @block.scalar
            def _(act):
                for k, (t, w) in enumerate(steps):
                    act.wait_ge(s_junk, k + 1)
                    if k >= 2:
                        act.wait_ge(s_vp, k - 1)
                        act.wait_ge(s_T, 3 * k - 3)
                    nc.scalar.activation(v3(xc[0:rows[t], k % 2]), window(t, w), ACT.Identity,
                                         bias=neg_mean[0:rows[t], k:k + 1]).then_inc(s_xc, 1)

            def rstd_of(pool, k):
                r = rows[steps[k][0]]
                pool.wait_ge(s_var, k + 1)
                nc.gpsimd.tensor_tensor(rstd[0:r, k:k + 1], var_eps[0:r, k:k + 1], half[0:r], ALU.pow).then_inc(s_rs, 1)

            @block.gpsimd
            def _(pool):
                for k, (t, w) in enumerate(steps):
                    r = rows[t]
                    pool.wait_ge(s_xc, k + 1)
                    if k >= 2:
                        pool.wait_ge(s_vp, k - 1)
                    nc.gpsimd.tensor_tensor(xm[0:r, k % 2], xc[0:r, k % 2], mult[0:r], ALU.mult).then_inc(s_xm, 1)
                    if k >= 1:
                        rstd_of(pool, k - 1)
                rstd_of(pool, 11)

            @block.tensor
            def _(pe):
                pe.wait_ge(s_bcol, 1)
                for i in range(5 * NCH):
                    nc.tensor.matmul(tb[4][:, 0:D], beta_cols[:, i, :], w5[:, i // NCH, i % NCH, :], start=(i == 0), stop=False)
                nc.tensor.matmul(tb[4][:, 0:D], ones[0:1, :], b_row[:], start=False, stop=True).then_inc(s_cp, 1)
                for k, (t, w) in enumerate(steps):
                    r = rows[t]
                    pe.wait_ge(s_xc, k + 1)
                    for c in range(NCH):
                        if c % 4 == 0 and k:
                            pe.wait_ge(s_xT, 3 * (k - 1) + c // 4 + 1)
                        last = nc.tensor.transpose(tb[c // 4][0:CH, (c % 4) * P:(c % 4) * P + r], xc[0:r, k % 2, c * CH:(c + 1) * CH], ident[0:r, 0:r])
                        if c in (3, 7, 8):
                            last.then_inc(s_T, 1)
                    pe.wait_ge(s_gw, 5)
                    if k:
                        pe.wait_ge(s_out, k)
                    for c in range(NCH):
                        if c % 4 == 0:
                            pe.wait_ge(s_xT, 3 * k + c // 4 + 1)
                        last = nc.tensor.matmul(tb[3][0:r, 0:D], xT[:, c, 0:r], w_eff[:, c, :], start=(c == 0), stop=(c == NCH - 1))
                    last.then_inc(s_mm, 1)


def tok_layout(x):
    xp = np.zeros((B, 3, 98, 98), np.float32)
    xp[:, :, 1:97, 1:97] = x["x"]
    tok_x = np.stack([xp[:, :, 16 * h:16 * h + 18, :] for h in range(6)], axis=1).reshape(6 * B, 3, 18, 98)
    shifts = [(1, 1), (1, 0), (1, 2), (0, 1), (2, 1)]

    def spread(a):
        n = a.shape[1]
        a = a.reshape(16, 16, 5, 3, n)
        out = np.zeros((5, 3, 18, 18, n), np.float32)
        for s, (dy, dx) in enumerate(shifts):
            out[s, :, dy:dy + 16, dx:dx + 16] = a[:, :, s].transpose(2, 0, 1, 3)
        return np.ascontiguousarray(out.reshape(5, 9, 108, n).transpose(2, 0, 1, 3))

    mult = np.zeros((3, 18, 18), np.float32)
    for dy, dx in shifts:
        mult[:, dy:dy + 16, dx:dx + 16] += 1
    return dict(tok_x=tok_x, tok_w5=spread(x["L0_tok_W"]), tok_g5=spread(x["L0_tok_gamma"][:, None])[..., 0],
                tok_b5=spread(x["L0_tok_beta"][:, None])[..., 0], tok_b=x["L0_tok_b"][None], tok_mult=mult.reshape(-1))


class Steps:

    def __init__(self, engine, semaphore, per, j):
        self.engine, self.semaphore, self.per, self.j, self.n = engine, semaphore, per, j, 0

    def done(self, instruction):
        self.n += 1
        instruction.then_inc(self.semaphore, 1)
        return self.n

    def wait(self, n=None):
        self.engine.wait_ge(self.semaphore, self.per * self.j + (self.n if n is None else n))


NPAIR = B // 2
W2T = 2 * T
W3T = 3 * T


def ssm_and_slots(nc, io, sem, H, H_img, consts):
    ident, half = consts["ident"], consts["half"]
    with ExitStack() as ctx:
        def sb(name, shape, dt=F32):
            return ctx.enter_context(nc.sbuf_tensor(name, shape, dt))

        wB, wC = (sb(n, [P, 4, NS * D], F16) for n in ("wB", "wC"))
        wi0, wi1 = sb("wi0", [P, 2 * D]), sb("wi1", [D1 + 1, 2 * D])
        wdt0, wdt1 = sb("wdt0", [P, D]), sb("wdt1", [D1 + 1, D])
        wso0, wso1 = sb("wso0", [P, D]), sb("wso1", [D1 + 1, D])
        a_neg = sb("a_neg", [P, 2, NS])
        wconv = sb("wconv", [P, 2, KC + 2])
        slots0, slots1 = sb("slots0", [P, SLOTS]), sb("slots1", [D1, SLOTS])
        xt0, xt1 = sb("xt0", [P, B, SLOTS]), sb("xt1", [D1 + 1, B, SLOTS])
        c_all = sb("c_all", [SLOTS, NPAIR, W2T])
        half4 = sb("half4", [P, 2, 4])
        pb = [ctx.enter_context(nc.psum_tensor(f"bank{i}", [P, 512], F32)) for i in range(8)]

        with ExitStack() as tmp:
            def t(name, shape):
                return tmp.enter_context(nc.sbuf_tensor(name, shape, F32))
            a_log = t("a_log", [P, 2, NS])
            raw0, raw1 = t("raw0", [P, SLOTS]), t("raw1", [D1, SLOTS])
            sq = t("sq", [P, 2, SLOTS])
            nrm = t("nrm", [P, 4, 2, NP_])
            scale = t("scale", [P, 1])
            stage = t("stage", [P, 3, NS * D])
            high = tmp.enter_context(nc.sbuf_tensor("high", [P, NS * D], F16))
            low_rows = t("low_rows", [P, 1])
            l_st, z_st, z_h, z_l, z_sc = sem("stage_loaded"), sem("stage_zeroed"), sem("high_ready"), sem("low_ready"), sem("stage_scaled")
            l_w, l_s = sem("ssm_weights_loaded"), sem("slots_loaded")
            z_v, z_p, z_a, z_set = sem("setup_dve"), sem("setup_pool"), sem("setup_act"), sem("setup_zeroed")
            with nc.Block() as block:
                @block.sync
                def _(sp):
                    for dst, src in ((raw0[:], io["slot_params"][0:P]), (raw1[:], io["slot_params"][P:D]),
                                     (scale[:], io["slot_scale"].partition_broadcast(P)), (a_log[:], io["a_log"])):
                        sp.dma_start(dst, src).then_inc(l_s, 16)
                    for dst, src in ((wconv[:], io["wconv"]), (wi0[:], io["wi"][0:P]), (wi1[:], io["wi"][P:D + 1]),
                                     (wdt0[:], io["wdt"][0:P]), (wdt1[:], io["wdt"][P:D + 1]),
                                     (wso0[:], io["wso"][0:P]), (wso1[:], io["wso"][P:D + 1])):
                        sp.dma_start(dst, src).then_inc(l_w, 16)
                    sp.wait_ge(z_st, 1)
                    for i, name in enumerate(("wB", "wC")):
                        sp.wait_ge(z_l, 2 * i)
                        sp.wait_ge(z_h, 3 * i)
                        w = io[name]
                        for dst, src in ((stage[:, 0], w[0:P]), (stage[0:D1, 1], w[P:D]), (stage[D1:P, 1], w[P:D]),
                                         (stage[0:D1, 2], w[P:D]), (stage[D1:D1 + 1, 2], w[D:D + 1]), (stage[96:97, 2], w[D:D + 1])):
                            sp.dma_start(dst, src).then_inc(l_st, 16)
                    sp.wait_ge(l_w, 16 * 7)

                @block.scalar
                def _(act):
                    act.wait_ge(l_s, 64)
                    nc.scalar.activation(a_neg[:], a_log[:], ACT.Exp).then_inc(z_a, 1)
                    for i, w in enumerate((wB, wC)):
                        act.wait_ge(z_sc, i + 1)
                        nc.scalar.copy(w[:, 0], stage[:, 0]).then_inc(z_h, 1)
                        nc.scalar.copy(w[:, 2], stage[:, 1]).then_inc(z_h, 1)
                        act.wait_ge(z_l, 2 * i)
                        nc.scalar.copy(high[:], stage[:, 2]).then_inc(z_h, 1)

                @block.vector
                def _(dve):
                    nc.vector.memset(half4[:, 0, :], -0.5)
                    nc.vector.memset(half4[:, 1, :], 0.5)
                    nc.vector.memset(xt1[:], 1.0)
                    nc.vector.memset(stage[:, 2], 0.0).then_inc(z_st, 1)
                    nc.vector.memset(low_rows[:D1], -1.0)
                    nc.vector.memset(low_rows[D1:96], 0.0)
                    nc.vector.memset(low_rows[96:], -1.0)
                    nc.vector.memset(sq[:], 0.0).then_inc(z_set, 1)
                    dve.wait_ge(z_set, 1)
                    dve.wait_ge(l_s, 64)
                    for c, (raw, r) in enumerate(((raw0, P), (raw1, D1))):
                        nc.vector.tensor_tensor(sq[0:r, c], raw[:], raw[:], ALU.mult).then_inc(z_v, 1)
                    dve.wait_ge(z_v, 2)
                    nc.vector.tensor_reduce(nrm[:, 0], sq[:].rearrange("p c (n q) -> p c q n", n=NE), AX.X, ALU.add).then_inc(z_v, 1)
                    dve.wait_ge(z_a, 1)
                    nc.vector.tensor_scalar(a_neg[:], a_neg[:], -1.0, None, ALU.mult)
                    dve.wait_ge(z_p, 1)
                    nc.vector.tensor_scalar(nrm[:, 2], nrm[:, 1], 1e-6, None, ALU.add).then_inc(z_v, 1)
                    dve.wait_ge(z_v, 4)
                    nc.vector.reciprocal(nrm[:, 3], nrm[:, 2]).then_inc(z_v, 1)
                    dve.wait_ge(z_v, 5)
                    for c, (raw, slots, r) in enumerate(((raw0, slots0, P), (raw1, slots1, D1))):
                        nc.vector.scalar_tensor_tensor(slots[:].rearrange("p (n q) -> p n q", n=NE), raw[:].rearrange("p (n q) -> p n q", n=NE),
                                                       scale[0:r, 0:1], nrm[0:r, 3, c].unsqueeze(1).to_broadcast([r, NE, NP_]), ALU.mult, ALU.mult)
                    for i, w in enumerate((wB, wC)):
                        dve.wait_ge(l_st, 96 * (i + 1))
                        nc.vector.tensor_scalar(stage[:], stage[:], W_SCALE, None, ALU.mult).then_inc(z_sc, 1)
                        dve.wait_ge(z_sc, i + 1)
                        dve.wait_ge(z_h, 3 * i + 3)
                        nc.vector.tensor_tensor(w[:, 1], stage[:, 0], w[:, 0], ALU.subtract).then_inc(z_l, 1)
                        nc.vector.scalar_tensor_tensor(w[:, 3], high[:], low_rows[:, 0:1], stage[:, 2], ALU.mult, ALU.add).then_inc(z_l, 1)

                @block.gpsimd
                def _(pool):
                    pool.wait_ge(z_v, 3)
                    nc.gpsimd.tensor_tensor(nrm[:, 1], nrm[:, 0], half4[:, 1, 0:1].unsqueeze(2).to_broadcast([P, 2, NP_]), ALU.pow).then_inc(z_p, 1)

        with ExitStack() as tmp:
            def t(name, shape):
                return tmp.enter_context(nc.sbuf_tensor(name, shape, F32))
            st4 = t("st4", [P, 4, 6])
            mv_f, ve_f, rs_f = t("mv_f", [P, 4, 2]), t("ve_f", [P, 4]), t("rs_f", [P, 4])
            xn_t, xn_i = t("xn_t", [P, 2, D]), t("xn_i", [N_IMG, 2, D])
            xT0, xT1 = t("xT0", [P, W2T]), t("xT1", [D1 + 1, W2T])
            u_pad = t("u_pad", [P, 3, KC - 1 + T])
            conv = t("conv", [P, 2, 3, T])
            uc_n, uc1_n = t("uc_n", [P, 3, T]), t("uc1_n", [D1 + 1, W2T])
            ev_n = t("ev_n", [P, W3T])
            sp_a, sp_e, sp_l = t("sp_a", [P, W3T]), t("sp_e", [P, W3T]), t("sp_l", [P, W3T])
            dt_n = t("dt_n", [P, W3T])
            y0 = t("y0", [P, 3, T])
            u16, u16_n = (tmp.enter_context(nc.sbuf_tensor(n, [P, 4, W2T], F16)) for n in ("u16", "u16_n"))
            dt, dtu = t("dt", [P, 3, T]), t("dtu", [P, W3T])
            sg = t("sg", [P, 2, W3T])
            decay = t("decay", [P, 2, 3, T])
            inp = t("inp", [P, 2, W3T])
            state = t("state", [P, 2, W3T])
            cstate = t("cstate", [P, 2, W3T])
            y = t("y", [P, 2, W3T])
            yg, yg1 = t("yg", [P, W3T]), t("yg1", [D1 + 1, W2T])
            mv_b, sm = t("mv_b", [P, 4, 2]), t("sm", [P, 8, 4])
            zn_t, zn_i = t("zn_t", [P, 2, D]), t("zn_i", [N_IMG, 2, D])
            zT0, zT1 = t("zT0", [P, W2T]), t("zT1", [D1, W2T])
            cmax, cexp = t("cmax", [P, 3, 4]), t("cexp", [P, 3, 4, SLOTS])
            dmax, dexp = t("dmax", [SLOTS, 3, 2]), t("dexp", [SLOTS, 2, W2T])
            d_tok = t("d_tok", [P, 4, SLOTS])

            names = ("bn bn0 var rs xn T xT U V up v conv uc1 hi lo D l dt y0").split()
            F = {n: sem("front_" + n) for n in names}
            fd, fa = sem("front_dve_steps"), sem("front_act_steps")
            s_uc, s_dt, s_dtu, s_sg = sem("uc_ready"), sem("dt_ready"), sem("dtu_ready"), sem("sigmoid_ready")
            s_B, s_C, s_a, s_in, s_scan, s_cs, s_acc = (sem(n) for n in ("B_done", "C_done", "decay_ready", "input_ready", "scan_done", "cstate_ready", "y_added"))
            names = ("yg yg1 op h2 bn var pw zn T zT L mx e cd T3 ct dT x xt").split()
            K = {n: sem("back_" + n) for n in names}
            bd = sem("back_dve_steps")
            s_set = sem("scan_constants")
            FD, BD = 8, 10

            def v3(ap):
                return ap.rearrange("p (a t) -> p a t", a=3)

            with nc.Block() as block:
                @block.tensor
                def _(pe):
                    def mixed(bank, w0, w1, c0, x0, x1, done):
                        nc.tensor.matmul(bank[:, 0:W2T], w0[:, c0:c0 + P], x0, start=True, stop=False)
                        nc.tensor.matmul(bank[:, 0:W2T], w1[:, c0:c0 + P], x1, start=False, stop=True)
                        for k, (w, x) in enumerate(((w0, x0), (w1, x1))):
                            for s in range(2):
                                last = nc.tensor.matmul(bank[D1 * s:D1 * s + D1, W2T:W3T], w[:, c0 + P:c0 + D], x[:, s * T:(s + 1) * T],
                                                        start=(k == 0), stop=(k == 1))
                        last.then_inc(done, 1)

                    def mixed_halves(bank, w, n, done):
                        passes = ((0, 0, P), (1, 0, P), (0, 1, P), (2, 2, P), (3, 3, 97))
                        for k, (a, b, r) in enumerate(passes):
                            nc.tensor.matmul(bank[:, 0:W2T], w[0:r, a, n * D:n * D + P], u16[0:r, b, :], start=(k == 0), stop=(k == 4))
                        for k, (a, b, r) in enumerate(passes):
                            for s in range(2):
                                last = nc.tensor.matmul(bank[D1 * s:D1 * s + D1, W2T:W3T], w[0:r, a, n * D + P:(n + 1) * D],
                                                        u16[0:r, b, s * T:(s + 1) * T], start=(k == 0), stop=(k == 4))
                        last.then_inc(done, 1)

                    def to_channels(b0, b1, z_t, z_i, done):
                        for s in range(2):
                            c = s * T
                            nc.tensor.transpose(b0[:, c + N_IMG:c + T], z_t[:, s, 0:P], ident[:])
                            nc.tensor.transpose(b0[:, c:c + N_IMG], z_i[:, s, 0:P], ident[0:N_IMG, 0:N_IMG])
                            nc.tensor.transpose(b1[0:D1, c:c + N_IMG], z_i[:, s, P:D], ident[0:N_IMG, 0:N_IMG])
                            last = nc.tensor.transpose(b1[0:D1, c + N_IMG:c + T], z_t[:, s, P:D], ident[:])
                        last.then_inc(done, 1)

                    def front_T(j):
                        pe.wait_ge(F["xn"], j + 1)
                        pe.wait_ge(F["dt"], j)
                        pe.wait_ge(F["v"], j)
                        to_channels(pb[6], pb[7], xn_t, xn_i, F["T"])

                    def front_uv(j):
                        pe.wait_ge(F["xT"], j + 1)
                        mixed(pb[6], wi0, wi1, 0, xT0[:], xT1[:], F["U"])
                        mixed(pb[7], wi0, wi1, D, xT0[:], xT1[:], F["V"])

                    def front_dt(j):
                        pe.wait_ge(F["uc1"], j + 1)
                        pe.wait_ge(F["up"], j + 1)
                        mixed(pb[6], wdt0, wdt1, 0, uc_n[:].rearrange("p a t -> p (a t)")[:, 0:W2T], uc1_n[:], F["D"])

                    def back_op(j):
                        pe.wait_ge(K["yg1"], j + 1)
                        pe.wait_ge(K["xt"], j)
                        pe.wait_ge(K["dT"], j)
                        for s in range(2):
                            c = s * T
                            nc.tensor.matmul(pb[4][:, s * D:(s + 1) * D], yg[:, c + N_IMG:c + T], wso0[:], start=True, stop=False)
                            nc.tensor.matmul(pb[4][:, s * D:(s + 1) * D], yg1[:, c + N_IMG:c + T], wso1[:], start=False, stop=True)
                            nc.tensor.matmul(pb[5][0:N_IMG, s * D:(s + 1) * D], yg[:, c:c + N_IMG], wso0[:], start=True, stop=False)
                            last = nc.tensor.matmul(pb[5][0:N_IMG, s * D:(s + 1) * D], yg1[:, c:c + N_IMG], wso1[:], start=False, stop=True)
                        last.then_inc(K["op"], 1)

                    def back_T(j):
                        pe.wait_ge(K["zn"], j + 1)
                        to_channels(pb[4], pb[5], zn_t, zn_i, K["T"])

                    def back_logits(j):
                        pe.wait_ge(K["zT"], j + 1)
                        for i in range(4):
                            s, c = i % 2, (i % 2) * T + (N_IMG if i < 2 else 0)
                            out = pb[4][:, i * SLOTS:(i + 1) * SLOTS]
                            nc.tensor.matmul(out, zT0[:, c:c + P], slots0[:], start=True, stop=False)
                            nc.tensor.matmul(out, zT1[:, c:c + P], slots1[:], start=False, stop=True)
                        nc.tensor.matmul(pb[5][0:SLOTS, 0:W2T], slots0[:], zT0[:], start=True, stop=False)
                        nc.tensor.matmul(pb[5][0:SLOTS, 0:W2T], slots1[:], zT1[:], start=False, stop=True).then_inc(K["L"], 1)

                    def back_T3(j):
                        pe.wait_ge(K["cd"], j + 1)
                        for i in range(4):
                            s, c = i % 2, (i % 2) * T + (N_IMG if i < 2 else 0)
                            r = P if i < 2 else N_IMG
                            nc.tensor.transpose(pb[4][0:SLOTS, c:c + r], cexp[0:r, 2, i, :], ident[0:r, 0:r])
                            last = nc.tensor.transpose(pb[5][:, i * SLOTS:(i + 1) * SLOTS], dexp[:, 1, c:c + P], ident[0:SLOTS, 0:SLOTS])
                        last.then_inc(K["T3"], 1)

                    def back_x(j):
                        pe.wait_ge(K["ct"], j + 1)
                        pe.wait_ge(K["dT"], j + 1)
                        for s in range(2):
                            for m, (lo, hi) in enumerate(((0, P), (P, D))):
                                out = pb[4][0:hi - lo, m * 2 * SLOTS + s * SLOTS:m * 2 * SLOTS + (s + 1) * SLOTS]
                                nc.tensor.matmul(out, zn_t[:, s, lo:hi], d_tok[:, s, :], start=True, stop=False)
                                last = nc.tensor.matmul(out, zn_i[:, s, lo:hi], d_tok[0:N_IMG, 2 + s, :], start=False, stop=True)
                        last.then_inc(K["x"], 1)

                    def scan_steps(j, first, last_pair):
                        pe.wait_ge(s_uc, j + 1)
                        for n in range(NS):
                            m = NS * j + n
                            if not first:
                                if n == 3:
                                    back_op(j - 1)
                                if n == 6:
                                    back_T(j - 1)
                                if n == 7:
                                    back_logits(j - 1)
                                if n == 10:
                                    back_T3(j - 1)
                                if n == 12:
                                    back_x(j - 1)
                            if not last_pair:
                                if n == 3:
                                    front_T(j + 1)
                                if n == 4:
                                    front_uv(j + 1)
                                if n == 7:
                                    front_dt(j + 1)
                            if n >= 2 or not first:
                                pe.wait_ge(s_in, m - 1)
                            mixed_halves(pb[n % 2], wB, n, s_B)
                            if n >= 2 or not first:
                                pe.wait_ge(s_cs, m - 1)
                            mixed_halves(pb[2 + n % 2], wC, n, s_C)

                    front_T(0)
                    front_uv(0)
                    front_dt(0)
                    scan_steps(0, True, False)
                    with pe.Fori(1, NPAIR - 1) as j:
                        scan_steps(j, False, False)
                    scan_steps(NPAIR - 1, False, True)
                    for piece in (back_op, back_T, back_logits, back_T3, back_x):
                        piece(NPAIR - 1)

                @block.scalar
                def _(act):
                    def front_xT(j):
                        act.wait_ge(F["T"], j + 1)
                        act.wait_ge(F["V"], j)
                        nc.scalar.copy(xT0[:], pb[6][:, 0:W2T])
                        nc.scalar.copy(xT1[0:D1, :], pb[7][0:D1, 0:W2T]).then_inc(F["xT"], 1)

                    def front_up(j):
                        act.wait_ge(F["U"], j + 1)
                        act.wait_ge(F["conv"], j)
                        nc.scalar.copy(u_pad[:, :, KC - 1:], v3(pb[6][:, 0:W3T])).then_inc(F["up"], 1)
                        act.wait_ge(F["V"], j + 1)
                        act.wait_ge(s_sg, 2 * j)
                        nc.scalar.activation(ev_n[:], pb[7][:, 0:W3T], ACT.Exp, scale=-1.0).then_inc(F["v"], 1)

                    def front_uc1(j):
                        act.wait_ge(F["conv"], j + 1)
                        act.wait_ge(F["D"], j)
                        nc.scalar.copy(uc1_n[0:D1, 0:T], uc_n[0:D1, 2, :])
                        nc.scalar.copy(uc1_n[0:D1, T:W2T], uc_n[D1:P, 2, :]).then_inc(F["uc1"], 1)
                        act.wait_ge(F["uc1"], j + 1)
                        act.wait_ge(s_uc, j)
                        nc.scalar.copy(u16_n[:, 0, :], uc_n[:, 0:2, :].rearrange("p a t -> p (a t)"))
                        nc.scalar.copy(u16_n[0:D1, 2, :], uc1_n[0:D1, :])
                        nc.scalar.copy(u16_n[0:D1, 3, :], uc1_n[0:D1, :]).then_inc(F["hi"], 1)

                    def front_softplus(j):
                        act.wait_ge(F["D"], j + 1)
                        act.wait_ge(F["dt"], j)
                        nc.scalar.activation(sp_a[:], pb[6][:, 0:W3T], ACT.Abs).then_inc(fa, 1)
                        act.wait_ge(fa, 2 * j + 1)
                        nc.scalar.activation(sp_e[:], sp_a[:], ACT.Exp, scale=-1.0).then_inc(fa, 1)
                        act.wait_ge(fa, 2 * j + 2)
                        nc.scalar.activation(sp_l[:], sp_e[:], ACT.Ln, bias=1.0).then_inc(F["l"], 1)

                    def back_yg1(j):
                        act.wait_ge(K["yg"], j + 1)
                        act.wait_ge(K["op"], j)
                        nc.scalar.copy(yg1[0:D1, 0:T], yg[0:D1, W2T:W3T])
                        nc.scalar.copy(yg1[0:D1, T:W2T], yg[D1:P, W2T:W3T]).then_inc(K["yg1"], 1)

                    def back_zT(j):
                        act.wait_ge(K["T"], j + 1)
                        nc.scalar.copy(zT0[:], pb[4][:, 0:W2T])
                        nc.scalar.copy(zT1[:], pb[5][0:D1, 0:W2T]).then_inc(K["zT"], 1)

                    def back_exp(j):
                        act.wait_ge(K["mx"], j + 1)
                        nc.scalar.activation(cexp[:, 1], cexp[:, 0], ACT.Exp)
                        for s in range(2):
                            last = nc.scalar.activation(dexp[:, 0, s * T:(s + 1) * T], pb[5][0:SLOTS, s * T:(s + 1) * T], ACT.Exp,
                                                        bias=dmax[:, 0, s:s + 1])
                        last.then_inc(K["e"], 1)

                    def back_ct(j):
                        act.wait_ge(K["T3"], j + 1)
                        nc.scalar.copy(c_all[:, bass.ds(j, 1), :], pb[4][0:SLOTS, 0:W2T].unsqueeze(1)).then_inc(K["ct"], 1)

                    def back_xt(j):
                        act.wait_ge(K["x"], j + 1)
                        nc.scalar.copy(xt0[:, bass.ds(2 * j, 2), :], pb[4][:, 0:2 * SLOTS].rearrange("p (s k) -> p s k", s=2))
                        nc.scalar.copy(xt1[0:D1, bass.ds(2 * j, 2), :],
                                       pb[4][0:D1, 2 * SLOTS:4 * SLOTS].rearrange("p (s k) -> p s k", s=2)).then_inc(K["xt"], 1)

                    def scan_steps(j, first, last_pair):
                        act.wait_ge(s_dt, j + 1)
                        for n in range(NS):
                            m = NS * j + n
                            if not first:
                                if n == 2:
                                    back_yg1(j - 1)
                                if n == 6:
                                    back_zT(j - 1)
                                if n == 8:
                                    back_exp(j - 1)
                                if n == 10:
                                    back_ct(j - 1)
                                if n == 12:
                                    back_xt(j - 1)
                            if not last_pair:
                                if n == 3:
                                    front_xT(j + 1)
                                if n == 5:
                                    front_up(j + 1)
                                if n == 6:
                                    front_uc1(j + 1)
                                if n == 8:
                                    front_softplus(j + 1)
                            if n >= 2 or not first:
                                act.wait_ge(s_scan, m - 1)
                            nc.scalar.activation(decay[:, n % 2, 0:2, 1:], dt[:, 0:2, 1:], ACT.Exp, scale=a_neg[:, 0, n:n + 1])
                            nc.scalar.activation(decay[:, n % 2, 2, 1:], dt[:, 2, 1:], ACT.Exp, scale=a_neg[:, 1, n:n + 1]).then_inc(s_a, 1)

                    act.wait_ge(s_set, 1)
                    for piece in (front_xT, front_up, front_uc1, front_softplus):
                        piece(0)
                    scan_steps(0, True, False)
                    with act.Fori(1, NPAIR - 1) as j:
                        scan_steps(j, False, False)
                    scan_steps(NPAIR - 1, False, True)
                    for piece in (back_yg1, back_zT, back_exp, back_ct, back_xt):
                        piece(NPAIR - 1)

                @block.vector
                def _(dve):
                    def rows_of(i, j, arrays):
                        return arrays[i // 2][:, 2 * j + i % 2, :], (P if i < 2 else N_IMG)

                    def statistics(j, bn, count, mv):
                        for i in range(4):
                            x, r = rows_of(i, j, (H, H_img))
                            last = nc.vector.bn_stats(st4[0:r, i, :], x)
                        last.then_inc(bn, 1)
                        dve.wait_ge(s_set, 1)
                        dve.wait_ge(bn, count)
                        for i in range(4):
                            r = P if i < 2 else N_IMG
                            last = nc.vector.bn_aggr(mv[0:r, i, :], st4[0:r, i, :])
                        return last

                    def normalise(j, mv, factor, z_t, z_i):
                        for i in range(4):
                            x, r = rows_of(i, j, (H, H_img))
                            z = (z_t, z_i)[i // 2][:, i % 2, :]
                            last = nc.vector.tensor_scalar(z, x, mv[0:r, i, 0:1], factor[0:r, i:i + 1], ALU.subtract, ALU.mult)
                        return last

                    def front_norm_a(j):
                        st = Steps(dve, fd, FD, j)
                        at_start = isinstance(j, int) and j == 0
                        st.done(statistics(j, F["bn0"] if at_start else F["bn"], 1 if at_start else j, mv_f))
                        st.wait()
                        nc.vector.tensor_scalar(ve_f[:], mv_f[:, :, 1], EPS, None, ALU.add).then_inc(F["var"], 1)

                    def front_norm_b(j):
                        dve.wait_ge(F["rs"], j + 1)
                        dve.wait_ge(F["T"], j)
                        normalise(j, mv_f, rs_f, xn_t, xn_i).then_inc(F["xn"], 1)

                    def front_conv(j):
                        st = Steps(dve, fd, FD, j)
                        st.n = 1
                        dve.wait_ge(F["up"], j + 1)
                        dve.wait_ge(F["hi"], j)
                        dve.wait_ge(F["D"], j)
                        parts = ((slice(0, 2), 0), (slice(2, 3), 1))
                        for k in range(KC):
                            for seg, w in parts:
                                x = u_pad[:, seg, k:k + T]
                                out = uc_n[:, seg] if k == KC - 1 else conv[:, k % 2, seg]
                                if k == 0:
                                    st.done(nc.vector.tensor_scalar(out, x, wconv[:, w, 0:1], wconv[:, w, KC:KC + 1], ALU.mult, ALU.add))
                                else:
                                    st.wait(st.n - 1)
                                    last = nc.vector.scalar_tensor_tensor(out, x, wconv[:, w, k:k + 1], conv[:, (k - 1) % 2, seg],
                                                                          ALU.mult, ALU.add)
                                    if (k, w) == (KC - 1, 1):
                                        last.then_inc(F["conv"], 1)
                                    else:
                                        st.done(last)
                        dve.wait_ge(F["conv"], j + 1)
                        if not (isinstance(j, int) and j == 0):
                            dve.wait_ge(s_acc, NS * j - NS + 1)
                        for seg, w in parts:
                            last = nc.vector.tensor_scalar(y0[:, seg], uc_n[:, seg], wconv[:, w, KC + 1:KC + 2], W_SCALE, ALU.mult, ALU.mult)
                        last.then_inc(F["y0"], 1)

                    def front_dt(j):
                        dve.wait_ge(F["l"], j + 1)
                        nc.vector.scalar_tensor_tensor(dt_n[:], pb[6][:, 0:W3T], 0.0, sp_l[:], ALU.max, ALU.add).then_inc(F["dt"], 1)

                    def front_low(j):
                        dve.wait_ge(F["hi"], j + 1)
                        dve.wait_ge(F["D"], j + 1)
                        nc.vector.tensor_tensor(u16_n[:, 1, :], uc_n[:, 0:2, :].rearrange("p a t -> p (a t)"), u16_n[:, 0, :], ALU.subtract)
                        nc.vector.tensor_tensor(u16_n[D1:P, 2, :], uc1_n[0:D1, :], u16_n[0:D1, 3, :], ALU.subtract).then_inc(F["lo"], 1)

                    def take_dt(j):
                        dve.wait_ge(F["lo"], j + 1)
                        dve.wait_ge(s_C, NS * j)
                        nc.vector.tensor_copy(u16[:].rearrange("p a t -> p (a t)"), u16_n[:].rearrange("p a t -> p (a t)")).then_inc(s_uc, 1)
                        dve.wait_ge(F["dt"], j + 1)
                        dve.wait_ge(F["y0"], j + 1)
                        dve.wait_ge(s_a, NS * j)
                        nc.vector.tensor_copy(dt[:].rearrange("p a t -> p (a t)"), dt_n[:]).then_inc(s_dt, 1)
                        nc.vector.scalar_tensor_tensor(dtu[:], dt_n[:], 1.0 / W_SCALE, uc_n[:].rearrange("p a t -> p (a t)"),
                                                       ALU.mult, ALU.mult).then_inc(s_dtu, 1)

                    def gate(j):
                        dve.wait_ge(F["v"], j + 1)
                        nc.vector.tensor_scalar(sg[:, 0, :], ev_n[:], 1.0, W_SCALE, ALU.add, ALU.mult).then_inc(s_sg, 1)
                        dve.wait_ge(s_sg, 2 * j + 1)
                        nc.vector.reciprocal(sg[:, 1, :], sg[:, 0, :]).then_inc(s_sg, 1)

                    def back_yg(j):
                        dve.wait_ge(s_acc, NS * j + NS)
                        dve.wait_ge(s_sg, 2 * j + 2)
                        dve.wait_ge(K["op"], j)
                        nc.vector.tensor_tensor(yg[:], y[:, 1, :], sg[:, 1, :], ALU.mult).then_inc(K["yg"], 1)

                    def back_residual(j):
                        st = Steps(dve, bd, BD, j)
                        dve.wait_ge(K["op"], j + 1)
                        for i in range(4):
                            x, r = rows_of(i, j, (H, H_img))
                            last = nc.vector.tensor_tensor(x, pb[4 + i // 2][0:r, (i % 2) * D:(i % 2 + 1) * D], x, ALU.add)
                        last.then_inc(K["h2"], 1)
                        dve.wait_ge(s_set, 1)
                        dve.wait_ge(K["h2"], j + 1)
                        st.done(statistics(j, K["bn"], j + 1, mv_b))
                        st.wait()
                        nc.vector.tensor_scalar(sm[:, 0, :], mv_b[:, :, 1], EPS, None, ALU.add)
                        nc.vector.tensor_scalar(sm[:, 1, :], mv_b[:, :, 1], float(D), None, ALU.mult).then_inc(K["var"], 1)

                    def back_norm(j):
                        st = Steps(dve, bd, BD, j)
                        st.n = 1
                        dve.wait_ge(K["pw"], j + 1)
                        st.done(nc.vector.tensor_tensor(sm[:, 4, :], sm[:, 2, :], sm[:, 3, :], ALU.mult))
                        st.wait()
                        st.done(nc.vector.tensor_scalar(sm[:, 5, :], sm[:, 4, :], 1e-6, None, ALU.add))
                        st.wait()
                        st.done(nc.vector.reciprocal(sm[:, 6, :], sm[:, 5, :]))
                        st.wait()
                        st.done(nc.vector.tensor_tensor(sm[:, 7, :], sm[:, 6, :], sm[:, 2, :], ALU.mult))
                        st.wait()
                        dve.wait_ge(K["x"], j)
                        normalise(j, mv_b, sm[:, 7, :], zn_t, zn_i).then_inc(K["zn"], 1)

                    def back_max(j):
                        st = Steps(dve, bd, BD, j)
                        st.n = 5
                        dve.wait_ge(K["L"], j + 1)
                        logits = pb[4][:, 0:4 * SLOTS].rearrange("p (i k) -> p i k", i=4)
                        st.done(nc.vector.tensor_reduce(cmax[:, 0, :], logits, AX.X, ALU.max))
                        nc.vector.tensor_reduce(dmax[:, 0, :], pb[5][0:SLOTS, 0:W2T].rearrange("p (s t) -> p s t", s=2), AX.X, ALU.max, negate=True)
                        st.wait()
                        nc.vector.tensor_tensor(cexp[:, 0], logits, cmax[:, 0, :].unsqueeze(2).to_broadcast([P, 4, SLOTS]),
                                                ALU.subtract).then_inc(K["mx"], 1)

                    def back_softmax(j):
                        st = Steps(dve, bd, BD, j)
                        st.n = 6
                        dve.wait_ge(K["e"], j + 1)
                        dview = dexp[:, 0, :].rearrange("p (s t) -> p s t", s=2)
                        st.done(nc.vector.tensor_reduce(cmax[:, 1, :], cexp[:, 1], AX.X, ALU.add))
                        st.done(nc.vector.tensor_reduce(dmax[:, 1, :], dview, AX.X, ALU.add))
                        st.wait(st.n - 1)
                        st.done(nc.vector.reciprocal(cmax[:, 2, :], cmax[:, 1, :]))
                        st.wait(st.n - 1)
                        st.done(nc.vector.reciprocal(dmax[:, 2, :], dmax[:, 1, :]))
                        st.wait(st.n - 1)
                        dve.wait_ge(K["T3"], j)
                        nc.vector.tensor_tensor(cexp[:, 2], cexp[:, 1], cmax[:, 2, :].unsqueeze(2).to_broadcast([P, 4, SLOTS]), ALU.mult)
                        st.wait()
                        nc.vector.tensor_tensor(dexp[:, 1, :].rearrange("p (s t) -> p s t", s=2), dview,
                                                dmax[:, 2, :].unsqueeze(2).to_broadcast([SLOTS, 2, T]), ALU.mult).then_inc(K["cd"], 1)

                    def back_dtok(j):
                        dve.wait_ge(K["T3"], j + 1)
                        dve.wait_ge(K["x"], j)
                        nc.vector.tensor_copy(d_tok[:].rearrange("p i k -> p (i k)"), pb[5][:, 0:4 * SLOTS]).then_inc(K["dT"], 1)

                    def input_of(j, n):
                        m = NS * j + n
                        dve.wait_ge(s_B, m + 1)
                        nc.vector.tensor_tensor(inp[:, n % 2, :], pb[n % 2][:, 0:W3T], dtu[:], ALU.mult).then_inc(s_in, 1)

                    def scan_steps(j, first, last_pair):
                        take_dt(j)
                        dve.wait_ge(s_dtu, j + 1)
                        input_of(j, 0)
                        for n in range(NS):
                            m = NS * j + n
                            dve.wait_ge(s_a, m + 1)
                            dve.wait_ge(s_in, m + 1)
                            nc.vector.tensor_tensor_scan(state[:, n % 2, :], decay[:, n % 2].rearrange("p a t -> p (a t)"), inp[:, n % 2, :], 0.0,
                                                         ALU.mult, ALU.add).then_inc(s_scan, 1)
                            if n + 1 < NS:
                                input_of(j, n + 1)
                            dve.wait_ge(s_C, m + 1)
                            dve.wait_ge(s_scan, m + 1)
                            if n >= 2 or not first:
                                dve.wait_ge(s_acc, m - 1)
                            nc.vector.tensor_tensor(cstate[:, n % 2, :], pb[2 + n % 2][:, 0:W3T], state[:, n % 2, :], ALU.mult).then_inc(s_cs, 1)
                            if n == 0 and not last_pair:
                                front_norm_a(j + 1)
                            if n == 1:
                                if not last_pair:
                                    front_norm_b(j + 1)
                                if not first:
                                    back_yg(j - 1)
                                gate(j)
                            if not last_pair:
                                if n == 5:
                                    front_conv(j + 1)
                                if n == 8:
                                    front_low(j + 1)
                                    front_dt(j + 1)
                            if not first:
                                if n == 3:
                                    back_residual(j - 1)
                                if n == 4:
                                    back_norm(j - 1)
                                if n == 7:
                                    back_max(j - 1)
                                if n == 8:
                                    back_softmax(j - 1)
                                if n == 10:
                                    back_dtok(j - 1)

                    nc.vector.memset(mv_f[:], 1.0)
                    nc.vector.memset(mv_b[:], 1.0)
                    nc.vector.memset(xT1[:], 1.0)
                    nc.vector.memset(uc1_n[:], 1.0)
                    nc.vector.memset(u16_n[:], 1.0)
                    nc.vector.memset(yg1[:], 1.0)
                    nc.vector.memset(u_pad[:], 0.0)
                    nc.vector.memset(decay[:], 0.0).then_inc(s_set, 1)
                    dve.wait_ge(s_set, 1)
                    front_norm_a(0)
                    front_norm_b(0)
                    front_conv(0)
                    front_low(0)
                    front_dt(0)
                    scan_steps(0, True, False)
                    with dve.Fori(1, NPAIR - 1) as j:
                        scan_steps(j, False, False)
                    scan_steps(NPAIR - 1, False, True)
                    for piece in (back_yg, back_residual, back_norm, back_max, back_softmax, back_dtok):
                        piece(NPAIR - 1)

                @block.gpsimd
                def _(pool):
                    def front_rs(j):
                        pool.wait_ge(F["var"], j + 1)
                        pool.wait_ge(F["xn"], j)
                        nc.gpsimd.tensor_tensor(rs_f[:], ve_f[:], half4[:, 0, :], ALU.pow).then_inc(F["rs"], 1)

                    def back_pw(j):
                        pool.wait_ge(K["var"], j + 1)
                        pool.wait_ge(K["zn"], j)
                        nc.gpsimd.tensor_tensor(sm[:, 2, :], sm[:, 0, :], half4[:, 0, :], ALU.pow)
                        nc.gpsimd.tensor_tensor(sm[:, 3, :], sm[:, 1, :], half4[:, 1, :], ALU.pow).then_inc(K["pw"], 1)

                    def scan_steps(j, first, last_pair):
                        for n in range(NS):
                            m = NS * j + n
                            if n == 1 and not last_pair:
                                front_rs(j + 1)
                            if n == 4 and not first:
                                back_pw(j - 1)
                            pool.wait_ge(s_cs, m + 1)
                            if n == 0:
                                pool.wait_ge(F["y0"], j + 1)
                                pool.wait_ge(s_acc, NS * j)
                                src = y0[:].rearrange("p a t -> p (a t)")
                            else:
                                pool.wait_ge(s_acc, m)
                                src = y[:, (n - 1) % 2, :]
                            if n == 1:
                                pool.wait_ge(K["yg"], j)
                            nc.gpsimd.tensor_tensor(y[:, n % 2, :], src, cstate[:, n % 2, :], ALU.add).then_inc(s_acc, 1)

                    front_rs(0)
                    scan_steps(0, True, False)
                    with pool.Fori(1, NPAIR - 1) as j:
                        scan_steps(j, False, False)
                    scan_steps(NPAIR - 1, False, True)
                    back_pw(NPAIR - 1)

        slot_experts(nc, io, sem, H, H_img, xt0, xt1, c_all, pb)


def slot_experts(nc, io, sem, H, H_img, xt0, xt1, c_all, pb):
    with ExitStack() as ctx:
        def sb(name, shape, dt=F32):
            return ctx.enter_context(nc.sbuf_tensor(name, shape, dt))

        wd0, wd1 = sb("wd0", [P, NE, HID]), sb("wd1", [D1 + 1, NE, HID])
        wu = sb("wu", [HID + 1, NE, D])
        hid = sb("hid", [HID + 8, NE, P])
        y_rows = sb("y_rows", [P, NE, D])
        y_slots = sb("y_slots", [SLOTS, B, D])
        ct = sb("ct", [SLOTS, 2, W2T])
        out_t, out_i = sb("out_t", [P, 2, 2, D]), sb("out_i", [N_IMG, 2, 2, D])
        x_w, x_one = sem("expert_weights"), sem("expert_ones")
        x_h, x_g, x_y, x_ye = sem("expert_hidden"), sem("expert_gelu"), sem("expert_y"), sem("expert_y_copied")
        x_scr, x_sl = sem("slots_written"), sem("slots_loaded_back")
        o_ct, o_mm, o_sum = sem("out_c_copied"), sem("out_product"), sem("out_summed")
        o_st = [sem(f"out_stored{i}") for i in range(2)]
        out = io["out"]
        with nc.Block() as block:
            @block.sync
            def _(sp):
                sp.dma_start(wd0[:], io["wd"][0:P]).then_inc(x_w, 16)
                sp.dma_start(wd1[:], io["wd"][P:D + 1]).then_inc(x_w, 16)
                sp.dma_start(wu[:], io["wu"]).then_inc(x_w, 16)
                sp.wait_ge(x_ye, NE // 2)
                sp.dma_start(io["scratch_y"], y_rows[:].rearrange("p e d -> p (e d)")).then_inc(x_scr, 16)
                sp.wait_ge(x_scr, 16)
                for e in range(NE):
                    sp.dma_start(y_slots[NP_ * e:NP_ * (e + 1)],
                                 io["scratch_y"].rearrange("(b p) (e d) -> e p b d", p=NP_, e=NE)[e]).then_inc(x_sl, 16)

                def store(j, par):
                    sp.wait_ge(o_sum, j + 1)
                    sp.dma_start(out[bass.ds(2 * j, 2), N_IMG:T, :].rearrange("b t d -> t b d"), out_t[:, par]).then_inc(o_st[par], 16)
                    sp.dma_start(out[bass.ds(2 * j, 2), 0:N_IMG, :].rearrange("b t d -> t b d"), out_i[:, par]).then_inc(o_st[par], 16)

                with sp.Fori(0, NPAIR // 2) as i:
                    store(2 * i, 0)
                    store(2 * i + 1, 1)
                for stored in o_st:
                    sp.wait_ge(stored, 16 * NPAIR)

            @block.tensor
            def _(pe):
                pe.wait_ge(x_w, 48)
                for e in range(NE):
                    o = pb[e // 4][0:HID, (e % 4) * P:(e % 4 + 1) * P].rearrange("h (b p) -> h b p", p=NP_)
                    nc.tensor.matmul(o, wd0[:, e, :], xt0[:, :, NP_ * e:NP_ * (e + 1)], start=True, stop=False)
                    last = nc.tensor.matmul(o, wd1[:, e, :], xt1[:, :, NP_ * e:NP_ * (e + 1)], start=False, stop=True)
                    if e % 4 == 3:
                        last.then_inc(x_h, 1)
                for e in range(NE):
                    if e % 4 == 0:
                        pe.wait_ge(x_g, e // 4 + 1)
                    last = nc.tensor.matmul(pb[2 + e // 2][:, (e % 2) * D:(e % 2 + 1) * D], hid[0:HID + 1, e, :], wu[:, e, :], start=True, stop=True)
                    if e % 2:
                        last.then_inc(x_y, 1)
                pe.wait_ge(x_sl, 16 * NE)
                pe.wait_ge(x_ye, NE // 2)

                def product(j, par):
                    pe.wait_ge(o_ct, j + 1)
                    if not (isinstance(j, int) and j < 2):
                        pe.wait_ge(o_sum, j - 1)
                    for s in range(2):
                        rhs = y_slots[:, bass.ds(2 * j + s, 1), :].rearrange("k b d -> k (b d)")
                        c = s * T
                        nc.tensor.matmul(pb[2 * par][:, s * D:(s + 1) * D], ct[:, par, c + N_IMG:c + T], rhs, start=True, stop=True)
                        last = nc.tensor.matmul(pb[2 * par + 1][:, s * D:(s + 1) * D], ct[:, par, c:c + P], rhs, start=True, stop=True)
                    last.then_inc(o_mm, 1)

                product(0, 0)
                product(1, 1)
                with pe.Fori(1, NPAIR // 2) as i:
                    product(2 * i, 0)
                    product(2 * i + 1, 1)

            @block.scalar
            def _(act):
                act.wait_ge(x_one, 1)
                for i in range(2):
                    act.wait_ge(x_h, i + 1)
                    nc.scalar.activation(hid[0:HID, 4 * i:4 * i + 4, :], pb[i][0:HID, :].rearrange("h (e n) -> h e n", e=4), ACT.Gelu).then_inc(x_g, 1)

                def copy_c(j, par):
                    if not (isinstance(j, int) and j < 2):
                        act.wait_ge(o_mm, j - 1)
                    nc.scalar.copy(ct[:, par, :], c_all[:, bass.ds(j, 1), :].rearrange("k a t -> k (a t)")).then_inc(o_ct, 1)

                copy_c(0, 0)
                copy_c(1, 1)
                with act.Fori(1, NPAIR // 2) as i:
                    copy_c(2 * i, 0)
                    copy_c(2 * i + 1, 1)

            @block.vector
            def _(dve):
                nc.vector.memset(hid[:], 1.0).then_inc(x_one, 1)
                for i in range(NE // 2):
                    dve.wait_ge(x_y, i + 1)
                    nc.vector.tensor_copy(y_rows[:, 2 * i:2 * i + 2, :], pb[2 + i][:, 0:2 * D].rearrange("p (e d) -> p e d", e=2)).then_inc(x_ye, 1)

                def total(i, par):
                    j = 2 * i + par
                    dve.wait_ge(o_mm, j + 1)
                    dve.wait_ge(o_st[par], 32 * i)
                    nc.vector.tensor_tensor(out_t[:, par], pb[2 * par][:, 0:2 * D].rearrange("p (s d) -> p s d", s=2),
                                            H[:, bass.ds(2 * j, 2), :], ALU.add)
                    nc.vector.tensor_tensor(out_i[:, par], pb[2 * par + 1][0:N_IMG, 0:2 * D].rearrange("p (s d) -> p s d", s=2),
                                            H_img[:, bass.ds(2 * j, 2), :], ALU.add).then_inc(o_sum, 1)

                with dve.Fori(0, NPAIR // 2) as i:
                    total(i, 0)
                    total(i, 1)


def ssm_layout(x):
    def bias_row(w, b):
        return np.concatenate([w, b[None]], axis=0)

    def mixed(a):
        return np.stack([a[:P], np.concatenate([a[P:], a[P:]])], axis=1)

    def by_state(w, b):
        w = bias_row(w, b)
        return np.ascontiguousarray(w.reshape(D + 1, D, NS).transpose(0, 2, 1))

    wconv = np.concatenate([x["L0_attn_Wconv"], x["L0_attn_bconv"][:, None], x["L0_attn_D"][:, None]], axis=1)
    wd = np.concatenate([x["L0_ffn_W_down"], x["L0_ffn_b_down"][:, None, :]], axis=1).transpose(1, 0, 2)
    wu = np.concatenate([x["L0_ffn_W_up"], x["L0_ffn_b_up"][:, None, :]], axis=1).transpose(1, 0, 2)
    return dict(
        wi=bias_row(x["L0_attn_Wi"], x["L0_attn_bi"]), wdt=bias_row(x["L0_attn_Wdt"], x["L0_attn_bdt"]),
        wso=bias_row(x["L0_attn_Wo"], x["L0_attn_bo"]), wB=by_state(x["L0_attn_WB"], x["L0_attn_bB"]),
        wC=by_state(x["L0_attn_WC"], x["L0_attn_bC"]), a_log=mixed(x["L0_attn_A_log"]), wconv=mixed(wconv),
        slot_params=x["L0_ffn_slot_params"].reshape(D, SLOTS), slot_scale=x["L0_ffn_scale"].reshape(1),
        wd=wd, wu=wu)


def build(nc, io):
    with ExitStack() as ctx:
        def sb(name, shape, dt=F32):
            return ctx.enter_context(nc.sbuf_tensor(name, shape, dt))

        def sem(name):
            return ctx.enter_context(nc.semaphore(name))

        H = sb("H", [P, B, D])
        H_img = sb("H_img", [N_IMG, B, D])
        ident = sb("ident", [P, P])
        ident_bf = sb("ident_bf", [P, P], BF16)
        band_f = sb("band_f", [P, P])
        band = sb("band", [P, P], BF16)
        half = sb("half", [P, 1])
        s_id = sem("identity_loaded")
        with nc.Block() as block:
            @block.sync
            def _(sp):
                sp.dma_start(ident[:], io["ident"]).then_inc(s_id, 16)
                sp.dma_start(band_f[:], io["band"]).then_inc(s_id, 16)

            @block.vector
            def _(dve):
                nc.vector.memset(half[:], -0.5)
                dve.wait_ge(s_id, 32)
                nc.vector.tensor_copy(ident_bf[:], ident[:])
                nc.vector.tensor_copy(band[:], band_f[:])
        consts = dict(ident=ident, ident_bf=ident_bf, band=band, half=half)
        patch_embedding(nc, io, sem, H_img, consts)
        text_encoder(nc, io, sem, H, consts)
        ssm_and_slots(nc, io, sem, H, H_img, consts)


def kernel(**inputs):
    import concourse.bacc as _bacc
    from concourse.bass_utils import run_bass_kernel_spmd as _run

    x = {k: np.asarray(v) for k, v in inputs.items()}
    far = np.abs(np.arange(P)[:, None] - np.arange(P)[None, :]) > WIN
    arrays = {**text_layout(x), **tok_layout(x), **ssm_layout(x),
              "ident": np.eye(P, dtype=np.float32), "band": np.where(far, MASKED, 0.0).astype(np.float32)}
    nc = _bacc.Bacc("TRN2", target_bir_lowering=False, num_devices=1)
    io, feeds = {}, {}
    for name, a in arrays.items():
        a = np.ascontiguousarray(a)
        feeds[f"in_{name}"] = a
        io[name] = nc.dram_tensor(f"in_{name}", a.shape, mybir.dt.from_np(a.dtype), kind="ExternalInput").ap()
    io["out"] = nc.dram_tensor("out_h", (B, T, D), F32, kind="ExternalOutput").ap()
    io["scratch_tok"] = nc.dram_tensor("scratch_tok", (6 * B, 6 * D), F32, kind="Internal").ap()
    io["scratch_y"] = nc.dram_tensor("scratch_y", (P, NE * D), F32, kind="Internal").ap()
    build(nc, io)
    r = _run(nc, [feeds], core_ids=[0])
    return r.results[0]["out_h"]
```

```python
from contextlib import ExitStack

import numpy as np

import concourse.bass as bass
from concourse import mybir

ALU = mybir.AluOpType
ACT = mybir.ActivationFunctionType
AX = mybir.AxisListType
F32 = mybir.dt.float32
BF16 = mybir.dt.bfloat16
F16 = mybir.dt.float16
I32 = mybir.dt.int32

P = 128
D = 192
D1 = D - P
B = 32
S = 128
N_IMG = 36
T = N_IMG + S
L = 4
NH = 12
DH = D // NH
FF = 4 * D
NF = FF // P
WIN = 64
N_PAD = WIN
EPS_TXT = 1e-12
EPS = 1e-5
MASKED = -999292928.0
NS = 16
KC = 4
W_SCALE = 64.0
SLOTS = 32
NE = 8
NP_ = 4
HID = 24


HEADS_OF_GROUP = [(2, 3, 8), (6, 7, 9), (0, 1, 10), (4, 5, 11)]
ROW_GROUP = (1, 3, 0, 2)


QKV = 5 * P + D
PASSES = ((0, 0, P), (1, 0, P), (0, 1, P), (2, 2, P), (3, 3, 97))


def text_encoder(nc, io, sem, H, consts):
    ident, ident_bf, ident_h, band, half = (consts[k] for k in ("ident", "ident_bf", "ident_h", "band", "half"))
    with ExitStack() as ctx:
        def sb(name, shape, dt=F32):
            return ctx.enter_context(nc.sbuf_tensor(name, shape, dt))

        def psum(name, shape, dt=F32):
            return ctx.enter_context(nc.psum_tensor(name, shape, dt))

        key_bias = sb("key_bias", [P, B, S], BF16)
        w_qkv_raw, w_qkv = sb("w_qkv_raw", [P, 3, QKV]), sb("w_qkv", [P, 4, QKV], F16)
        w_qkv_high3 = sb("w_qkv_high3", [P, QKV], F16)
        wo0, wo1 = sb("wo0", [P, D]), sb("wo1", [D1 + 1, D])
        w1_raw, w2_raw = sb("w1_raw", [P, 3, FF]), sb("w2_raw", [P, NF, D])
        w1 = sb("w1", [P, 4, FF], F16)
        w1_high3 = sb("w1_high3", [P, FF], F16)
        w2 = sb("w2", [P, 2, NF, D], F16)
        low_scale = sb("low_scale", [P, 1])
        b2_rows = sb("b2_rows", [P, D])
        ln1_s, ln1_b = sb("ln1_s", [P, D]), sb("ln1_b", [P, D])
        ln2_s, ln2_b = sb("ln2_s", [P, D]), sb("ln2_b", [P, D])
        x16 = sb("x16", [P, 2, 2, D], F16)
        xT16 = sb("xT16", [P, 2, 4, S], F16)
        v_sb = sb("v_sb", [P, 2, NH // 2, 3 * DH])
        oT0, oT1 = sb("oT0", [P, S]), sb("oT1", [D1 + 1, S])
        xres = sb("xres", [P, 2, D])
        stats = sb("stats", [P, 6])
        mv = sb("mv", [P, 2, 2])
        rstd = sb("rstd", [P, 1])
        var_eps = sb("var_eps", [P, 2])
        ln_y = sb("ln_y", [P, 3, D])
        bank = [psum(f"txt_bank{i}", [P, 512]) for i in range(8)]

        def norm_rows(pool, chain, n, x, mean, var_eps, scale, shift, out):
            nc.gpsimd.tensor_tensor(rstd[:], var_eps, half[:], ALU.pow).then_inc(chain, 1)
            nc.gpsimd.tensor_tensor(ln_y[:, 0, :], x, mean.to_broadcast([P, D]), ALU.subtract).then_inc(chain, 1)
            pool.wait_ge(chain, n + 2)
            nc.gpsimd.tensor_tensor(ln_y[:, 1, :], ln_y[:, 0, :], rstd[:].to_broadcast([P, D]), ALU.mult).then_inc(chain, 1)
            pool.wait_ge(chain, n + 3)
            nc.gpsimd.tensor_tensor(ln_y[:, 2, :], ln_y[:, 1, :], scale, ALU.mult).then_inc(chain, 1)
            pool.wait_ge(chain, n + 4)
            return nc.gpsimd.tensor_tensor(out, ln_y[:, 2, :], shift, ALU.add)

        s_const, s_zero = sem("txt_constants_set"), sem("raw_weights_zeroed")
        f_h = sem("layer_h_written")
        with ExitStack() as emb_ctx:
            def tmp(name, shape, dt=F32):
                return emb_ctx.enter_context(nc.sbuf_tensor(name, shape, dt))
            ids = tmp("ids", [P, B], I32)
            ids_f = tmp("ids_f", [P, 3, B])
            rows_of = tmp("rows_of", [P, B], I32)
            pos = tmp("pos", [P, D])
            mask_i = tmp("mask_i", [P, B * S], I32)
            emb_s, emb_b = tmp("emb_s", [P, D]), tmp("emb_b", [P, D])
            s_ids = sem("txt_ids_loaded")
            s_rows = sem("txt_rows_known")
            s_gath = sem("txt_rows_gathered")
            s_loads = sem("txt_small_loads")
            s_dve = sem("txt_dve_steps")
            s_pool = sem("txt_pool_steps")
            s_stat = sem("txt_emb_stats")
            with nc.Block() as block:
                @block.sync
                def _(sp):
                    sp.dma_start(ids[:], io["ids"]).then_inc(s_ids, 16)
                    sp.dma_start(pos[:], io["pos"]).then_inc(s_loads, 16)
                    sp.dma_start(emb_s[:], io["emb_ln_s"].partition_broadcast(P)).then_inc(s_loads, 16)
                    sp.dma_start(emb_b[:], io["emb_ln_b"].partition_broadcast(P)).then_inc(s_loads, 16)
                    sp.dma_start(mask_i[:], io["mask"].partition_broadcast(P)).then_inc(s_loads, 16)

                @block.vector
                def _(dve):
                    V = io["emb"].shape[0]
                    dve.wait_ge(s_ids, 16)
                    nc.vector.tensor_copy(ids_f[:, 0, :], ids[:]).then_inc(s_dve, 1)
                    dve.wait_ge(s_dve, 1)
                    nc.vector.tensor_scalar(ids_f[:, 1, :], ids_f[:, 0, :], 0.0, float(V),
                                            ALU.is_lt, ALU.mult).then_inc(s_dve, 1)
                    dve.wait_ge(s_dve, 2)
                    nc.vector.tensor_tensor(ids_f[:, 2, :], ids_f[:, 0, :], ids_f[:, 1, :], ALU.add).then_inc(s_dve, 1)
                    dve.wait_ge(s_dve, 3)
                    nc.vector.tensor_scalar(rows_of[:], ids_f[:, 2, :], 0.0, float(V - 1), ALU.max, ALU.min).then_inc(s_rows, 1)
                    nc.vector.memset(v_sb[:], 0.0)
                    nc.vector.memset(xT16[:], 1.0)
                    nc.vector.memset(w1_raw[:, 2], 0.0)
                    nc.vector.memset(w_qkv_raw[:, 2], 0.0)
                    nc.vector.memset(low_scale[:D1], W_SCALE)
                    nc.vector.memset(low_scale[D1:96], 0.0)
                    nc.vector.memset(low_scale[96:], W_SCALE).then_inc(s_zero, 1)
                    nc.vector.memset(oT1[:], 1.0).then_inc(s_const, 1)
                    dve.wait_ge(s_loads, 64)
                    nc.vector.tensor_scalar(key_bias[:].rearrange("p b s -> p (b s)"), mask_i[:], 0.0, MASKED,
                                            ALU.is_le, ALU.mult).then_inc(s_dve, 1)
                    dve.wait_ge(s_dve, 4)
                    nc.vector.tensor_tensor(key_bias[:], key_bias[:], band[:].unsqueeze(1).to_broadcast([P, B, S]),
                                            ALU.min).then_inc(s_dve, 1)
                    dve.wait_ge(s_gath, 16 * B)
                    for b in range(B):
                        if b >= 2:
                            dve.wait_ge(f_h, b - 1)
                        nc.vector.tensor_tensor(xres[:, b % 2, :], H[:, b, :], pos[:], ALU.add).then_inc(s_dve, 1)
                        dve.wait_ge(s_dve, 6 + 3 * b)
                        nc.vector.bn_stats(stats[:], xres[:, b % 2, :]).then_inc(s_dve, 1)
                        dve.wait_ge(s_dve, 7 + 3 * b)
                        nc.vector.bn_aggr(mv[:, b % 2, :], stats[:]).then_inc(s_dve, 1)
                        dve.wait_ge(s_dve, 8 + 3 * b)
                        nc.vector.tensor_scalar(var_eps[:, b % 2:b % 2 + 1], mv[:, b % 2, 1:2], EPS_TXT, None, ALU.add).then_inc(s_stat, 1)

                @block.gpsimd
                def _(pool):
                    pool.wait_ge(s_rows, 1)
                    for b in range(B):
                        nc.gpsimd.indirect_dma_start(
                            out=H[:, b, :], out_offset=None, in_=io["emb"],
                            in_offset=bass.IndirectOffsetOnAxis(ap=rows_of[:, b:b + 1], axis=0)).then_inc(s_gath, 16)
                    pool.wait_ge(s_loads, 64)
                    for b in range(B):
                        pool.wait_ge(s_stat, b + 1)
                        norm_rows(pool, s_pool, 4 * b, xres[:, b % 2, :], mv[:, b % 2, 0:1], var_eps[:, b % 2:b % 2 + 1],
                                  emb_s[:], emb_b[:], H[:, b, :]).then_inc(f_h, 1)

        q_sb, k_sb = sb("q_sb", [P, 3, S]), sb("k_sb", [P, 2, S])
        neg_max = sb("neg_max", [P, 4, 3])
        pad_exp, sums = sb("pad_exp", [P, 4, 3]), sb("sums", [P, 4, 3])
        den = sb("den", [P, 2, 4, 3])
        probs = sb("probs", [P, 4, 3, S])
        pT = sb("pT", [P, 2, 3 * S])
        fT, fT16 = sb("fT", [P, 2, NF * S]), sb("fT16", [P, 2, 2, NF * S], F16)

        w_attn, w_ffn = sem("attn_weights"), sem("ffn_weights")
        a_high, a_low = sem("attn_weights_high"), sem("attn_weights_low")
        s_xh, s_xin, s_hTp, s_hT = sem("attn_x_high"), sem("attn_x_copied"), sem("attn_xT_done"), sem("attn_xT_copied")
        s_sc, s_max, s_exp, s_pad = sem("scores_done"), sem("max_done"), sem("exp_done"), sem("pad_exp_done")
        s_q, s_kv = sem("q_done"), sem("kv_done")
        s_qe, s_ke, s_ve = sem("q_copied"), sem("k_copied"), sem("v_copied")
        s_pTp, s_pTe, s_pv = sem("probsT_done"), sem("probsT_copied"), sem("pv_done")
        s_den, s_norm, s_oTe = sem("denominator_steps"), sem("probs_normalised"), sem("oT_copied")
        s_wo, s_xadd, s_st, s_stat = sem("wo_done"), sem("attn_added"), sem("attn_bn"), sem("attn_stats")
        s_h, s_pc = sem("attn_h_written"), sem("attn_pool_steps")
        s_ag, f_ag = sem("attn_aggr"), sem("ffn_aggr")
        f_xin, f_T, f_hT = sem("ffn_x_copied"), sem("ffn_xT_done"), sem("ffn_xT_copied")
        f_1, f_g, f_2 = sem("ffn1_done"), sem("gelu_done"), sem("ffn2_done")
        f_c, f_st, f_stat = sem("ffn_added"), sem("ffn_bn"), sem("ffn_stats")
        f_pc = sem("ffn_pool_steps")
        N_WA = 10
        N_WF = 10
        f_high, f_low = sem("ffn_weights_high"), sem("ffn_weights_low")
        f_xh, f_fh, f_fl = sem("ffn_x_high"), sem("gelu_high"), sem("gelu_low")
        with nc.Block() as block:
            @block.sync
            def _(sp):
                def load_attn(l):
                    w = io["wqkv"][l]
                    for dst, src in ((w_qkv_raw[:, 0], w[0:P]), (w_qkv_raw[0:D1, 1], w[P:D]), (w_qkv_raw[D1:P, 1], w[P:D]),
                                     (w_qkv_raw[0:D1, 2], w[P:D]), (w_qkv_raw[D1:D1 + 1, 2], w[D:D + 1]), (w_qkv_raw[96:97, 2], w[D:D + 1]),
                                     (wo0[:], io["wo"][l, 0:P]), (wo1[:], io["wo"][l, P:D + 1]),
                                     (ln1_s[:], io["ln1_s"][l].partition_broadcast(P)),
                                     (ln1_b[:], io["ln1_b"][l].partition_broadcast(P))):
                        sp.dma_start(dst, src).then_inc(w_attn, 16)

                def load_ffn(l):
                    for dst, src in ((w1_raw[:, 0], io["w1"][l, 0:P]), (w1_raw[0:D1, 1], io["w1"][l, P:D]),
                                     (w1_raw[D1:P, 1], io["w1"][l, P:D]), (w1_raw[0:D1, 2], io["w1"][l, P:D]),
                                     (w1_raw[D1:D1 + 1, 2], io["w1"][l, D:D + 1]), (w1_raw[96:97, 2], io["w1"][l, D:D + 1]),
                                     (w2_raw[:], io["w2"][l].rearrange("(c p) n -> p c n", p=P)),
                                     (b2_rows[:], io["b2"][l].partition_broadcast(P)),
                                     (ln2_s[:], io["ln2_s"][l].partition_broadcast(P)),
                                     (ln2_b[:], io["ln2_b"][l].partition_broadcast(P))):
                        sp.dma_start(dst, src).then_inc(w_ffn, 16)

                sp.wait_ge(s_zero, 1)
                load_attn(0)
                load_ffn(0)
                with sp.Fori(1, L) as l:
                    sp.wait_ge(s_h, B * l)
                    load_attn(l)
                    sp.wait_ge(f_h, B * l + B)
                    load_ffn(l)

            @block.tensor
            def _(pe):
                def x_transposed(b, par, done):
                    for part, half_of_x, at, row in ((0, 0, slice(0, P), 0), (1, 1, slice(0, P), 0), (2, 0, slice(P, D), 0),
                                                     (2, 1, slice(P, D), D1), (3, 0, slice(P, D), 0)):
                        rows = at.stop - at.start
                        last = nc.tensor.matmul(b[row:row + rows, part * S:(part + 1) * S], x16[:, par, half_of_x, at], ident_h[:],
                                                start=True, stop=True)
                    last.then_inc(done, 1)

                def attn_x_transposed(g, par):
                    pe.wait_ge(s_xin, g + 1)
                    x_transposed(bank[7], par, s_hTp)

                def project_q(g, par):
                    pe.wait_ge(s_hT, g + 1)
                    for t in range(3):
                        for k, (a, b, rows) in enumerate(PASSES):
                            last = nc.tensor.matmul(bank[4][:, t * S:(t + 1) * S], w_qkv[0:rows, a, t * P:(t + 1) * P], xT16[0:rows, par, b, :],
                                                    start=(k == 0), stop=(k == len(PASSES) - 1))
                    last.then_inc(s_q, 1)

                def project_kv(g, par):
                    pe.wait_ge(s_hT, g + 1)
                    for t in (3, 4):
                        for k, (a, b, rows) in enumerate(PASSES):
                            nc.tensor.matmul(bank[5][:, (t - 3) * S:(t - 2) * S], w_qkv[0:rows, a, t * P:(t + 1) * P], xT16[0:rows, par, b, :],
                                             start=(k == 0), stop=(k == len(PASSES) - 1))
                    for k, (a, b, rows) in enumerate(PASSES):
                        last = nc.tensor.matmul(bank[5][:, 256:256 + D], xT16[0:rows, par, b, :], w_qkv[0:rows, a, 5 * P:QKV],
                                                start=(k == 0), stop=(k == len(PASSES) - 1))
                    last.then_inc(s_kv, 1)

                def scores(g, u, first):
                    pe.wait_ge(s_qe, g + 1)
                    pe.wait_ge(s_ke, g + 1)
                    for r0 in (0, 2):
                        for r in (r0, r0 + 1):
                            if not first:
                                pe.wait_ge(s_exp, 4 * g - 3 + r)
                            nc.tensor.matmul(bank[r][:, 0:3 * S].rearrange("p (i s) -> p i s", i=3), ident_bf[:],
                                             key_bias[:, bass.ds(u, 1), :].to_broadcast([P, 3, S]),
                                             start=True, stop=True)
                        for i, (qt, kt) in enumerate(((0, 0), (1, 0), (2, 1))):
                            for r in (r0, r0 + 1):
                                at = slice(32 * ROW_GROUP[r], 32 * ROW_GROUP[r] + 32)
                                last = nc.tensor.matmul(bank[r][:, i * S:(i + 1) * S], q_sb[at, qt, :], k_sb[at, kt, :],
                                                        start=False, stop=True, skip_group_check=True)
                        last.then_inc(s_sc, 1)

                def probs_transposed(g, r):
                    pe.wait_ge(s_norm, 4 * g + r + 1)
                    for i in range(3):
                        last = nc.tensor.transpose(bank[6 + r % 2][:, i * S:(i + 1) * S], probs[:, r, i, :], ident[:])
                    last.then_inc(s_pTp, 1)

                def outputs(g, r0, par):
                    pe.wait_ge(s_ve, g + 1)
                    pe.wait_ge(s_pTe, 4 * g + r0 + 2)
                    for i, r in ((0, r0), (0, r0 + 1), (2, r0), (1, r0), (1, r0 + 1), (2, r0 + 1)):
                        h = HEADS_OF_GROUP[r][i]
                        pair, odd = h // 2, h % 2
                        row = 32 * pair if pair < 4 else D1 + 32 * (pair - 4)
                        last = nc.tensor.matmul(bank[6 + pair // 4][row:row + 32, 3 * S:4 * S], v_sb[:, par, pair, DH * odd:DH * odd + 2 * DH],
                                                pT[:, r % 2, i * S:(i + 1) * S], start=(odd == 0), stop=(odd == 1),
                                                skip_group_check=True)
                    last.then_inc(s_pv, 1)

                def project_o(g):
                    pe.wait_ge(s_oTe, g + 1)
                    nc.tensor.matmul(bank[4][:, 0:D], oT0[:], wo0[:], start=True, stop=False)
                    nc.tensor.matmul(bank[4][:, 0:D], oT1[:], wo1[:], start=False, stop=True).then_inc(s_wo, 1)

                def attention_unit(l, u, par, first, more):
                    g = l * B + u
                    if more >= 1:
                        scores(g + 1, u + 1, False)
                    if not first:
                        pe.wait_ge(s_oTe, g)
                    if more >= 2:
                        pe.wait_ge(s_hT, g + 3)
                    for r in (0, 1):
                        probs_transposed(g, r)
                    if more >= 2:
                        pe.wait_ge(s_ve, g + 2)
                        project_kv(g + 2, par)
                    if not first:
                        project_o(g - 1)
                    outputs(g, 0, par)
                    for r in (2, 3):
                        probs_transposed(g, r)
                    if more >= 2:
                        if not first:
                            pe.wait_ge(s_xadd, g)
                        project_q(g + 2, par)
                    outputs(g, 2, par)
                    if more >= 3:
                        attn_x_transposed(g + 3, 1 - par)

                def ffn_x_transposed(w, par):
                    pe.wait_ge(f_xin, w + 1)
                    x_transposed(bank[0], par, f_T)

                def ffn_unit(l, u, par, first, last_unit, second=False):
                    w = l * B + u
                    if not last_unit:
                        pe.wait_ge(f_hT, w + 1)
                        ffn_x_transposed(w + 1, 1 - par)
                    pe.wait_ge(f_hT, w + 1)
                    for c in range(NF):
                        if c == 0 and not first:
                            pe.wait_ge(f_g, 2 * w - 1)
                        if c == 4 and not first:
                            pe.wait_ge(f_g, 2 * w)
                        out = bank[1 + c // 4][:, (c % 4) * S:(c % 4 + 1) * S]
                        for k, (a, b, rows) in enumerate(PASSES):
                            last = nc.tensor.matmul(out, w1[0:rows, a, c * P:(c + 1) * P], xT16[0:rows, par, b, :],
                                                    start=(k == 0), stop=(k == len(PASSES) - 1))
                        if c in (3, NF - 1):
                            last.then_inc(f_1, 1)
                    if not first:
                        ffn2(w - 1, 1 - par, second)

                def ffn2(w, par, first):
                    if not first:
                        pe.wait_ge(f_c, 2 * w - 1)
                    for c in range(NF):
                        if c in (0, 4):
                            pe.wait_ge(f_fl, 2 * w + 1 + c // 4)
                        for a, b in ((0, 0), (0, 1), (1, 0)):
                            last = nc.tensor.matmul(bank[3][:, 0:D], fT16[:, par, a, c * S:(c + 1) * S], w2[:, b, c, :],
                                                    start=(c + a + b == 0), stop=(c == NF - 1 and a == 1))
                    last.then_inc(f_2, 1)

                with pe.Fori(0, L) as l:
                    pe.wait_ge(f_h, B * l + B)
                    attn_x_transposed(l * B, 0)
                    pe.wait_ge(w_attn, 16 * N_WA * l + 16 * N_WA)
                    pe.wait_ge(a_low, l + 1)
                    project_kv(l * B, 0)
                    project_q(l * B, 0)
                    attn_x_transposed(l * B + 1, 1)
                    scores(l * B, 0, True)
                    pe.wait_ge(s_ve, l * B + 1)
                    project_kv(l * B + 1, 1)
                    project_q(l * B + 1, 1)
                    attn_x_transposed(l * B + 2, 0)
                    attention_unit(l, 0, 0, True, 3)
                    with pe.Fori(0, B // 2 - 2) as j:
                        attention_unit(l, 2 * j + 1, 1, False, 3)
                        attention_unit(l, 2 * j + 2, 0, False, 3)
                    for u in range(B - 3, B):
                        attention_unit(l, u, u % 2, False, B - 1 - u)
                    project_o(l * B + B - 1)
                    pe.wait_ge(s_h, B * l + B)
                    ffn_x_transposed(l * B, 0)
                    pe.wait_ge(f_low, 2 * l + 2)
                    ffn_unit(l, 0, 0, True, False)
                    ffn_unit(l, 1, 1, False, False, second=True)
                    with pe.Fori(1, B // 2 - 1) as j:
                        ffn_unit(l, 2 * j, 0, False, False)
                        ffn_unit(l, 2 * j + 1, 1, False, False)
                    ffn_unit(l, B - 2, 0, False, False)
                    ffn_unit(l, B - 1, 1, False, True)
                    ffn2(l * B + B - 1, 1, False)

            @block.scalar
            def _(act):
                def attn_weights_high(l):
                    act.wait_ge(w_attn, 16 * N_WA * l + 16 * N_WA)
                    nc.scalar.mul(w_qkv[:, 0], w_qkv_raw[:, 0], W_SCALE)
                    nc.scalar.mul(w_qkv[:, 2], w_qkv_raw[:, 1], W_SCALE)
                    nc.scalar.mul(w_qkv_high3[:], w_qkv_raw[:, 2], low_scale[:, 0:1]).then_inc(a_high, 1)

                def copy_xT(g, par, first):
                    act.wait_ge(s_hTp, g + 1)
                    if not first:
                        act.wait_ge(s_q, g - 1)
                        act.wait_ge(s_kv, g - 1)
                    nc.scalar.copy(xT16[:, par, 0:3, :].rearrange("p k s -> p (k s)"), bank[7][:, 0:3 * S])
                    nc.scalar.copy(xT16[0:D1, par, 3, :], bank[7][0:D1, 3 * S:4 * S]).then_inc(s_hT, 1)

                def copy_q(g, first):
                    act.wait_ge(s_q, g + 1)
                    if not first:
                        act.wait_ge(s_sc, 2 * g)
                    nc.scalar.mul(q_sb[:].rearrange("p t s -> p (t s)"), bank[4][:, 0:3 * S], DH ** -0.5 / W_SCALE).then_inc(s_qe, 1)

                def copy_oT(g, first, x_too):
                    act.wait_ge(s_pv, 2 * g + 2)
                    if x_too:
                        act.wait_ge(s_hTp, g + 4)
                    if not first:
                        act.wait_ge(s_wo, g)
                    nc.scalar.copy(oT0[:], bank[6][:, 3 * S:4 * S])
                    nc.scalar.copy(oT1[0:D1, :], bank[7][D1:P, 3 * S:4 * S]).then_inc(s_oTe, 1)

                def padding(g, r0, first):
                    act.wait_ge(s_max, 4 * g + r0 + 2)
                    if not first:
                        act.wait_ge(s_den, 4 * g - 3 + r0)
                    nc.scalar.activation(pad_exp[:, r0:r0 + 2], neg_max[:, r0:r0 + 2], ACT.Exp, bias=MASKED).then_inc(s_pad, 1)

                def probabilities(g, r, first):
                    if not first:
                        act.wait_ge(s_pTp, 4 * g - 3 + r)
                    for i in range(3):
                        last = nc.scalar.activation(probs[:, r, i, :], bank[r][:, i * S:(i + 1) * S], ACT.Exp,
                                                    bias=neg_max[:, r, i:i + 1], accum_out=sums[:, r, i:i + 1])
                    last.then_inc(s_exp, 1)

                def attention_unit(l, u, par, first, more):
                    g = l * B + u
                    if more >= 1:
                        for r in range(4):
                            if r % 2 == 0:
                                padding(g + 1, r, False)
                            if r == 3 and more >= 2:
                                copy_q(g + 2, False)
                            probabilities(g + 1, r, False)
                    copy_oT(g, first, more >= 3)
                    if more >= 3:
                        copy_xT(g + 3, 1 - par, False)

                def ffn_weights_high(l):
                    act.wait_ge(w_ffn, 16 * N_WF * l + 16 * N_WF)
                    nc.scalar.mul(w1[:, 0], w1_raw[:, 0], W_SCALE)
                    nc.scalar.mul(w1[:, 2], w1_raw[:, 1], W_SCALE)
                    nc.scalar.mul(w1_high3[:], w1_raw[:, 2], low_scale[:, 0:1]).then_inc(f_high, 1)
                    nc.scalar.mul(w2[:, 0], w2_raw[:], W_SCALE).then_inc(f_high, 1)

                def ffn_copy(w, par):
                    act.wait_ge(f_T, w + 1)
                    nc.scalar.copy(xT16[:, par, 0:3, :].rearrange("p k s -> p (k s)"), bank[0][:, 0:3 * S])
                    nc.scalar.copy(xT16[0:D1, par, 3, :], bank[0][0:D1, 3 * S:4 * S]).then_inc(f_hT, 1)

                def ffn_unit(l, u, par, first, last_unit, second=False):
                    w = l * B + u
                    if not last_unit:
                        if not first:
                            act.wait_ge(f_1, 2 * w)
                        ffn_copy(w + 1, 1 - par)
                    if not (first or second):
                        act.wait_ge(f_2, w - 1)
                    for k, (lo, hi) in enumerate(((0, 512), (512, NF * S))):
                        act.wait_ge(f_1, 2 * w + k + 1)
                        nc.scalar.activation(fT[:, par, lo:hi], bank[1 + k][:, 0:hi - lo], ACT.Gelu, scale=1.0 / W_SCALE).then_inc(f_g, 1)
                        act.wait_ge(f_g, 2 * w + k + 1)
                        nc.scalar.copy(fT16[:, par, 0, lo:hi], fT[:, par, lo:hi]).then_inc(f_fh, 1)

                with act.Fori(0, L) as l:
                    attn_weights_high(l)
                    copy_xT(l * B, 0, True)
                    copy_q(l * B, True)
                    copy_xT(l * B + 1, 1, True)
                    for r in range(4):
                        if r % 2 == 0:
                            padding(l * B, r, True)
                        probabilities(l * B, r, True)
                    copy_q(l * B + 1, False)
                    copy_xT(l * B + 2, 0, False)
                    attention_unit(l, 0, 0, True, 3)
                    with act.Fori(0, B // 2 - 2) as j:
                        attention_unit(l, 2 * j + 1, 1, False, 3)
                        attention_unit(l, 2 * j + 2, 0, False, 3)
                    for u in range(B - 3, B):
                        attention_unit(l, u, u % 2, False, B - 1 - u)
                    ffn_weights_high(l)
                    ffn_copy(l * B, 0)
                    ffn_unit(l, 0, 0, True, False)
                    ffn_unit(l, 1, 1, False, False, second=True)
                    with act.Fori(1, B // 2 - 1) as j:
                        ffn_unit(l, 2 * j, 0, False, False)
                        ffn_unit(l, 2 * j + 1, 1, False, False)
                    ffn_unit(l, B - 2, 0, False, False)
                    ffn_unit(l, B - 1, 1, False, True)

            @block.vector
            def _(dve):
                def attn_weights_low(l):
                    dve.wait_ge(a_high, l + 1)
                    nc.vector.scalar_tensor_tensor(w_qkv[:, 1], w_qkv_raw[:, 0], W_SCALE, w_qkv[:, 0], ALU.mult, ALU.subtract)
                    nc.vector.scalar_tensor_tensor(w_qkv[:, 3], w_qkv_raw[:, 2], W_SCALE, w_qkv_high3[:], ALU.mult, ALU.subtract).then_inc(a_low, 1)

                def x_halves(n, u, buffer, high, done):
                    nc.vector.tensor_copy(x16[:, buffer, 0, :], H[:, u, :]).then_inc(high, 1)
                    dve.wait_ge(s_const, 1)
                    dve.wait_ge(high, n + 1)
                    nc.vector.tensor_tensor(x16[:, buffer, 1, :], H[:, u, :], x16[:, buffer, 0, :], ALU.subtract).then_inc(done, 1)

                def copy_k(g):
                    dve.wait_ge(s_kv, g + 1)
                    nc.vector.tensor_scalar(k_sb[:].rearrange("p t s -> p (t s)"), bank[5][:, 0:2 * S], 1.0 / W_SCALE, None, ALU.mult).then_inc(s_ke, 1)

                def copy_v(g, par):
                    dve.wait_ge(s_kv, g + 1)
                    for odd in range(2):
                        last = nc.vector.tensor_scalar(v_sb[:, par, :, 2 * DH * odd:2 * DH * odd + DH],
                                                       bank[5][:, 256:256 + D].rearrange("p (n b e) -> p n b e", b=2, e=DH)[:, :, odd, :],
                                                       1.0 / W_SCALE, None, ALU.mult)
                    last.then_inc(s_ve, 1)

                def residual(g, u, first):
                    dve.wait_ge(s_wo, g + 1)
                    if not first:
                        dve.wait_ge(s_h, g)
                    nc.vector.tensor_tensor(xres[:, 0, :], bank[4][:, 0:D], H[:, u, :], ALU.add).then_inc(s_xadd, 1)

                def residual_stats(g):
                    dve.wait_ge(s_xadd, g + 1)
                    nc.vector.bn_stats(stats[:], xres[:, 0, :]).then_inc(s_st, 1)
                    dve.wait_ge(s_const, 1)
                    dve.wait_ge(s_st, g + 1)
                    nc.vector.bn_aggr(mv[:, 0, :], stats[:]).then_inc(s_ag, 1)
                    dve.wait_ge(s_ag, g + 1)
                    nc.vector.tensor_scalar(var_eps[:, 0:1], mv[:, 0, 1:2], EPS_TXT, None, ALU.add).then_inc(s_stat, 1)

                def negative_max(g, r, first):
                    dve.wait_ge(s_sc, 2 * g + r // 2 + 1)
                    if not first:
                        dve.wait_ge(s_exp, 4 * g - 3 + r)
                    nc.vector.tensor_reduce(neg_max[:, r, :], bank[r][:, 0:3 * S].rearrange("p (i s) -> p i s", i=3),
                                            AX.X, ALU.max, negate=True).then_inc(s_max, 1)

                def denominators(g, r0, first):
                    at = slice(r0, r0 + 2)
                    dve.wait_ge(s_exp, 4 * g + r0 + 2)
                    nc.vector.scalar_tensor_tensor(den[:, 0, at], pad_exp[:, at], float(N_PAD), sums[:, at], ALU.mult, ALU.add).then_inc(s_den, 1)
                    dve.wait_ge(s_den, 4 * g + r0 + 1)
                    if not first:
                        dve.wait_ge(s_norm, 4 * g - 2 + r0)
                    nc.vector.reciprocal(den[:, 1, at], den[:, 0, at]).then_inc(s_den, 1)

                def copy_pT(g, r, first):
                    dve.wait_ge(s_pTp, 4 * g + r + 1)
                    if not first or r >= 2:
                        dve.wait_ge(s_pv, 2 * g + r // 2)
                    nc.vector.tensor_copy(pT[:, r % 2, :], bank[6 + r % 2][:, 0:3 * S]).then_inc(s_pTe, 1)

                def attention_unit(l, u, par, first, more, second=False):
                    g = l * B + u
                    if more >= 3:
                        dve.wait_ge(s_hTp, g + 2)
                        x_halves(g + 3, u + 3, 1 - par, s_xh, s_xin)
                    if more >= 1:
                        for r in (0, 1, 2):
                            negative_max(g + 1, r, False)
                    for r in (0, 1):
                        copy_pT(g, r, first)
                    if more >= 1:
                        negative_max(g + 1, 3, False)
                    if not first:
                        residual(g - 1, u - 1, second)
                    for r in (2, 3):
                        copy_pT(g, r, first)
                    if more >= 1:
                        denominators(g + 1, 0, False)
                    if more >= 2:
                        copy_k(g + 2)
                    if not first:
                        residual_stats(g - 1)
                    if more >= 2:
                        dve.wait_ge(s_pv, 2 * g + 2)
                        copy_v(g + 2, par)
                    if more >= 1:
                        denominators(g + 1, 2, False)

                def ffn_weights_low(l):
                    dve.wait_ge(f_high, 2 * l + 1)
                    nc.vector.scalar_tensor_tensor(w1[:, 1], w1_raw[:, 0], W_SCALE, w1[:, 0], ALU.mult, ALU.subtract)
                    nc.vector.scalar_tensor_tensor(w1[:, 3], w1_raw[:, 2], W_SCALE, w1_high3[:], ALU.mult, ALU.subtract).then_inc(f_low, 1)
                    dve.wait_ge(f_high, 2 * l + 2)
                    nc.vector.scalar_tensor_tensor(w2[:, 1], w2_raw[:], W_SCALE, w2[:, 0], ALU.mult, ALU.subtract).then_inc(f_low, 1)

                def ffn_gelu_low(w, par):
                    for k, (lo, hi) in enumerate(((0, 512), (512, NF * S))):
                        dve.wait_ge(f_fh, 2 * w + k + 1)
                        nc.vector.tensor_tensor(fT16[:, par, 1, lo:hi], fT[:, par, lo:hi], fT16[:, par, 0, lo:hi], ALU.subtract).then_inc(f_fl, 1)

                def ffn_residual(w, u, par, few):
                    dve.wait_ge(f_2, w + 1)
                    if not few:
                        dve.wait_ge(f_h, B + w - 1)
                    nc.vector.scalar_tensor_tensor(xres[:, par, :], bank[3][:, 0:D], 1.0 / W_SCALE, H[:, u, :], ALU.mult, ALU.add).then_inc(f_c, 1)
                    dve.wait_ge(f_c, 2 * w + 1)
                    nc.vector.tensor_tensor(xres[:, par, :], xres[:, par, :], b2_rows[:], ALU.add).then_inc(f_c, 1)
                    dve.wait_ge(f_c, 2 * w + 2)
                    nc.vector.bn_stats(stats[:], xres[:, par, :]).then_inc(f_st, 1)
                    dve.wait_ge(s_const, 1)
                    dve.wait_ge(f_st, w + 1)
                    nc.vector.bn_aggr(mv[:, par, :], stats[:]).then_inc(f_ag, 1)
                    dve.wait_ge(f_ag, w + 1)
                    nc.vector.tensor_scalar(var_eps[:, par:par + 1], mv[:, par, 1:2], EPS_TXT, None, ALU.add).then_inc(f_stat, 1)

                with dve.Fori(0, L) as l:
                    attn_weights_low(l)
                    dve.wait_ge(f_h, B * l + B)
                    dve.wait_ge(w_attn, 16 * N_WA * l + 16 * N_WA)
                    x_halves(l * B, 0, 0, s_xh, s_xin)
                    x_halves(l * B + 1, 1, 1, s_xh, s_xin)
                    copy_k(l * B)
                    copy_v(l * B, 0)
                    dve.wait_ge(s_hTp, B * l + 1)
                    x_halves(l * B + 2, 2, 0, s_xh, s_xin)
                    for r in range(4):
                        negative_max(l * B, r, True)
                    for r0 in (0, 2):
                        denominators(l * B, r0, True)
                    copy_k(l * B + 1)
                    copy_v(l * B + 1, 1)
                    attention_unit(l, 0, 0, True, 3)
                    attention_unit(l, 1, 1, False, 3, second=True)
                    with dve.Fori(1, B // 2 - 2) as j:
                        attention_unit(l, 2 * j, 0, False, 3)
                        attention_unit(l, 2 * j + 1, 1, False, 3)
                    for u in range(B - 4, B):
                        attention_unit(l, u, u % 2, False, min(3, B - 1 - u))
                    residual(l * B + B - 1, B - 1, False)
                    residual_stats(l * B + B - 1)
                    ffn_weights_low(l)
                    for u in range(4):
                        if u == 0:
                            dve.wait_ge(s_h, B * l + B)
                        if u >= 2:
                            dve.wait_ge(f_T, B * l + u - 1)
                        x_halves(l * B + u, u, u % 2, f_xh, f_xin)
                        if u == 2:
                            ffn_gelu_low(l * B, 0)
                    ffn_gelu_low(l * B + 1, 1)
                    ffn_residual(l * B, 0, 0, True)
                    with dve.Fori(0, B // 2 - 2) as j:
                        for c in range(2):
                            u = 2 * j + c + 1
                            dve.wait_ge(f_T, l * B + 2 * j + c + 3)
                            x_halves(l * B + u + 3, u + 3, c, f_xh, f_xin)
                            ffn_gelu_low(l * B + u + 1, c)
                            ffn_residual(l * B + u, u, 1 - c, False)
                    for u in range(B - 3, B):
                        if u + 1 < B:
                            ffn_gelu_low(l * B + u + 1, (u + 1) % 2)
                        ffn_residual(l * B + u, u, u % 2, False)

            @block.gpsimd
            def _(pool):
                def attention_norm(g, u):
                    pool.wait_ge(s_stat, g + 1)
                    norm_rows(pool, s_pc, 4 * g, xres[:, 0, :], mv[:, 0, 0:1], var_eps[:, 0:1], ln1_s[:], ln1_b[:], H[:, u, :]).then_inc(s_h, 1)

                def ffn_norm(w, u, par):
                    pool.wait_ge(f_stat, w + 1)
                    norm_rows(pool, f_pc, 4 * w, xres[:, par, :], mv[:, par, 0:1], var_eps[:, par:par + 1], ln2_s[:], ln2_b[:], H[:, u, :]).then_inc(f_h, 1)

                def normalise(g):
                    for r in range(4):
                        pool.wait_ge(s_const, 1)
                        pool.wait_ge(s_den, 4 * g + 2 * (r // 2) + 2)
                        nc.gpsimd.tensor_tensor(probs[:, r], probs[:, r], den[:, 1, r].unsqueeze(2).to_broadcast([P, 3, S]),
                                                ALU.mult).then_inc(s_norm, 1)

                with pool.Fori(0, L) as l:
                    normalise(l * B)
                    normalise(l * B + 1)
                    with pool.Fori(2, B) as u:
                        normalise(l * B + u)
                        attention_norm(l * B + u - 2, u - 2)
                    for u in range(B - 2, B):
                        attention_norm(l * B + u, u)
                    with pool.Fori(0, B // 2) as j:
                        ffn_norm(l * B + 2 * j, 2 * j, 0)
                        ffn_norm(l * B + 2 * j + 1, 2 * j + 1, 1)


def text_layout(x):
    def with_bias(w, b):
        return np.concatenate([w, b[:, None, :]], axis=1)

    wq = with_bias(x["L0_txt_Wq"], x["L0_txt_bq"])
    wk = with_bias(x["L0_txt_Wk"], x["L0_txt_bk"])
    wv = with_bias(x["L0_txt_Wv"], x["L0_txt_bv"])
    wq_tiles = np.zeros((L, D + 1, 3 * P), np.float32)
    wk_tiles = np.zeros((L, D + 1, 2 * P), np.float32)
    for r in range(4):
        for i, (qt, kt) in enumerate(((0, 0), (1, 0), (2, 1))):
            h = HEADS_OF_GROUP[r][i]
            rows = 32 * ROW_GROUP[r]
            a = qt * P + rows + DH * (h % 2)
            wq_tiles[:, :, a:a + DH] = wq[:, :, DH * h:DH * h + DH]
            pair = h // 2
            wk_tiles[:, :, kt * P + rows:kt * P + rows + 2 * DH] = wk[:, :, 2 * DH * pair:2 * DH * pair + 2 * DH]
    wo = with_bias(x["L0_txt_Wo"], x["L0_txt_bo"])
    return dict(
        ids=np.ascontiguousarray(x["x_txt"].T), mask=x["mask_BS_i1_0"].reshape(-1),
        emb=x["L0_txt_emb_word"], pos=x["L0_txt_emb_pos"][:S],
        emb_ln_s=x["L0_txt_emb_ln_s"], emb_ln_b=x["L0_txt_emb_ln_b"],
        wqkv=np.concatenate([wq_tiles, wk_tiles, wv], axis=2), wo=wo,
        w1=with_bias(x["L0_txt_W1"], x["L0_txt_b1"]), w2=x["L0_txt_W2"], b2=x["L0_txt_b2"],
        ln1_s=x["L0_txt_ln1_s"], ln1_b=x["L0_txt_ln1_b"], ln2_s=x["L0_txt_ln2_s"], ln2_b=x["L0_txt_ln2_b"],
    )


def patch_embedding(nc, io, sem, H_img, consts):
    ident, half = consts["ident"], consts["half"]
    NP, WF, CH = 6, 3 * 18 * 18, 108
    NCH = WF // CH
    PD = 16 * 16 * 15
    with ExitStack() as ctx:
        def sb(name, shape, dt=F32):
            return ctx.enter_context(nc.sbuf_tensor(name, shape, dt))

        rows = [P, 6 * B - P]
        xw = [sb(f"tok_x{i}", [P, 3, 18, 98]) for i in range(2)]
        w5 = sb("tok_w5", [CH, 5, NCH, D])
        g5 = sb("tok_g5", [CH, 5, NCH])
        b5 = sb("tok_b5", [CH, 5, NCH])
        w_eff = sb("tok_w_eff", [CH, NCH, D])
        mult = sb("tok_mult", [P, WF])
        ones = sb("tok_ones", [CH, P])
        b_row = sb("tok_b", [1, D])
        beta_cols = sb("tok_beta_cols", [CH, 5 * NCH, P])
        const_rows = sb("tok_const", [P, D])
        xc = sb("tok_xc", [P, 2, WF])
        xm = sb("tok_xm", [P, 2, WF])
        junk = sb("tok_junk", [P, WF])
        xT = sb("tok_xT", [CH, NCH, P])
        neg_mean = sb("tok_neg_mean", [P, 12])
        var = sb("tok_var", [P, 12])
        var_eps = sb("tok_var_eps", [P, 12])
        rstd = sb("tok_rstd", [P, 12])
        tok_out = sb("tok_out", [P, 2, NP, D])
        tb = [ctx.enter_context(nc.psum_tensor(f"tok_bank{i}", [P, 512], F32)) for i in range(5)]

        s_x, s_w, s_one = sem("tok_x_loaded"), sem("tok_w_loaded"), sem("tok_ones_set")
        s_bcol, s_gw, s_const = sem("tok_beta_cols"), sem("tok_w_steps"), sem("tok_const_ready")
        s_cp = sem("tok_const_product")
        s_mean, s_xc, s_xm, s_var, s_rs = sem("tok_mean"), sem("tok_centred"), sem("tok_weighted"), sem("tok_var"), sem("tok_rstd")
        s_vp = sem("tok_var_sum")
        s_T, s_xT, s_mm, s_out = sem("tok_T"), sem("tok_xT"), sem("tok_mm"), sem("tok_out")
        s_junk = sem("tok_junk")
        s_scr, s_back = sem("tok_scratch_written"), sem("tok_scratch_read")
        steps = [(t, w) for t in range(2) for w in range(NP)]

        def window(t, w):
            return xw[t][0:rows[t], :, :, 16 * w:16 * w + 18]

        def v3(ap):
            return ap.rearrange("p (c y x) -> p c y x", c=3, y=18)

        with nc.Block() as block:
            @block.sync
            def _(sp):
                sp.dma_start(xw[0][:], io["tok_x"][0:P]).then_inc(s_x, 16)
                sp.dma_start(mult[:], io["tok_mult"].partition_broadcast(P)).then_inc(s_x, 16)
                sp.dma_start(g5[:], io["tok_g5"]).then_inc(s_w, 16)
                sp.dma_start(b5[:], io["tok_b5"]).then_inc(s_w, 16)
                sp.dma_start(b_row[:], io["tok_b"]).then_inc(s_w, 16)
                sp.dma_start(w5[:], io["tok_w5"]).then_inc(s_w, 16)
                sp.dma_start(xw[1][0:rows[1]], io["tok_x"][P:6 * B]).then_inc(s_x, 16)
                for t in range(2):
                    sp.wait_ge(s_out, NP * (t + 1))
                    sp.dma_start(io["scratch_tok"][t * P:t * P + rows[t]],
                                 tok_out[0:rows[t], t].rearrange("p w e -> p (w e)")).then_inc(s_scr, 16)
                sp.wait_ge(s_scr, 32)
                sp.dma_start(H_img[:], io["scratch_tok"].rearrange("(b h) n -> b (h n)", h=NP).rearrange(
                    "b (t e) -> t b e", e=D)).then_inc(s_back, 16)
                sp.wait_ge(s_back, 16)

            @block.vector
            def _(dve):
                nc.vector.memset(ones[:], 1.0).then_inc(s_one, 1)
                dve.wait_ge(s_w, 64)
                dve.wait_ge(s_one, 1)
                nc.vector.tensor_tensor(beta_cols[:], b5[:].rearrange("p s c -> p (s c)").unsqueeze(2).to_broadcast([CH, 5 * NCH, P]),
                                        ones[:].unsqueeze(1).to_broadcast([CH, 5 * NCH, P]), ALU.mult).then_inc(s_bcol, 1)
                dve.wait_ge(s_x, 48)
                for k, (t, w) in enumerate(steps):
                    if k:
                        dve.wait_ge(s_junk, k)
                    nc.vector.tensor_tensor_reduce(v3(junk[0:rows[t]]), window(t, w), v3(mult[0:rows[t]]), -1.0 / PD, 0.0,
                                                   ALU.mult, ALU.add, neg_mean[0:rows[t], k:k + 1]).then_inc(s_junk, 1)
                dve.wait_ge(s_junk, 12)
                for s in range(5):
                    if s:
                        dve.wait_ge(s_gw, s)
                    for c in range(NCH):
                        if s == 0:
                            last = nc.vector.tensor_scalar(w_eff[:, c, :], w5[:, 0, c, :], g5[:, 0, c:c + 1], None, ALU.mult)
                        else:
                            last = nc.vector.scalar_tensor_tensor(w_eff[:, c, :], w5[:, s, c, :], g5[:, s, c:c + 1], w_eff[:, c, :], ALU.mult, ALU.add)
                    last.then_inc(s_gw, 1)
                dve.wait_ge(s_cp, 1)
                nc.vector.tensor_copy(const_rows[:], tb[4][:, 0:D]).then_inc(s_const, 1)
                for k, (t, w) in enumerate(steps):
                    r = rows[t]
                    dve.wait_ge(s_xm, k + 1)
                    if k:
                        dve.wait_ge(s_vp, k)
                    nc.vector.tensor_tensor_reduce(junk[0:r], xc[0:r, k % 2], xm[0:r, k % 2], 1.0 / PD, 0.0,
                                                   ALU.mult, ALU.add, var[0:r, k:k + 1]).then_inc(s_vp, 1)
                    dve.wait_ge(s_vp, k + 1)
                    nc.vector.tensor_scalar(var_eps[0:r, k:k + 1], var[0:r, k:k + 1], EPS, None, ALU.add).then_inc(s_var, 1)
                    for q in range(2):
                        dve.wait_ge(s_T, 3 * k + q + 1)
                        if q == 0 and k:
                            dve.wait_ge(s_mm, k)
                        nc.vector.tensor_copy(xT[:, 4 * q:4 * q + 4, 0:r], tb[q][0:CH, :].rearrange("p (c n) -> p c n", c=4)[:, :, 0:r]).then_inc(s_xT, 1)
                    dve.wait_ge(s_T, 3 * k + 3)
                    nc.vector.tensor_copy(xT[:, 8, 0:r], tb[2][0:CH, 0:r]).then_inc(s_xT, 1)
                    dve.wait_ge(s_mm, k + 1)
                    dve.wait_ge(s_rs, k + 1)
                    dve.wait_ge(s_const, 1)
                    nc.vector.scalar_tensor_tensor(tok_out[0:r, t, w, :], tb[3][0:r, 0:D], rstd[0:r, k:k + 1], const_rows[0:r],
                                                   ALU.mult, ALU.add).then_inc(s_out, 1)

            @block.scalar
            def _(act):
                for k, (t, w) in enumerate(steps):
                    act.wait_ge(s_junk, k + 1)
                    if k >= 2:
                        act.wait_ge(s_vp, k - 1)
                        act.wait_ge(s_T, 3 * k - 3)
                    nc.scalar.activation(v3(xc[0:rows[t], k % 2]), window(t, w), ACT.Identity,
                                         bias=neg_mean[0:rows[t], k:k + 1]).then_inc(s_xc, 1)

            def rstd_of(pool, k):
                r = rows[steps[k][0]]
                pool.wait_ge(s_var, k + 1)
                nc.gpsimd.tensor_tensor(rstd[0:r, k:k + 1], var_eps[0:r, k:k + 1], half[0:r], ALU.pow).then_inc(s_rs, 1)

            @block.gpsimd
            def _(pool):
                for k, (t, w) in enumerate(steps):
                    r = rows[t]
                    pool.wait_ge(s_xc, k + 1)
                    if k >= 2:
                        pool.wait_ge(s_vp, k - 1)
                    nc.gpsimd.tensor_tensor(xm[0:r, k % 2], xc[0:r, k % 2], mult[0:r], ALU.mult).then_inc(s_xm, 1)
                    if k >= 1:
                        rstd_of(pool, k - 1)
                rstd_of(pool, 11)

            @block.tensor
            def _(pe):
                pe.wait_ge(s_bcol, 1)
                for i in range(5 * NCH):
                    nc.tensor.matmul(tb[4][:, 0:D], beta_cols[:, i, :], w5[:, i // NCH, i % NCH, :], start=(i == 0), stop=False)
                nc.tensor.matmul(tb[4][:, 0:D], ones[0:1, :], b_row[:], start=False, stop=True).then_inc(s_cp, 1)
                for k, (t, w) in enumerate(steps):
                    r = rows[t]
                    pe.wait_ge(s_xc, k + 1)
                    for c in range(NCH):
                        if c % 4 == 0 and k:
                            pe.wait_ge(s_xT, 3 * (k - 1) + c // 4 + 1)
                        last = nc.tensor.transpose(tb[c // 4][0:CH, (c % 4) * P:(c % 4) * P + r], xc[0:r, k % 2, c * CH:(c + 1) * CH], ident[0:r, 0:r])
                        if c in (3, 7, 8):
                            last.then_inc(s_T, 1)
                    pe.wait_ge(s_gw, 5)
                    if k:
                        pe.wait_ge(s_out, k)
                    for c in range(NCH):
                        if c % 4 == 0:
                            pe.wait_ge(s_xT, 3 * k + c // 4 + 1)
                        last = nc.tensor.matmul(tb[3][0:r, 0:D], xT[:, c, 0:r], w_eff[:, c, :], start=(c == 0), stop=(c == NCH - 1))
                    last.then_inc(s_mm, 1)


def tok_layout(x):
    xp = np.zeros((B, 3, 98, 98), np.float32)
    xp[:, :, 1:97, 1:97] = x["x"]
    tok_x = np.stack([xp[:, :, 16 * h:16 * h + 18, :] for h in range(6)], axis=1).reshape(6 * B, 3, 18, 98)
    shifts = [(1, 1), (1, 0), (1, 2), (0, 1), (2, 1)]

    def spread(a):
        n = a.shape[1]
        a = a.reshape(16, 16, 5, 3, n)
        out = np.zeros((5, 3, 18, 18, n), np.float32)
        for s, (dy, dx) in enumerate(shifts):
            out[s, :, dy:dy + 16, dx:dx + 16] = a[:, :, s].transpose(2, 0, 1, 3)
        return np.ascontiguousarray(out.reshape(5, 9, 108, n).transpose(2, 0, 1, 3))

    mult = np.zeros((3, 18, 18), np.float32)
    for dy, dx in shifts:
        mult[:, dy:dy + 16, dx:dx + 16] += 1
    return dict(tok_x=tok_x, tok_w5=spread(x["L0_tok_W"]), tok_g5=spread(x["L0_tok_gamma"][:, None])[..., 0],
                tok_b5=spread(x["L0_tok_beta"][:, None])[..., 0], tok_b=x["L0_tok_b"][None], tok_mult=mult.reshape(-1))


class Steps:

    def __init__(self, engine, semaphore, per, j):
        self.engine, self.semaphore, self.per, self.j, self.n = engine, semaphore, per, j, 0

    def done(self, instruction):
        self.n += 1
        instruction.then_inc(self.semaphore, 1)
        return self.n

    def wait(self, n=None):
        self.engine.wait_ge(self.semaphore, self.per * self.j + (self.n if n is None else n))


NPAIR = B // 2
W2T = 2 * T
W3T = 3 * T


def ssm_and_slots(nc, io, sem, H, H_img, consts):
    ident, half = consts["ident"], consts["half"]
    with ExitStack() as ctx:
        def sb(name, shape, dt=F32):
            return ctx.enter_context(nc.sbuf_tensor(name, shape, dt))

        wB, wC = (sb(n, [P, 4, NS * D], F16) for n in ("wB", "wC"))
        wi0, wi1 = sb("wi0", [P, 2 * D]), sb("wi1", [D1 + 1, 2 * D])
        wdt0, wdt1 = sb("wdt0", [P, D]), sb("wdt1", [D1 + 1, D])
        wso0, wso1 = sb("wso0", [P, D]), sb("wso1", [D1 + 1, D])
        a_neg = sb("a_neg", [P, 2, NS])
        wconv = sb("wconv", [P, 2, KC + 2])
        slots0, slots1 = sb("slots0", [P, SLOTS]), sb("slots1", [D1, SLOTS])
        xt0, xt1 = sb("xt0", [P, B, SLOTS]), sb("xt1", [D1 + 1, B, SLOTS])
        c_all = sb("c_all", [SLOTS, NPAIR, W2T])
        half4 = sb("half4", [P, 2, 4])
        pb = [ctx.enter_context(nc.psum_tensor(f"bank{i}", [P, 512], F32)) for i in range(8)]

        with ExitStack() as tmp:
            def t(name, shape):
                return tmp.enter_context(nc.sbuf_tensor(name, shape, F32))
            a_log = t("a_log", [P, 2, NS])
            raw0, raw1 = t("raw0", [P, SLOTS]), t("raw1", [D1, SLOTS])
            sq = t("sq", [P, 2, SLOTS])
            nrm = t("nrm", [P, 4, 2, NP_])
            scale = t("scale", [P, 1])
            stage = t("stage", [P, 3, NS * D])
            high = tmp.enter_context(nc.sbuf_tensor("high", [P, NS * D], F16))
            low_rows = t("low_rows", [P, 1])
            l_st, z_st, z_h, z_l, z_sc = sem("stage_loaded"), sem("stage_zeroed"), sem("high_ready"), sem("low_ready"), sem("stage_scaled")
            l_w, l_s = sem("ssm_weights_loaded"), sem("slots_loaded")
            z_v, z_p, z_a, z_set = sem("setup_dve"), sem("setup_pool"), sem("setup_act"), sem("setup_zeroed")
            with nc.Block() as block:
                @block.sync
                def _(sp):
                    for dst, src in ((raw0[:], io["slot_params"][0:P]), (raw1[:], io["slot_params"][P:D]),
                                     (scale[:], io["slot_scale"].partition_broadcast(P)), (a_log[:], io["a_log"])):
                        sp.dma_start(dst, src).then_inc(l_s, 16)
                    for dst, src in ((wconv[:], io["wconv"]), (wi0[:], io["wi"][0:P]), (wi1[:], io["wi"][P:D + 1]),
                                     (wdt0[:], io["wdt"][0:P]), (wdt1[:], io["wdt"][P:D + 1]),
                                     (wso0[:], io["wso"][0:P]), (wso1[:], io["wso"][P:D + 1])):
                        sp.dma_start(dst, src).then_inc(l_w, 16)
                    sp.wait_ge(z_st, 1)
                    for i, name in enumerate(("wB", "wC")):
                        sp.wait_ge(z_l, 2 * i)
                        sp.wait_ge(z_h, 3 * i)
                        w = io[name]
                        for dst, src in ((stage[:, 0], w[0:P]), (stage[0:D1, 1], w[P:D]), (stage[D1:P, 1], w[P:D]),
                                         (stage[0:D1, 2], w[P:D]), (stage[D1:D1 + 1, 2], w[D:D + 1]), (stage[96:97, 2], w[D:D + 1])):
                            sp.dma_start(dst, src).then_inc(l_st, 16)
                    sp.wait_ge(l_w, 16 * 7)

                @block.scalar
                def _(act):
                    act.wait_ge(l_s, 64)
                    nc.scalar.activation(a_neg[:], a_log[:], ACT.Exp).then_inc(z_a, 1)
                    for i, w in enumerate((wB, wC)):
                        act.wait_ge(z_sc, i + 1)
                        nc.scalar.copy(w[:, 0], stage[:, 0]).then_inc(z_h, 1)
                        nc.scalar.copy(w[:, 2], stage[:, 1]).then_inc(z_h, 1)
                        act.wait_ge(z_l, 2 * i)
                        nc.scalar.copy(high[:], stage[:, 2]).then_inc(z_h, 1)

                @block.vector
                def _(dve):
                    nc.vector.memset(half4[:, 0, :], -0.5)
                    nc.vector.memset(half4[:, 1, :], 0.5)
                    nc.vector.memset(xt1[:], 1.0)
                    nc.vector.memset(stage[:, 2], 0.0).then_inc(z_st, 1)
                    nc.vector.memset(low_rows[:D1], -1.0)
                    nc.vector.memset(low_rows[D1:96], 0.0)
                    nc.vector.memset(low_rows[96:], -1.0)
                    nc.vector.memset(sq[:], 0.0).then_inc(z_set, 1)
                    dve.wait_ge(z_set, 1)
                    dve.wait_ge(l_s, 64)
                    for c, (raw, r) in enumerate(((raw0, P), (raw1, D1))):
                        nc.vector.tensor_tensor(sq[0:r, c], raw[:], raw[:], ALU.mult).then_inc(z_v, 1)
                    dve.wait_ge(z_v, 2)
                    nc.vector.tensor_reduce(nrm[:, 0], sq[:].rearrange("p c (n q) -> p c q n", n=NE), AX.X, ALU.add).then_inc(z_v, 1)
                    dve.wait_ge(z_a, 1)
                    nc.vector.tensor_scalar(a_neg[:], a_neg[:], -1.0, None, ALU.mult)
                    dve.wait_ge(z_p, 1)
                    nc.vector.tensor_scalar(nrm[:, 2], nrm[:, 1], 1e-6, None, ALU.add).then_inc(z_v, 1)
                    dve.wait_ge(z_v, 4)
                    nc.vector.reciprocal(nrm[:, 3], nrm[:, 2]).then_inc(z_v, 1)
                    dve.wait_ge(z_v, 5)
                    for c, (raw, slots, r) in enumerate(((raw0, slots0, P), (raw1, slots1, D1))):
                        nc.vector.scalar_tensor_tensor(slots[:].rearrange("p (n q) -> p n q", n=NE), raw[:].rearrange("p (n q) -> p n q", n=NE),
                                                       scale[0:r, 0:1], nrm[0:r, 3, c].unsqueeze(1).to_broadcast([r, NE, NP_]), ALU.mult, ALU.mult)
                    for i, w in enumerate((wB, wC)):
                        dve.wait_ge(l_st, 96 * (i + 1))
                        nc.vector.tensor_scalar(stage[:], stage[:], W_SCALE, None, ALU.mult).then_inc(z_sc, 1)
                        dve.wait_ge(z_sc, i + 1)
                        dve.wait_ge(z_h, 3 * i + 3)
                        nc.vector.tensor_tensor(w[:, 1], stage[:, 0], w[:, 0], ALU.subtract).then_inc(z_l, 1)
                        nc.vector.scalar_tensor_tensor(w[:, 3], high[:], low_rows[:, 0:1], stage[:, 2], ALU.mult, ALU.add).then_inc(z_l, 1)

                @block.gpsimd
                def _(pool):
                    pool.wait_ge(z_v, 3)
                    nc.gpsimd.tensor_tensor(nrm[:, 1], nrm[:, 0], half4[:, 1, 0:1].unsqueeze(2).to_broadcast([P, 2, NP_]), ALU.pow).then_inc(z_p, 1)

        with ExitStack() as tmp:
            def t(name, shape):
                return tmp.enter_context(nc.sbuf_tensor(name, shape, F32))
            st4 = t("st4", [P, 4, 6])
            mv_f, ve_f, rs_f = t("mv_f", [P, 4, 2]), t("ve_f", [P, 4]), t("rs_f", [P, 4])
            xn_t, xn_i = t("xn_t", [P, 2, D]), t("xn_i", [N_IMG, 2, D])
            xT0, xT1 = t("xT0", [P, W2T]), t("xT1", [D1 + 1, W2T])
            u_pad = t("u_pad", [P, 3, KC - 1 + T])
            conv = t("conv", [P, 2, 3, T])
            uc_n, uc1_n = t("uc_n", [P, 3, T]), t("uc1_n", [D1 + 1, W2T])
            ev_n = t("ev_n", [P, W3T])
            sp_a, sp_e, sp_l = t("sp_a", [P, W3T]), t("sp_e", [P, W3T]), t("sp_l", [P, W3T])
            dt_n = t("dt_n", [P, W3T])
            y0 = t("y0", [P, 3, T])
            u16, u16_n = (tmp.enter_context(nc.sbuf_tensor(n, [P, 4, W2T], F16)) for n in ("u16", "u16_n"))
            dt, dtu = t("dt", [P, 3, T]), t("dtu", [P, W3T])
            sg = t("sg", [P, 2, W3T])
            decay = t("decay", [P, 2, 3, T])
            inp = t("inp", [P, 2, W3T])
            state = t("state", [P, 2, W3T])
            cstate = t("cstate", [P, 2, W3T])
            y = t("y", [P, 2, W3T])
            yg, yg1 = t("yg", [P, W3T]), t("yg1", [D1 + 1, W2T])
            mv_b, sm = t("mv_b", [P, 4, 2]), t("sm", [P, 8, 4])
            zn_t, zn_i = t("zn_t", [P, 2, D]), t("zn_i", [N_IMG, 2, D])
            zT0, zT1 = t("zT0", [P, W2T]), t("zT1", [D1, W2T])
            cmax, cexp = t("cmax", [P, 3, 4]), t("cexp", [P, 3, 4, SLOTS])
            dmax, dexp = t("dmax", [SLOTS, 3, 2]), t("dexp", [SLOTS, 2, W2T])
            d_tok = t("d_tok", [P, 4, SLOTS])

            names = ("bn bn0 var rs xn T xT U V up v conv uc1 hi lo D l dt y0").split()
            F = {n: sem("front_" + n) for n in names}
            fd, fa = sem("front_dve_steps"), sem("front_act_steps")
            s_uc, s_dt, s_dtu, s_sg = sem("uc_ready"), sem("dt_ready"), sem("dtu_ready"), sem("sigmoid_ready")
            s_B, s_C, s_a, s_in, s_scan, s_cs, s_acc = (sem(n) for n in ("B_done", "C_done", "decay_ready", "input_ready", "scan_done", "cstate_ready", "y_added"))
            names = ("yg yg1 op h2 bn var pw zn T zT L mx e cd T3 ct dT x xt").split()
            K = {n: sem("back_" + n) for n in names}
            bd = sem("back_dve_steps")
            s_set = sem("scan_constants")
            FD, BD = 8, 10

            def v3(ap):
                return ap.rearrange("p (a t) -> p a t", a=3)

            with nc.Block() as block:
                @block.tensor
                def _(pe):
                    def mixed(bank, w0, w1, c0, x0, x1, done):
                        nc.tensor.matmul(bank[:, 0:W2T], w0[:, c0:c0 + P], x0, start=True, stop=False)
                        nc.tensor.matmul(bank[:, 0:W2T], w1[:, c0:c0 + P], x1, start=False, stop=True)
                        for k, (w, x) in enumerate(((w0, x0), (w1, x1))):
                            for s in range(2):
                                last = nc.tensor.matmul(bank[D1 * s:D1 * s + D1, W2T:W3T], w[:, c0 + P:c0 + D], x[:, s * T:(s + 1) * T],
                                                        start=(k == 0), stop=(k == 1))
                        last.then_inc(done, 1)

                    def mixed_halves(bank, w, n, done):
                        passes = ((0, 0, P), (1, 0, P), (0, 1, P), (2, 2, P), (3, 3, 97))
                        for k, (a, b, r) in enumerate(passes):
                            nc.tensor.matmul(bank[:, 0:W2T], w[0:r, a, n * D:n * D + P], u16[0:r, b, :], start=(k == 0), stop=(k == 4))
                        for k, (a, b, r) in enumerate(passes):
                            for s in range(2):
                                last = nc.tensor.matmul(bank[D1 * s:D1 * s + D1, W2T:W3T], w[0:r, a, n * D + P:(n + 1) * D],
                                                        u16[0:r, b, s * T:(s + 1) * T], start=(k == 0), stop=(k == 4))
                        last.then_inc(done, 1)

                    def to_channels(b0, b1, z_t, z_i, done):
                        for s in range(2):
                            c = s * T
                            nc.tensor.transpose(b0[:, c + N_IMG:c + T], z_t[:, s, 0:P], ident[:])
                            nc.tensor.transpose(b0[:, c:c + N_IMG], z_i[:, s, 0:P], ident[0:N_IMG, 0:N_IMG])
                            nc.tensor.transpose(b1[0:D1, c:c + N_IMG], z_i[:, s, P:D], ident[0:N_IMG, 0:N_IMG])
                            last = nc.tensor.transpose(b1[0:D1, c + N_IMG:c + T], z_t[:, s, P:D], ident[:])
                        last.then_inc(done, 1)

                    def front_T(j):
                        pe.wait_ge(F["xn"], j + 1)
                        pe.wait_ge(F["dt"], j)
                        pe.wait_ge(F["v"], j)
                        to_channels(pb[6], pb[7], xn_t, xn_i, F["T"])

                    def front_uv(j):
                        pe.wait_ge(F["xT"], j + 1)
                        mixed(pb[6], wi0, wi1, 0, xT0[:], xT1[:], F["U"])
                        mixed(pb[7], wi0, wi1, D, xT0[:], xT1[:], F["V"])

                    def front_dt(j):
                        pe.wait_ge(F["uc1"], j + 1)
                        pe.wait_ge(F["up"], j + 1)
                        mixed(pb[6], wdt0, wdt1, 0, uc_n[:].rearrange("p a t -> p (a t)")[:, 0:W2T], uc1_n[:], F["D"])

                    def back_op(j):
                        pe.wait_ge(K["yg1"], j + 1)
                        pe.wait_ge(K["xt"], j)
                        pe.wait_ge(K["dT"], j)
                        for s in range(2):
                            c = s * T
                            nc.tensor.matmul(pb[4][:, s * D:(s + 1) * D], yg[:, c + N_IMG:c + T], wso0[:], start=True, stop=False)
                            nc.tensor.matmul(pb[4][:, s * D:(s + 1) * D], yg1[:, c + N_IMG:c + T], wso1[:], start=False, stop=True)
                            nc.tensor.matmul(pb[5][0:N_IMG, s * D:(s + 1) * D], yg[:, c:c + N_IMG], wso0[:], start=True, stop=False)
                            last = nc.tensor.matmul(pb[5][0:N_IMG, s * D:(s + 1) * D], yg1[:, c:c + N_IMG], wso1[:], start=False, stop=True)
                        last.then_inc(K["op"], 1)

                    def back_T(j):
                        pe.wait_ge(K["zn"], j + 1)
                        to_channels(pb[4], pb[5], zn_t, zn_i, K["T"])

                    def back_logits(j):
                        pe.wait_ge(K["zT"], j + 1)
                        for i in range(4):
                            s, c = i % 2, (i % 2) * T + (N_IMG if i < 2 else 0)
                            out = pb[4][:, i * SLOTS:(i + 1) * SLOTS]
                            nc.tensor.matmul(out, zT0[:, c:c + P], slots0[:], start=True, stop=False)
                            nc.tensor.matmul(out, zT1[:, c:c + P], slots1[:], start=False, stop=True)
                        nc.tensor.matmul(pb[5][0:SLOTS, 0:W2T], slots0[:], zT0[:], start=True, stop=False)
                        nc.tensor.matmul(pb[5][0:SLOTS, 0:W2T], slots1[:], zT1[:], start=False, stop=True).then_inc(K["L"], 1)

                    def back_T3(j):
                        pe.wait_ge(K["cd"], j + 1)
                        for i in range(4):
                            s, c = i % 2, (i % 2) * T + (N_IMG if i < 2 else 0)
                            r = P if i < 2 else N_IMG
                            nc.tensor.transpose(pb[4][0:SLOTS, c:c + r], cexp[0:r, 2, i, :], ident[0:r, 0:r])
                            last = nc.tensor.transpose(pb[5][:, i * SLOTS:(i + 1) * SLOTS], dexp[:, 1, c:c + P], ident[0:SLOTS, 0:SLOTS])
                        last.then_inc(K["T3"], 1)

                    def back_x(j):
                        pe.wait_ge(K["ct"], j + 1)
                        pe.wait_ge(K["dT"], j + 1)
                        for s in range(2):
                            for m, (lo, hi) in enumerate(((0, P), (P, D))):
                                out = pb[4][0:hi - lo, m * 2 * SLOTS + s * SLOTS:m * 2 * SLOTS + (s + 1) * SLOTS]
                                nc.tensor.matmul(out, zn_t[:, s, lo:hi], d_tok[:, s, :], start=True, stop=False)
                                last = nc.tensor.matmul(out, zn_i[:, s, lo:hi], d_tok[0:N_IMG, 2 + s, :], start=False, stop=True)
                        last.then_inc(K["x"], 1)

                    def scan_steps(j, first, last_pair):
                        pe.wait_ge(s_uc, j + 1)
                        back = {3: back_op, 7: back_T, 9: back_logits, 13: back_T3, 15: back_x}
                        front = {4: front_T, 6: front_uv, 10: front_dt}
                        for n in range(NS):
                            m = NS * j + n
                            if n in back and not first:
                                back[n](j - 1)
                            if n in front and not last_pair:
                                front[n](j + 1)
                            if n >= 2 or not first:
                                pe.wait_ge(s_in, m - 1)
                            mixed_halves(pb[n % 2], wB, n, s_B)
                            if n >= 2 or not first:
                                pe.wait_ge(s_cs, m - 1)
                            mixed_halves(pb[2 + n % 2], wC, n, s_C)

                    front_T(0)
                    front_uv(0)
                    front_dt(0)
                    scan_steps(0, True, False)
                    scan_steps(1, False, False)
                    with pe.Fori(2, NPAIR - 1) as j:
                        scan_steps(j, False, False)
                    scan_steps(NPAIR - 1, False, True)
                    for piece in (back_op, back_T, back_logits, back_T3, back_x):
                        piece(NPAIR - 1)

                @block.scalar
                def _(act):
                    def front_xT(j):
                        act.wait_ge(F["T"], j + 1)
                        act.wait_ge(F["V"], j)
                        nc.scalar.copy(xT0[:], pb[6][:, 0:W2T])
                        nc.scalar.copy(xT1[0:D1, :], pb[7][0:D1, 0:W2T]).then_inc(F["xT"], 1)

                    def front_up(j):
                        act.wait_ge(F["U"], j + 1)
                        act.wait_ge(F["conv"], j)
                        nc.scalar.copy(u_pad[:, :, KC - 1:], v3(pb[6][:, 0:W3T])).then_inc(F["up"], 1)
                        act.wait_ge(F["V"], j + 1)
                        act.wait_ge(s_sg, 2 * j)
                        nc.scalar.activation(ev_n[:], pb[7][:, 0:W3T], ACT.Exp, scale=-1.0).then_inc(F["v"], 1)

                    def front_uc1(j):
                        act.wait_ge(F["conv"], j + 1)
                        act.wait_ge(F["D"], j)
                        nc.scalar.copy(uc1_n[0:D1, 0:T], uc_n[0:D1, 2, :])
                        nc.scalar.copy(uc1_n[0:D1, T:W2T], uc_n[D1:P, 2, :]).then_inc(F["uc1"], 1)
                        act.wait_ge(F["uc1"], j + 1)
                        act.wait_ge(s_uc, j)
                        nc.scalar.copy(u16_n[:, 0, :], uc_n[:, 0:2, :].rearrange("p a t -> p (a t)"))
                        nc.scalar.copy(u16_n[0:D1, 2, :], uc1_n[0:D1, :])
                        nc.scalar.copy(u16_n[0:D1, 3, :], uc1_n[0:D1, :]).then_inc(F["hi"], 1)

                    def front_softplus(j):
                        act.wait_ge(F["D"], j + 1)
                        act.wait_ge(F["dt"], j)
                        nc.scalar.activation(sp_a[:], pb[6][:, 0:W3T], ACT.Abs).then_inc(fa, 1)
                        act.wait_ge(fa, 2 * j + 1)
                        nc.scalar.activation(sp_e[:], sp_a[:], ACT.Exp, scale=-1.0).then_inc(fa, 1)
                        act.wait_ge(fa, 2 * j + 2)
                        nc.scalar.activation(sp_l[:], sp_e[:], ACT.Ln, bias=1.0).then_inc(F["l"], 1)

                    def back_yg1(j):
                        act.wait_ge(K["yg"], j + 1)
                        act.wait_ge(K["op"], j)
                        nc.scalar.copy(yg1[0:D1, 0:T], yg[0:D1, W2T:W3T])
                        nc.scalar.copy(yg1[0:D1, T:W2T], yg[D1:P, W2T:W3T]).then_inc(K["yg1"], 1)

                    def back_zT(j):
                        act.wait_ge(K["T"], j + 1)
                        nc.scalar.copy(zT0[:], pb[4][:, 0:W2T])
                        nc.scalar.copy(zT1[:], pb[5][0:D1, 0:W2T]).then_inc(K["zT"], 1)

                    def back_exp(j):
                        act.wait_ge(K["mx"], j + 1)
                        nc.scalar.activation(cexp[:, 1], cexp[:, 0], ACT.Exp)
                        for s in range(2):
                            last = nc.scalar.activation(dexp[:, 0, s * T:(s + 1) * T], pb[5][0:SLOTS, s * T:(s + 1) * T], ACT.Exp,
                                                        bias=dmax[:, 0, s:s + 1])
                        last.then_inc(K["e"], 1)

                    def back_ct(j):
                        act.wait_ge(K["T3"], j + 1)
                        nc.scalar.copy(c_all[:, bass.ds(j, 1), :], pb[4][0:SLOTS, 0:W2T].unsqueeze(1)).then_inc(K["ct"], 1)

                    def back_xt(j):
                        act.wait_ge(K["x"], j + 1)
                        nc.scalar.copy(xt0[:, bass.ds(2 * j, 2), :], pb[4][:, 0:2 * SLOTS].rearrange("p (s k) -> p s k", s=2))
                        nc.scalar.copy(xt1[0:D1, bass.ds(2 * j, 2), :],
                                       pb[4][0:D1, 2 * SLOTS:4 * SLOTS].rearrange("p (s k) -> p s k", s=2)).then_inc(K["xt"], 1)

                    def scan_steps(j, first, last_pair):
                        act.wait_ge(s_dt, j + 1)
                        back = {2: back_yg1, 8: back_zT, 10: back_exp, 14: back_ct}
                        front = {5: front_xT, 7: front_up, 9: front_uc1, 11: front_softplus}
                        for n in range(NS):
                            m = NS * j + n
                            if n in back and not first:
                                back[n](j - 1)
                            if n in front and not last_pair:
                                front[n](j + 1)
                            if n >= 2 or not first:
                                act.wait_ge(s_scan, m - 1)
                            nc.scalar.activation(decay[:, n % 2, 0:2, 1:], dt[:, 0:2, 1:], ACT.Exp, scale=a_neg[:, 0, n:n + 1])
                            nc.scalar.activation(decay[:, n % 2, 2, 1:], dt[:, 2, 1:], ACT.Exp, scale=a_neg[:, 1, n:n + 1]).then_inc(s_a, 1)
                        if not first:
                            back_xt(j - 1)

                    act.wait_ge(s_set, 1)
                    for piece in (front_xT, front_up, front_uc1, front_softplus):
                        piece(0)
                    scan_steps(0, True, False)
                    scan_steps(1, False, False)
                    with act.Fori(2, NPAIR - 1) as j:
                        scan_steps(j, False, False)
                    scan_steps(NPAIR - 1, False, True)
                    for piece in (back_yg1, back_zT, back_exp, back_ct, back_xt):
                        piece(NPAIR - 1)

                @block.vector
                def _(dve):
                    def rows_of(i, j, arrays):
                        return arrays[i // 2][:, 2 * j + i % 2, :], (P if i < 2 else N_IMG)

                    def statistics(j, bn, count, mv):
                        for i in range(4):
                            x, r = rows_of(i, j, (H, H_img))
                            last = nc.vector.bn_stats(st4[0:r, i, :], x)
                        last.then_inc(bn, 1)
                        dve.wait_ge(s_set, 1)
                        dve.wait_ge(bn, count)
                        for i in range(4):
                            r = P if i < 2 else N_IMG
                            last = nc.vector.bn_aggr(mv[0:r, i, :], st4[0:r, i, :])
                        return last

                    def normalise(j, mv, factor, z_t, z_i):
                        for i in range(4):
                            x, r = rows_of(i, j, (H, H_img))
                            z = (z_t, z_i)[i // 2][:, i % 2, :]
                            last = nc.vector.tensor_scalar(z, x, mv[0:r, i, 0:1], factor[0:r, i:i + 1], ALU.subtract, ALU.mult)
                        return last

                    def front_norm_a(j):
                        st = Steps(dve, fd, FD, j)
                        at_start = isinstance(j, int) and j == 0
                        st.done(statistics(j, F["bn0"] if at_start else F["bn"], 1 if at_start else j, mv_f))
                        st.wait()
                        nc.vector.tensor_scalar(ve_f[:], mv_f[:, :, 1], EPS, None, ALU.add).then_inc(F["var"], 1)

                    def front_norm_b(j):
                        dve.wait_ge(F["rs"], j + 1)
                        dve.wait_ge(F["T"], j)
                        normalise(j, mv_f, rs_f, xn_t, xn_i).then_inc(F["xn"], 1)

                    def front_conv(j):
                        st = Steps(dve, fd, FD, j)
                        st.n = 1
                        dve.wait_ge(F["up"], j + 1)
                        dve.wait_ge(F["hi"], j)
                        dve.wait_ge(F["D"], j)
                        parts = ((slice(0, 2), 0), (slice(2, 3), 1))
                        for k in range(KC):
                            for seg, w in parts:
                                x = u_pad[:, seg, k:k + T]
                                out = uc_n[:, seg] if k == KC - 1 else conv[:, k % 2, seg]
                                if k == 0:
                                    st.done(nc.vector.tensor_scalar(out, x, wconv[:, w, 0:1], wconv[:, w, KC:KC + 1], ALU.mult, ALU.add))
                                else:
                                    st.wait(st.n - 1)
                                    last = nc.vector.scalar_tensor_tensor(out, x, wconv[:, w, k:k + 1], conv[:, (k - 1) % 2, seg],
                                                                          ALU.mult, ALU.add)
                                    if (k, w) == (KC - 1, 1):
                                        last.then_inc(F["conv"], 1)
                                    else:
                                        st.done(last)
                        dve.wait_ge(F["conv"], j + 1)
                        if not (isinstance(j, int) and j == 0):
                            dve.wait_ge(s_acc, NS * j - NS + 1)
                        for seg, w in parts:
                            last = nc.vector.tensor_scalar(y0[:, seg], uc_n[:, seg], wconv[:, w, KC + 1:KC + 2], W_SCALE, ALU.mult, ALU.mult)
                        last.then_inc(F["y0"], 1)

                    def front_dt(j):
                        dve.wait_ge(F["l"], j + 1)
                        nc.vector.scalar_tensor_tensor(dt_n[:], pb[6][:, 0:W3T], 0.0, sp_l[:], ALU.max, ALU.add).then_inc(F["dt"], 1)

                    def front_low(j):
                        dve.wait_ge(F["hi"], j + 1)
                        dve.wait_ge(F["D"], j + 1)
                        nc.vector.tensor_tensor(u16_n[:, 1, :], uc_n[:, 0:2, :].rearrange("p a t -> p (a t)"), u16_n[:, 0, :], ALU.subtract)
                        nc.vector.tensor_tensor(u16_n[D1:P, 2, :], uc1_n[0:D1, :], u16_n[0:D1, 3, :], ALU.subtract).then_inc(F["lo"], 1)

                    def take_dt(j):
                        dve.wait_ge(F["lo"], j + 1)
                        dve.wait_ge(s_C, NS * j)
                        nc.vector.tensor_copy(u16[:].rearrange("p a t -> p (a t)"), u16_n[:].rearrange("p a t -> p (a t)")).then_inc(s_uc, 1)
                        dve.wait_ge(F["dt"], j + 1)
                        dve.wait_ge(F["y0"], j + 1)
                        dve.wait_ge(s_a, NS * j)
                        nc.vector.tensor_copy(dt[:].rearrange("p a t -> p (a t)"), dt_n[:]).then_inc(s_dt, 1)
                        nc.vector.scalar_tensor_tensor(dtu[:], dt_n[:], 1.0 / W_SCALE, uc_n[:].rearrange("p a t -> p (a t)"),
                                                       ALU.mult, ALU.mult).then_inc(s_dtu, 1)

                    def gate(j):
                        dve.wait_ge(F["v"], j + 1)
                        nc.vector.tensor_scalar(sg[:, 0, :], ev_n[:], 1.0, W_SCALE, ALU.add, ALU.mult).then_inc(s_sg, 1)
                        dve.wait_ge(s_sg, 2 * j + 1)
                        nc.vector.reciprocal(sg[:, 1, :], sg[:, 0, :]).then_inc(s_sg, 1)

                    def back_yg(j):
                        dve.wait_ge(s_acc, NS * j + NS)
                        dve.wait_ge(s_sg, 2 * j + 2)
                        dve.wait_ge(K["op"], j)
                        nc.vector.tensor_tensor(yg[:], y[:, 1, :], sg[:, 1, :], ALU.mult).then_inc(K["yg"], 1)

                    def back_residual(j):
                        st = Steps(dve, bd, BD, j)
                        dve.wait_ge(K["op"], j + 1)
                        for i in range(4):
                            x, r = rows_of(i, j, (H, H_img))
                            last = nc.vector.tensor_tensor(x, pb[4 + i // 2][0:r, (i % 2) * D:(i % 2 + 1) * D], x, ALU.add)
                        last.then_inc(K["h2"], 1)
                        dve.wait_ge(s_set, 1)
                        dve.wait_ge(K["h2"], j + 1)
                        st.done(statistics(j, K["bn"], j + 1, mv_b))
                        st.wait()
                        nc.vector.tensor_scalar(sm[:, 0, :], mv_b[:, :, 1], EPS, None, ALU.add)
                        nc.vector.tensor_scalar(sm[:, 1, :], mv_b[:, :, 1], float(D), None, ALU.mult).then_inc(K["var"], 1)

                    def back_norm(j):
                        st = Steps(dve, bd, BD, j)
                        st.n = 1
                        dve.wait_ge(K["pw"], j + 1)
                        st.done(nc.vector.tensor_tensor(sm[:, 4, :], sm[:, 2, :], sm[:, 3, :], ALU.mult))
                        st.wait()
                        st.done(nc.vector.tensor_scalar(sm[:, 5, :], sm[:, 4, :], 1e-6, None, ALU.add))
                        st.wait()
                        st.done(nc.vector.reciprocal(sm[:, 6, :], sm[:, 5, :]))
                        st.wait()
                        st.done(nc.vector.tensor_tensor(sm[:, 7, :], sm[:, 6, :], sm[:, 2, :], ALU.mult))
                        st.wait()
                        dve.wait_ge(K["x"], j)
                        normalise(j, mv_b, sm[:, 7, :], zn_t, zn_i).then_inc(K["zn"], 1)

                    def back_max(j):
                        st = Steps(dve, bd, BD, j)
                        st.n = 5
                        dve.wait_ge(K["L"], j + 1)
                        logits = pb[4][:, 0:4 * SLOTS].rearrange("p (i k) -> p i k", i=4)
                        st.done(nc.vector.tensor_reduce(cmax[:, 0, :], logits, AX.X, ALU.max))
                        nc.vector.tensor_reduce(dmax[:, 0, :], pb[5][0:SLOTS, 0:W2T].rearrange("p (s t) -> p s t", s=2), AX.X, ALU.max, negate=True)
                        st.wait()
                        nc.vector.tensor_tensor(cexp[:, 0], logits, cmax[:, 0, :].unsqueeze(2).to_broadcast([P, 4, SLOTS]),
                                                ALU.subtract).then_inc(K["mx"], 1)

                    def back_softmax(j):
                        st = Steps(dve, bd, BD, j)
                        st.n = 6
                        dve.wait_ge(K["e"], j + 1)
                        dview = dexp[:, 0, :].rearrange("p (s t) -> p s t", s=2)
                        st.done(nc.vector.tensor_reduce(cmax[:, 1, :], cexp[:, 1], AX.X, ALU.add))
                        st.done(nc.vector.tensor_reduce(dmax[:, 1, :], dview, AX.X, ALU.add))
                        st.wait(st.n - 1)
                        st.done(nc.vector.reciprocal(cmax[:, 2, :], cmax[:, 1, :]))
                        st.wait(st.n - 1)
                        st.done(nc.vector.reciprocal(dmax[:, 2, :], dmax[:, 1, :]))
                        st.wait(st.n - 1)
                        dve.wait_ge(K["T3"], j)
                        nc.vector.tensor_tensor(cexp[:, 2], cexp[:, 1], cmax[:, 2, :].unsqueeze(2).to_broadcast([P, 4, SLOTS]), ALU.mult)
                        st.wait()
                        nc.vector.tensor_tensor(dexp[:, 1, :].rearrange("p (s t) -> p s t", s=2), dview,
                                                dmax[:, 2, :].unsqueeze(2).to_broadcast([SLOTS, 2, T]), ALU.mult).then_inc(K["cd"], 1)

                    def back_dtok(j):
                        dve.wait_ge(K["T3"], j + 1)
                        dve.wait_ge(K["x"], j)
                        nc.vector.tensor_copy(d_tok[:].rearrange("p i k -> p (i k)"), pb[5][:, 0:4 * SLOTS]).then_inc(K["dT"], 1)

                    def input_of(j, n):
                        m = NS * j + n
                        dve.wait_ge(s_B, m + 1)
                        nc.vector.tensor_tensor(inp[:, n % 2, :], pb[n % 2][:, 0:W3T], dtu[:], ALU.mult).then_inc(s_in, 1)

                    def scan_steps(j, first, last_pair):
                        take_dt(j)
                        dve.wait_ge(s_dtu, j + 1)
                        input_of(j, 0)
                        back = {0: back_yg, 3: back_residual, 4: back_norm, 9: back_max, 10: back_softmax, 12: back_dtok}
                        front = {0: (front_norm_a,), 1: (front_norm_b,), 6: (front_conv,), 12: (front_low, front_dt)}
                        for n in range(NS):
                            m = NS * j + n
                            dve.wait_ge(s_a, m + 1)
                            dve.wait_ge(s_in, m + 1)
                            nc.vector.tensor_tensor_scan(state[:, n % 2, :], decay[:, n % 2].rearrange("p a t -> p (a t)"), inp[:, n % 2, :], 0.0,
                                                         ALU.mult, ALU.add).then_inc(s_scan, 1)
                            if n + 1 < NS:
                                input_of(j, n + 1)
                            dve.wait_ge(s_C, m + 1)
                            dve.wait_ge(s_scan, m + 1)
                            if n >= 2 or not first:
                                dve.wait_ge(s_acc, m - 1)
                            nc.vector.tensor_tensor(cstate[:, n % 2, :], pb[2 + n % 2][:, 0:W3T], state[:, n % 2, :], ALU.mult).then_inc(s_cs, 1)
                            if n in back and not first:
                                back[n](j - 1)
                            if n == 0:
                                gate(j)
                            for piece in front.get(n, ()):
                                if not last_pair:
                                    piece(j + 1)

                    nc.vector.memset(mv_f[:], 1.0)
                    nc.vector.memset(mv_b[:], 1.0)
                    nc.vector.memset(xT1[:], 1.0)
                    nc.vector.memset(uc1_n[:], 1.0)
                    nc.vector.memset(u16_n[:], 1.0)
                    nc.vector.memset(yg1[:], 1.0)
                    nc.vector.memset(u_pad[:], 0.0)
                    nc.vector.memset(decay[:], 0.0).then_inc(s_set, 1)
                    dve.wait_ge(s_set, 1)
                    front_norm_a(0)
                    front_norm_b(0)
                    front_conv(0)
                    front_low(0)
                    front_dt(0)
                    scan_steps(0, True, False)
                    scan_steps(1, False, False)
                    with dve.Fori(2, NPAIR - 1) as j:
                        scan_steps(j, False, False)
                    scan_steps(NPAIR - 1, False, True)
                    for piece in (back_yg, back_residual, back_norm, back_max, back_softmax, back_dtok):
                        piece(NPAIR - 1)

                @block.gpsimd
                def _(pool):
                    def front_rs(j):
                        pool.wait_ge(F["var"], j + 1)
                        pool.wait_ge(F["xn"], j)
                        nc.gpsimd.tensor_tensor(rs_f[:], ve_f[:], half4[:, 0, :], ALU.pow).then_inc(F["rs"], 1)

                    def back_pw(j):
                        pool.wait_ge(K["var"], j + 1)
                        pool.wait_ge(K["zn"], j)
                        nc.gpsimd.tensor_tensor(sm[:, 2, :], sm[:, 0, :], half4[:, 0, :], ALU.pow)
                        nc.gpsimd.tensor_tensor(sm[:, 3, :], sm[:, 1, :], half4[:, 1, :], ALU.pow).then_inc(K["pw"], 1)

                    def scan_steps(j, first, last_pair):
                        for n in range(NS):
                            m = NS * j + n
                            if n == 1 and not last_pair:
                                front_rs(j + 1)
                            if n == 4 and not first:
                                back_pw(j - 1)
                            pool.wait_ge(s_cs, m + 1)
                            if n == 0:
                                pool.wait_ge(F["y0"], j + 1)
                                pool.wait_ge(s_acc, NS * j)
                                src = y0[:].rearrange("p a t -> p (a t)")
                            else:
                                pool.wait_ge(s_acc, m)
                                src = y[:, (n - 1) % 2, :]
                            if n == 1:
                                pool.wait_ge(K["yg"], j)
                            nc.gpsimd.tensor_tensor(y[:, n % 2, :], src, cstate[:, n % 2, :], ALU.add).then_inc(s_acc, 1)

                    front_rs(0)
                    scan_steps(0, True, False)
                    scan_steps(1, False, False)
                    with pool.Fori(2, NPAIR - 1) as j:
                        scan_steps(j, False, False)
                    scan_steps(NPAIR - 1, False, True)
                    back_pw(NPAIR - 1)

        slot_experts(nc, io, sem, H, H_img, xt0, xt1, c_all, pb)


def slot_experts(nc, io, sem, H, H_img, xt0, xt1, c_all, pb):
    with ExitStack() as ctx:
        def sb(name, shape, dt=F32):
            return ctx.enter_context(nc.sbuf_tensor(name, shape, dt))

        wd0, wd1 = sb("wd0", [P, NE, HID]), sb("wd1", [D1 + 1, NE, HID])
        wu = sb("wu", [HID + 1, NE, D])
        hid = sb("hid", [HID + 8, NE, P])
        y_rows = sb("y_rows", [P, NE, D])
        y_slots = sb("y_slots", [SLOTS, B, D])
        ct = sb("ct", [SLOTS, 2, W2T])
        out_t, out_i = sb("out_t", [P, 2, 2, D]), sb("out_i", [N_IMG, 2, 2, D])
        x_w, x_one = sem("expert_weights"), sem("expert_ones")
        x_h, x_g, x_y, x_ye = sem("expert_hidden"), sem("expert_gelu"), sem("expert_y"), sem("expert_y_copied")
        x_scr, x_sl = sem("slots_written"), sem("slots_loaded_back")
        o_ct, o_mm, o_sum = sem("out_c_copied"), sem("out_product"), sem("out_summed")
        o_st = [sem(f"out_stored{i}") for i in range(2)]
        out = io["out"]
        with nc.Block() as block:
            @block.sync
            def _(sp):
                sp.dma_start(wd0[:], io["wd"][0:P]).then_inc(x_w, 16)
                sp.dma_start(wd1[:], io["wd"][P:D + 1]).then_inc(x_w, 16)
                sp.dma_start(wu[:], io["wu"]).then_inc(x_w, 16)
                sp.wait_ge(x_ye, NE // 2)
                sp.dma_start(io["scratch_y"], y_rows[:].rearrange("p e d -> p (e d)")).then_inc(x_scr, 16)
                sp.wait_ge(x_scr, 16)
                for e in range(NE):
                    sp.dma_start(y_slots[NP_ * e:NP_ * (e + 1)],
                                 io["scratch_y"].rearrange("(b p) (e d) -> e p b d", p=NP_, e=NE)[e]).then_inc(x_sl, 16)

                def store(j, par):
                    sp.wait_ge(o_sum, j + 1)
                    sp.dma_start(out[bass.ds(2 * j, 2), N_IMG:T, :].rearrange("b t d -> t b d"), out_t[:, par]).then_inc(o_st[par], 16)
                    sp.dma_start(out[bass.ds(2 * j, 2), 0:N_IMG, :].rearrange("b t d -> t b d"), out_i[:, par]).then_inc(o_st[par], 16)

                with sp.Fori(0, NPAIR // 2) as i:
                    store(2 * i, 0)
                    store(2 * i + 1, 1)
                for stored in o_st:
                    sp.wait_ge(stored, 16 * NPAIR)

            @block.tensor
            def _(pe):
                pe.wait_ge(x_w, 48)
                for e in range(NE):
                    o = pb[e // 4][0:HID, (e % 4) * P:(e % 4 + 1) * P].rearrange("h (b p) -> h b p", p=NP_)
                    nc.tensor.matmul(o, wd0[:, e, :], xt0[:, :, NP_ * e:NP_ * (e + 1)], start=True, stop=False)
                    last = nc.tensor.matmul(o, wd1[:, e, :], xt1[:, :, NP_ * e:NP_ * (e + 1)], start=False, stop=True)
                    if e % 4 == 3:
                        last.then_inc(x_h, 1)
                for e in range(NE):
                    if e % 4 == 0:
                        pe.wait_ge(x_g, e // 4 + 1)
                    last = nc.tensor.matmul(pb[2 + e // 2][:, (e % 2) * D:(e % 2 + 1) * D], hid[0:HID + 1, e, :], wu[:, e, :], start=True, stop=True)
                    if e % 2:
                        last.then_inc(x_y, 1)
                pe.wait_ge(x_sl, 16 * NE)
                pe.wait_ge(x_ye, NE // 2)

                def product(j, par):
                    pe.wait_ge(o_ct, j + 1)
                    if not (isinstance(j, int) and j < 2):
                        pe.wait_ge(o_sum, j - 1)
                    for s in range(2):
                        rhs = y_slots[:, bass.ds(2 * j + s, 1), :].rearrange("k b d -> k (b d)")
                        c = s * T
                        nc.tensor.matmul(pb[2 * par][:, s * D:(s + 1) * D], ct[:, par, c + N_IMG:c + T], rhs, start=True, stop=True)
                        last = nc.tensor.matmul(pb[2 * par + 1][:, s * D:(s + 1) * D], ct[:, par, c:c + P], rhs, start=True, stop=True)
                    last.then_inc(o_mm, 1)

                product(0, 0)
                product(1, 1)
                with pe.Fori(1, NPAIR // 2) as i:
                    product(2 * i, 0)
                    product(2 * i + 1, 1)

            @block.scalar
            def _(act):
                act.wait_ge(x_one, 1)
                for i in range(2):
                    act.wait_ge(x_h, i + 1)
                    nc.scalar.activation(hid[0:HID, 4 * i:4 * i + 4, :], pb[i][0:HID, :].rearrange("h (e n) -> h e n", e=4), ACT.Gelu).then_inc(x_g, 1)

                def copy_c(j, par):
                    if not (isinstance(j, int) and j < 2):
                        act.wait_ge(o_mm, j - 1)
                    nc.scalar.copy(ct[:, par, :], c_all[:, bass.ds(j, 1), :].rearrange("k a t -> k (a t)")).then_inc(o_ct, 1)

                copy_c(0, 0)
                copy_c(1, 1)
                with act.Fori(1, NPAIR // 2) as i:
                    copy_c(2 * i, 0)
                    copy_c(2 * i + 1, 1)

            @block.vector
            def _(dve):
                nc.vector.memset(hid[:], 1.0).then_inc(x_one, 1)
                for i in range(NE // 2):
                    dve.wait_ge(x_y, i + 1)
                    nc.vector.tensor_copy(y_rows[:, 2 * i:2 * i + 2, :], pb[2 + i][:, 0:2 * D].rearrange("p (e d) -> p e d", e=2)).then_inc(x_ye, 1)

                def total(i, par):
                    j = 2 * i + par
                    dve.wait_ge(o_mm, j + 1)
                    dve.wait_ge(o_st[par], 32 * i)
                    nc.vector.tensor_tensor(out_t[:, par], pb[2 * par][:, 0:2 * D].rearrange("p (s d) -> p s d", s=2),
                                            H[:, bass.ds(2 * j, 2), :], ALU.add)
                    nc.vector.tensor_tensor(out_i[:, par], pb[2 * par + 1][0:N_IMG, 0:2 * D].rearrange("p (s d) -> p s d", s=2),
                                            H_img[:, bass.ds(2 * j, 2), :], ALU.add).then_inc(o_sum, 1)

                with dve.Fori(0, NPAIR // 2) as i:
                    total(i, 0)
                    total(i, 1)


def ssm_layout(x):
    def bias_row(w, b):
        return np.concatenate([w, b[None]], axis=0)

    def mixed(a):
        return np.stack([a[:P], np.concatenate([a[P:], a[P:]])], axis=1)

    def by_state(w, b):
        w = bias_row(w, b)
        return np.ascontiguousarray(w.reshape(D + 1, D, NS).transpose(0, 2, 1))

    wconv = np.concatenate([x["L0_attn_Wconv"], x["L0_attn_bconv"][:, None], x["L0_attn_D"][:, None]], axis=1)
    wd = np.concatenate([x["L0_ffn_W_down"], x["L0_ffn_b_down"][:, None, :]], axis=1).transpose(1, 0, 2)
    wu = np.concatenate([x["L0_ffn_W_up"], x["L0_ffn_b_up"][:, None, :]], axis=1).transpose(1, 0, 2)
    return dict(
        wi=bias_row(x["L0_attn_Wi"], x["L0_attn_bi"]), wdt=bias_row(x["L0_attn_Wdt"], x["L0_attn_bdt"]),
        wso=bias_row(x["L0_attn_Wo"], x["L0_attn_bo"]), wB=by_state(x["L0_attn_WB"], x["L0_attn_bB"]),
        wC=by_state(x["L0_attn_WC"], x["L0_attn_bC"]), a_log=mixed(x["L0_attn_A_log"]), wconv=mixed(wconv),
        slot_params=x["L0_ffn_slot_params"].reshape(D, SLOTS), slot_scale=x["L0_ffn_scale"].reshape(1),
        wd=wd, wu=wu)


def build(nc, io):
    with ExitStack() as ctx:
        def sb(name, shape, dt=F32):
            return ctx.enter_context(nc.sbuf_tensor(name, shape, dt))

        def sem(name):
            return ctx.enter_context(nc.semaphore(name))

        H = sb("H", [P, B, D])
        H_img = sb("H_img", [N_IMG, B, D])
        ident = sb("ident", [P, P])
        ident_bf = sb("ident_bf", [P, P], BF16)
        ident_h = sb("ident_h", [P, P], F16)
        band_f = sb("band_f", [P, P])
        band = sb("band", [P, P], BF16)
        half = sb("half", [P, 1])
        s_id = sem("identity_loaded")
        with nc.Block() as block:
            @block.sync
            def _(sp):
                sp.dma_start(ident[:], io["ident"]).then_inc(s_id, 16)
                sp.dma_start(band_f[:], io["band"]).then_inc(s_id, 16)

            @block.vector
            def _(dve):
                nc.vector.memset(half[:], -0.5)
                dve.wait_ge(s_id, 32)
                nc.vector.tensor_copy(ident_bf[:], ident[:])
                nc.vector.tensor_copy(ident_h[:], ident[:])
                nc.vector.tensor_copy(band[:], band_f[:])
        consts = dict(ident=ident, ident_bf=ident_bf, ident_h=ident_h, band=band, half=half)
        patch_embedding(nc, io, sem, H_img, consts)
        text_encoder(nc, io, sem, H, consts)
        ssm_and_slots(nc, io, sem, H, H_img, consts)


def kernel(**inputs):
    import concourse.bacc as _bacc
    from concourse.bass_utils import run_bass_kernel_spmd as _run

    x = {k: np.asarray(v) for k, v in inputs.items()}
    far = np.abs(np.arange(P)[:, None] - np.arange(P)[None, :]) > WIN
    arrays = {**text_layout(x), **tok_layout(x), **ssm_layout(x),
              "ident": np.eye(P, dtype=np.float32), "band": np.where(far, MASKED, 0.0).astype(np.float32)}
    nc = _bacc.Bacc("TRN2", target_bir_lowering=False, num_devices=1)
    io, feeds = {}, {}
    for name, a in arrays.items():
        a = np.ascontiguousarray(a)
        feeds[f"in_{name}"] = a
        io[name] = nc.dram_tensor(f"in_{name}", a.shape, mybir.dt.from_np(a.dtype), kind="ExternalInput").ap()
    io["out"] = nc.dram_tensor("out_h", (B, T, D), F32, kind="ExternalOutput").ap()
    io["scratch_tok"] = nc.dram_tensor("scratch_tok", (6 * B, 6 * D), F32, kind="Internal").ap()
    io["scratch_y"] = nc.dram_tensor("scratch_y", (P, NE * D), F32, kind="Internal").ap()
    build(nc, io)
    r = _run(nc, [feeds], core_ids=[0])
    return r.results[0]["out_h"]
```

```python
from contextlib import ExitStack

import numpy as np

import concourse.bass as bass
from concourse import mybir

ALU = mybir.AluOpType
ACT = mybir.ActivationFunctionType
AX = mybir.AxisListType
F32 = mybir.dt.float32
BF16 = mybir.dt.bfloat16
F16 = mybir.dt.float16
I32 = mybir.dt.int32

P = 128
D = 192
D1 = D - P
B = 32
S = 128
N_IMG = 36
T = N_IMG + S
L = 4
NH = 12
DH = D // NH
FF = 4 * D
NF = FF // P
WIN = 64
N_PAD = WIN
EPS_TXT = 1e-12
EPS = 1e-5
MASKED = -999292928.0
NS = 16
KC = 4
W_SCALE = 64.0
Q_SCALE = DH ** -0.5 / W_SCALE
SLOTS = 32
NE = 8
NP_ = 4
HID = 24


HEADS_OF_GROUP = [(2, 3, 8), (6, 7, 9), (0, 1, 10), (4, 5, 11)]
ROW_GROUP = (1, 3, 0, 2)

QKV = 6 * P + D

PASSES = ((0, 0, P), (1, 0, P), (0, 1, P), (2, 2, P), (3, 3, 97))


def text_encoder(nc, io, sem, H, image_loaded, consts):
    ident, ident_bf, ident_h, band, half = (consts[k] for k in ("ident", "ident_bf", "ident_h", "band", "half"))
    with ExitStack() as ctx:
        def sb(name, shape, dt=F32):
            return ctx.enter_context(nc.sbuf_tensor(name, shape, dt))

        def psum(name, shape, dt=F32):
            return ctx.enter_context(nc.psum_tensor(name, shape, dt))

        key_bias = sb("key_bias", [P, B, S], BF16)
        w_qkv_raw, w_qkv = sb("w_qkv_raw", [P, 3, QKV]), sb("w_qkv", [P, 4, QKV], F16)
        w_qkv_high3 = sb("w_qkv_high3", [P, QKV], F16)
        wo0, wo1 = sb("wo0", [P, D]), sb("wo1", [D1 + 1, D])
        w1_raw, w2_raw = sb("w1_raw", [P, 3, FF]), sb("w2_raw", [P, NF, D])
        w1 = sb("w1", [P, 4, FF], F16)
        w1_high3 = sb("w1_high3", [P, FF], F16)
        w2 = sb("w2", [P, 2, NF, D], F16)
        low_scale = sb("low_scale", [P, 1])
        q_scale = sb("q_scale", [P, 1])
        b2_rows = sb("b2_rows", [P, D])
        ln1_s, ln1_b = sb("ln1_s", [P, D]), sb("ln1_b", [P, D])
        ln2_s, ln2_b = sb("ln2_s", [P, D]), sb("ln2_b", [P, D])
        x16 = sb("x16", [P, 2, 2, D], F16)
        xT16 = sb("xT16", [P, 2, 4, S], F16)
        v_sb = sb("v_sb", [P, 2, NH // 2, 3 * DH])
        oT0, oT1 = sb("oT0", [P, S]), sb("oT1", [D1 + 1, S])
        xres = sb("xres", [P, 2, D])
        stats = sb("stats", [P, 6])
        mv = sb("mv", [P, 2, 2])
        rstd = sb("rstd", [P, 1])
        var_eps = sb("var_eps", [P, 2])
        ln_y = sb("ln_y", [P, 3, D])
        bank = [psum(f"txt_bank{i}", [P, 512]) for i in range(8)]

        def norm_rows(pool, chain, n, x, mean, var_eps, scale, shift, out):
            nc.gpsimd.tensor_tensor(rstd[:], var_eps, half[:], ALU.pow).then_inc(chain, 1)
            nc.gpsimd.tensor_tensor(ln_y[:, 0, :], x, mean.to_broadcast([P, D]), ALU.subtract).then_inc(chain, 1)
            pool.wait_ge(chain, n + 2)
            nc.gpsimd.tensor_tensor(ln_y[:, 1, :], ln_y[:, 0, :], rstd[:].to_broadcast([P, D]), ALU.mult).then_inc(chain, 1)
            pool.wait_ge(chain, n + 3)
            nc.gpsimd.tensor_tensor(ln_y[:, 2, :], ln_y[:, 1, :], scale, ALU.mult).then_inc(chain, 1)
            pool.wait_ge(chain, n + 4)
            return nc.gpsimd.tensor_tensor(out, ln_y[:, 2, :], shift, ALU.add)

        s_const = sem("txt_constants_set")
        f_h = sem("layer_h_written")
        w_attn, w_ffn = sem("attn_weights"), sem("ffn_weights")
        N_WA = 10
        N_WF = 10

        def load_attn(sp, l):
            w = io["wqkv"][l]
            for dst, src in ((w_qkv_raw[:, 0], w[0:P]), (w_qkv_raw[0:D1, 1], w[P:D]), (w_qkv_raw[D1:P, 1], w[P:D]),
                             (w_qkv_raw[0:D1, 2], w[P:D]), (w_qkv_raw[D1:D1 + 1, 2], w[D:D + 1]), (w_qkv_raw[96:97, 2], w[D:D + 1]),
                             (wo0[:], io["wo"][l, 0:P]), (wo1[:], io["wo"][l, P:D + 1]),
                             (ln1_s[:], io["ln1_s"][l].partition_broadcast(P)),
                             (ln1_b[:], io["ln1_b"][l].partition_broadcast(P))):
                sp.dma_start(dst, src).then_inc(w_attn, 16)

        def load_ffn(sp, l):
            for dst, src in ((w1_raw[:, 0], io["w1"][l, 0:P]), (w1_raw[0:D1, 1], io["w1"][l, P:D]),
                             (w1_raw[D1:P, 1], io["w1"][l, P:D]), (w1_raw[0:D1, 2], io["w1"][l, P:D]),
                             (w1_raw[D1:D1 + 1, 2], io["w1"][l, D:D + 1]), (w1_raw[96:97, 2], io["w1"][l, D:D + 1]),
                             (w2_raw[:], io["w2"][l].rearrange("(c p) n -> p c n", p=P)),
                             (b2_rows[:], io["b2"][l].partition_broadcast(P)),
                             (ln2_s[:], io["ln2_s"][l].partition_broadcast(P)),
                             (ln2_b[:], io["ln2_b"][l].partition_broadcast(P))):
                sp.dma_start(dst, src).then_inc(w_ffn, 16)

        with ExitStack() as emb_ctx:
            def tmp(name, shape, dt=F32):
                return emb_ctx.enter_context(nc.sbuf_tensor(name, shape, dt))
            pos = tmp("pos", [P, D])
            mask_i = tmp("mask_i", [P, B * S], I32)
            emb_s, emb_b = tmp("emb_s", [P, D]), tmp("emb_b", [P, D])
            emb_stats, emb_mv = tmp("emb_stats", [P, B, 6]), tmp("emb_mv", [P, B, 2])
            emb_var, emb_rstd = tmp("emb_var", [P, B]), tmp("emb_rstd", [P, B])
            BP = B // 4
            s_loads, s_mask, s_dve = sem("txt_small_loads"), sem("txt_mask_loaded"), sem("txt_dve_steps")
            s_var, s_rstd, s_n = sem("txt_emb_var"), sem("txt_emb_rstd"), sem("txt_emb_normalised")
            with nc.Block() as block:
                @block.sync
                def _(sp):
                    sp.dma_start(pos[:], io["pos"]).then_inc(s_loads, 16)
                    sp.dma_start(emb_s[:], io["emb_ln_s"].partition_broadcast(P)).then_inc(s_loads, 16)
                    sp.dma_start(emb_b[:], io["emb_ln_b"].partition_broadcast(P)).then_inc(s_loads, 16)
                    sp.dma_start(q_scale[:], io["q_scale"]).then_inc(s_mask, 16)
                    sp.dma_start(mask_i[:], io["mask"].partition_broadcast(P)).then_inc(s_mask, 16)
                    sp.wait_ge(s_const, 1)
                    load_attn(sp, 0)
                    load_ffn(sp, 0)
                    sp.wait_ge(image_loaded, 16)

                def over(ap, n):
                    return ap.unsqueeze(1).to_broadcast([P, n, D])

                @block.vector
                def _(dve):
                    nc.vector.memset(v_sb[:], 0.0)
                    nc.vector.memset(xT16[:], 1.0)
                    nc.vector.memset(w1_raw[:, 2], 0.0)
                    nc.vector.memset(w_qkv_raw[:, 2], 0.0)
                    nc.vector.memset(low_scale[:D1], W_SCALE)
                    nc.vector.memset(low_scale[D1:96], 0.0)
                    nc.vector.memset(low_scale[96:], W_SCALE)
                    nc.vector.memset(oT1[:], 1.0).then_inc(s_const, 1)
                    dve.wait_ge(s_loads, 48)
                    nc.vector.tensor_tensor(H[:], H[:], over(pos[:], B), ALU.add).then_inc(s_dve, 1)
                    dve.wait_ge(s_dve, 1)
                    for b in range(B):
                        last = nc.vector.bn_stats(emb_stats[:, b, :], H[:, b, :])
                    last.then_inc(s_dve, 1)
                    dve.wait_ge(s_dve, 2)
                    for b in range(B):
                        last = nc.vector.bn_aggr(emb_mv[:, b, :], emb_stats[:, b, :])
                    last.then_inc(s_dve, 1)
                    dve.wait_ge(s_dve, 3)
                    nc.vector.tensor_scalar(emb_var[:], emb_mv[:, :, 1], EPS_TXT, None, ALU.add).then_inc(s_var, 1)
                    dve.wait_ge(s_mask, 32)
                    nc.vector.tensor_scalar(key_bias[:].rearrange("p b s -> p (b s)"), mask_i[:], 0.0, MASKED,
                                            ALU.is_le, ALU.mult).then_inc(s_dve, 1)
                    dve.wait_ge(s_dve, 4)
                    nc.vector.tensor_tensor(key_bias[:], key_bias[:], band[:].unsqueeze(1).to_broadcast([P, B, S]), ALU.min).then_inc(s_dve, 1)
                    dve.wait_ge(s_rstd, 1)
                    for b in range(B):
                        last = nc.vector.tensor_scalar(H[:, b, :], H[:, b, :], emb_mv[:, b, 0:1], emb_rstd[:, b:b + 1], ALU.subtract, ALU.mult)
                        if b in (BP - 1, B - 1):
                            last.then_inc(s_n, 1)
                    dve.wait_ge(s_n, 2)
                    nc.vector.tensor_tensor(H[:, BP:], H[:, BP:], over(emb_s[:], B - BP), ALU.mult).then_inc(s_dve, 1)
                    dve.wait_ge(s_dve, 6)
                    nc.vector.tensor_tensor(H[:, BP:], H[:, BP:], over(emb_b[:], B - BP), ALU.add).then_inc(f_h, B - BP)

                @block.gpsimd
                def _(pool):
                    pool.wait_ge(s_var, 1)
                    nc.gpsimd.tensor_tensor(emb_rstd[:], emb_var[:], half[:].to_broadcast([P, B]), ALU.pow).then_inc(s_rstd, 1)
                    pool.wait_ge(s_n, 1)
                    pool.wait_ge(s_loads, 48)
                    nc.gpsimd.tensor_tensor(H[:, 0:BP], H[:, 0:BP], over(emb_s[:], BP), ALU.mult).then_inc(s_rstd, 1)
                    pool.wait_ge(s_rstd, 2)
                    nc.gpsimd.tensor_tensor(H[:, 0:BP], H[:, 0:BP], over(emb_b[:], BP), ALU.add).then_inc(f_h, BP)

        q16, q_masked = sb("q16", [P, 3, S], F16), sb("q_masked", [P, 3, S], F16)
        k16 = sb("k16", [P, 2, 3, S], F16)
        neg_max = sb("neg_max", [P, 4, 3])
        pad_exp, sums = sb("pad_exp", [P, 4, 3]), sb("sums", [P, 4, 3])
        den = sb("den", [P, 2, 4, 3])
        probs = sb("probs", [P, 4, 3, S])
        pT = sb("pT", [P, 2, 3 * S])
        fT, fT16 = sb("fT", [P, 2, NF * S]), sb("fT16", [P, 2, 2, NF * S], F16)

        a_high, a_low = sem("attn_weights_high"), sem("attn_weights_low")
        x_high, s_xin, s_hTp, s_hT = sem("x_high"), sem("attn_x_copied"), sem("attn_xT_done"), sem("attn_xT_copied")
        s_sc, s_max, s_exp, s_pad = sem("scores_done"), sem("max_done"), sem("exp_done"), sem("pad_exp_done")
        s_q, s_kv = sem("q_done"), sem("kv_done")
        s_qkh, s_qe, s_ke, s_ve = sem("qk_first_halves"), sem("q_copied"), sem("k_copied"), sem("v_copied")
        s_pTp, s_pTe, s_pv = sem("probsT_done"), sem("probsT_copied"), sem("pv_done")
        s_den, s_norm, s_oTe = sem("denominator_steps"), sem("probs_normalised"), sem("oT_copied")
        s_wo, s_xadd, s_st, s_stat = sem("wo_done"), sem("attn_added"), sem("attn_bn"), sem("attn_stats")
        s_h, s_pc = sem("attn_h_written"), sem("attn_pool_steps")
        s_ag, f_ag = sem("attn_aggr"), sem("ffn_aggr")
        f_xin, f_T, f_hT = sem("ffn_x_copied"), sem("ffn_xT_done"), sem("ffn_xT_copied")
        f_1, f_g, f_2 = sem("ffn1_done"), sem("gelu_done"), sem("ffn2_done")
        f_c, f_st, f_stat = sem("ffn_added"), sem("ffn_bn"), sem("ffn_stats")
        f_pc = sem("ffn_pool_steps")
        f_high, f_low = sem("ffn_weights_high"), sem("ffn_weights_low")
        f_fh, f_fl = sem("gelu_high"), sem("gelu_low")
        with nc.Block() as block:
            @block.sync
            def _(sp):
                with sp.Fori(1, L) as l:
                    sp.wait_ge(s_h, B * l)
                    load_attn(sp, l)
                    sp.wait_ge(f_h, B * l + B)
                    load_ffn(sp, l)

            @block.tensor
            def _(pe):
                def x_transposed(b, par, done):
                    for part, half_of_x, at, row in ((0, 0, slice(0, P), 0), (1, 1, slice(0, P), 0), (2, 0, slice(P, D), 0),
                                                     (2, 1, slice(P, D), D1), (3, 0, slice(P, D), 0)):
                        rows = at.stop - at.start
                        last = nc.tensor.matmul(b[row:row + rows, part * S:(part + 1) * S], x16[:, par, half_of_x, at], ident_h[:],
                                                start=True, stop=True)
                    last.then_inc(done, 1)

                def attn_x_transposed(g, par):
                    pe.wait_ge(s_xin, g + 1)
                    x_transposed(bank[7], par, s_hTp)

                def project_q(g, par):
                    pe.wait_ge(s_hT, g + 1)
                    for t in range(3):
                        for k, (a, b, rows) in enumerate(PASSES):
                            nc.tensor.matmul(bank[4][:, t * S:(t + 1) * S], w_qkv[0:rows, a, t * P:(t + 1) * P], xT16[0:rows, par, b, :],
                                             start=(k == 0), stop=(k == len(PASSES) - 1))
                    for k, (a, b, rows) in enumerate(PASSES):
                        last = nc.tensor.matmul(bank[4][:, 3 * S:3 * S + D1], xT16[0:rows, par, b, :], w_qkv[0:rows, a, 7 * P:QKV],
                                                start=(k == 0), stop=(k == len(PASSES) - 1))
                    last.then_inc(s_q, 1)

                def project_kv(g, par):
                    pe.wait_ge(s_hT, g + 1)
                    for t in (3, 4, 5):
                        for k, (a, b, rows) in enumerate(PASSES):
                            nc.tensor.matmul(bank[5][:, (t - 3) * S:(t - 2) * S], w_qkv[0:rows, a, t * P:(t + 1) * P], xT16[0:rows, par, b, :],
                                             start=(k == 0), stop=(k == len(PASSES) - 1))
                    for k, (a, b, rows) in enumerate(PASSES):
                        last = nc.tensor.matmul(bank[5][:, 3 * S:4 * S], xT16[0:rows, par, b, :], w_qkv[0:rows, a, 6 * P:7 * P],
                                                start=(k == 0), stop=(k == len(PASSES) - 1))
                    last.then_inc(s_kv, 1)

                def scores(g, u, first):
                    pe.wait_ge(s_qe, g + 1)
                    pe.wait_ge(s_ke, g + 1)
                    for r0 in (0, 2):
                        for r in (r0, r0 + 1):
                            if not first:
                                pe.wait_ge(s_exp, 4 * g - 3 + r)
                            nc.tensor.matmul(bank[r][:, 0:3 * S].rearrange("p (i s) -> p i s", i=3), ident_bf[:],
                                             key_bias[:, bass.ds(u, 1), :].to_broadcast([P, 3, S]),
                                             start=True, stop=True)
                        for i in range(3):
                            for part in range(2):
                                for r in (r0, r0 + 1):
                                    at = slice(32 * ROW_GROUP[r], 32 * ROW_GROUP[r] + 32)
                                    last = nc.tensor.matmul(bank[r][:, i * S:(i + 1) * S], q16[at, i, :], k16[at, part, i, :],
                                                            start=False, stop=(part == 1), skip_group_check=True)
                        last.then_inc(s_sc, 1)

                def probs_transposed(g, r):
                    pe.wait_ge(s_norm, 4 * g + r + 1)
                    for i in range(3):
                        last = nc.tensor.transpose(bank[6 + r % 2][:, i * S:(i + 1) * S], probs[:, r, i, :], ident[:])
                    last.then_inc(s_pTp, 1)

                def outputs(g, r0, par):
                    pe.wait_ge(s_ve, g + 1)
                    pe.wait_ge(s_pTe, 4 * g + r0 + 2)
                    for i, r in ((0, r0), (0, r0 + 1), (2, r0), (1, r0), (1, r0 + 1), (2, r0 + 1)):
                        h = HEADS_OF_GROUP[r][i]
                        pair, odd = h // 2, h % 2
                        row = 32 * pair if pair < 4 else D1 + 32 * (pair - 4)
                        last = nc.tensor.matmul(bank[6 + pair // 4][row:row + 32, 3 * S:4 * S], v_sb[:, par, pair, DH * odd:DH * odd + 2 * DH],
                                                pT[:, r % 2, i * S:(i + 1) * S], start=(odd == 0), stop=(odd == 1),
                                                skip_group_check=True)
                    last.then_inc(s_pv, 1)

                def project_o(g):
                    pe.wait_ge(s_oTe, g + 1)
                    nc.tensor.matmul(bank[4][:, 0:D], oT0[:], wo0[:], start=True, stop=False)
                    nc.tensor.matmul(bank[4][:, 0:D], oT1[:], wo1[:], start=False, stop=True).then_inc(s_wo, 1)

                def attention_unit(l, u, par, first, more):
                    g = l * B + u
                    if more >= 1:
                        scores(g + 1, u + 1, False)
                    if not first:
                        pe.wait_ge(s_oTe, g)
                    if more >= 2:
                        pe.wait_ge(s_hT, g + 3)
                    for r in (0, 1):
                        probs_transposed(g, r)
                    if more >= 2:
                        pe.wait_ge(s_ve, g + 2)
                        project_kv(g + 2, par)
                    if not first:
                        if more >= 1:
                            pe.wait_ge(s_ve, g + 2)
                        project_o(g - 1)
                    outputs(g, 0, par)
                    for r in (2, 3):
                        probs_transposed(g, r)
                    if more >= 2:
                        if not first:
                            pe.wait_ge(s_xadd, g)
                        project_q(g + 2, par)
                    outputs(g, 2, par)
                    if more >= 3:
                        attn_x_transposed(g + 3, 1 - par)

                def ffn_x_transposed(w, par):
                    pe.wait_ge(f_xin, w + 1)
                    x_transposed(bank[0], par, f_T)

                def ffn_unit(l, u, par, first, last_unit, second=False):
                    w = l * B + u
                    if not last_unit:
                        pe.wait_ge(f_hT, w + 1)
                        ffn_x_transposed(w + 1, 1 - par)
                    pe.wait_ge(f_hT, w + 1)
                    for c in range(NF):
                        if c == 0 and not first:
                            pe.wait_ge(f_g, 2 * w - 1)
                        if c == 4 and not first:
                            pe.wait_ge(f_g, 2 * w)
                        out = bank[1 + c // 4][:, (c % 4) * S:(c % 4 + 1) * S]
                        for k, (a, b, rows) in enumerate(PASSES):
                            last = nc.tensor.matmul(out, w1[0:rows, a, c * P:(c + 1) * P], xT16[0:rows, par, b, :],
                                                    start=(k == 0), stop=(k == len(PASSES) - 1))
                        if c in (3, NF - 1):
                            last.then_inc(f_1, 1)
                    if not first:
                        ffn2(w - 1, 1 - par, second)

                def ffn2(w, par, first):
                    if not first:
                        pe.wait_ge(f_c, 2 * w - 1)
                    for c in range(NF):
                        if c in (0, 4):
                            pe.wait_ge(f_fl, 2 * w + 1 + c // 4)
                        for a, b in ((0, 0), (0, 1), (1, 0)):
                            last = nc.tensor.matmul(bank[3][:, 0:D], fT16[:, par, a, c * S:(c + 1) * S], w2[:, b, c, :],
                                                    start=(c + a + b == 0), stop=(c == NF - 1 and a == 1))
                    last.then_inc(f_2, 1)

                with pe.Fori(0, L) as l:
                    pe.wait_ge(f_h, B * l + B)
                    attn_x_transposed(l * B, 0)
                    pe.wait_ge(w_attn, 16 * N_WA * l + 16 * N_WA)
                    pe.wait_ge(a_low, l + 1)
                    project_kv(l * B, 0)
                    project_q(l * B, 0)
                    attn_x_transposed(l * B + 1, 1)
                    scores(l * B, 0, True)
                    pe.wait_ge(s_ve, l * B + 1)
                    project_kv(l * B + 1, 1)
                    project_q(l * B + 1, 1)
                    attn_x_transposed(l * B + 2, 0)
                    attention_unit(l, 0, 0, True, 3)
                    with pe.Fori(0, B // 2 - 2) as j:
                        attention_unit(l, 2 * j + 1, 1, False, 3)
                        attention_unit(l, 2 * j + 2, 0, False, 3)
                    for u in range(B - 3, B):
                        attention_unit(l, u, u % 2, False, B - 1 - u)
                    project_o(l * B + B - 1)
                    pe.wait_ge(s_h, B * l + B)
                    ffn_x_transposed(l * B, 0)
                    pe.wait_ge(f_low, 2 * l + 2)
                    ffn_unit(l, 0, 0, True, False)
                    ffn_unit(l, 1, 1, False, False, second=True)
                    with pe.Fori(1, B // 2 - 1) as j:
                        ffn_unit(l, 2 * j, 0, False, False)
                        ffn_unit(l, 2 * j + 1, 1, False, False)
                    ffn_unit(l, B - 2, 0, False, False)
                    ffn_unit(l, B - 1, 1, False, True)
                    ffn2(l * B + B - 1, 1, False)

            @block.scalar
            def _(act):
                def attn_weights_high(l):
                    act.wait_ge(w_attn, 16 * N_WA * l + 16 * N_WA)
                    nc.scalar.mul(w_qkv[:, 0], w_qkv_raw[:, 0], W_SCALE)
                    nc.scalar.mul(w_qkv[:, 2], w_qkv_raw[:, 1], W_SCALE)
                    nc.scalar.mul(w_qkv_high3[:], w_qkv_raw[:, 2], low_scale[:, 0:1]).then_inc(a_high, 1)

                def copy_xT(g, par, first):
                    act.wait_ge(s_hTp, g + 1)
                    if not first:
                        act.wait_ge(s_q, g - 1)
                        act.wait_ge(s_kv, g - 1)
                    nc.scalar.copy(xT16[:, par, 0:3, :].rearrange("p k s -> p (k s)"), bank[7][:, 0:3 * S])
                    nc.scalar.copy(xT16[0:D1, par, 3, :], bank[7][0:D1, 3 * S:4 * S]).then_inc(s_hT, 1)

                def high_k(g, first):
                    act.wait_ge(s_kv, g + 1)
                    if not first:
                        act.wait_ge(s_sc, 2 * g)
                    nc.scalar.mul(k16[:, 0].rearrange("p t s -> p (t s)"), bank[5][:, 0:3 * S], 1.0 / W_SCALE).then_inc(s_qkh, 1)

                def masked_q(g, first):
                    act.wait_ge(s_q, g + 1)
                    if not first:
                        act.wait_ge(s_qe, g)
                    nc.scalar.mul(q_masked[:].rearrange("p t s -> p (t s)"), bank[4][:, 0:3 * S], q_scale[:, 0:1]).then_inc(s_qkh, 1)

                def copy_oT(g, first, x_too):
                    act.wait_ge(s_pv, 2 * g + 2)
                    if x_too:
                        act.wait_ge(s_hTp, g + 4)
                    if not first:
                        act.wait_ge(s_wo, g)
                    nc.scalar.copy(oT0[:], bank[6][:, 3 * S:4 * S])
                    nc.scalar.copy(oT1[0:D1, :], bank[7][D1:P, 3 * S:4 * S]).then_inc(s_oTe, 1)

                def padding(g, r0, first):
                    act.wait_ge(s_max, 4 * g + r0 + 2)
                    if not first:
                        act.wait_ge(s_den, 4 * g - 3 + r0)
                    nc.scalar.activation(pad_exp[:, r0:r0 + 2], neg_max[:, r0:r0 + 2], ACT.Exp, bias=MASKED).then_inc(s_pad, 1)

                def probabilities(g, r, first):
                    if not first:
                        act.wait_ge(s_pTp, 4 * g - 3 + r)
                    for i in range(3):
                        last = nc.scalar.activation(probs[:, r, i, :], bank[r][:, i * S:(i + 1) * S], ACT.Exp,
                                                    bias=neg_max[:, r, i:i + 1], accum_out=sums[:, r, i:i + 1])
                    last.then_inc(s_exp, 1)

                def attention_unit(l, u, par, first, more):
                    g = l * B + u
                    if more >= 1:
                        for r in range(4):
                            if r % 2 == 0:
                                padding(g + 1, r, False)
                            if r == 2 and more >= 2:
                                high_k(g + 2, False)
                            if r == 3 and more >= 2:
                                masked_q(g + 2, False)
                            probabilities(g + 1, r, False)
                    copy_oT(g, first, more >= 3)
                    if more >= 3:
                        copy_xT(g + 3, 1 - par, False)

                def ffn_weights_high(l):
                    act.wait_ge(w_ffn, 16 * N_WF * l + 16 * N_WF)
                    nc.scalar.mul(w1[:, 0], w1_raw[:, 0], W_SCALE)
                    nc.scalar.mul(w1[:, 2], w1_raw[:, 1], W_SCALE)
                    nc.scalar.mul(w1_high3[:], w1_raw[:, 2], low_scale[:, 0:1]).then_inc(f_high, 1)
                    nc.scalar.mul(w2[:, 0], w2_raw[:], W_SCALE).then_inc(f_high, 1)

                def ffn_copy(w, par):
                    act.wait_ge(f_T, w + 1)
                    nc.scalar.copy(xT16[:, par, 0:3, :].rearrange("p k s -> p (k s)"), bank[0][:, 0:3 * S])
                    nc.scalar.copy(xT16[0:D1, par, 3, :], bank[0][0:D1, 3 * S:4 * S]).then_inc(f_hT, 1)

                def ffn_unit(l, u, par, first, last_unit, second=False):
                    w = l * B + u
                    if not last_unit:
                        if not first:
                            act.wait_ge(f_1, 2 * w)
                        ffn_copy(w + 1, 1 - par)
                    if not (first or second):
                        act.wait_ge(f_2, w - 1)
                    for k, (lo, hi) in enumerate(((0, 512), (512, NF * S))):
                        act.wait_ge(f_1, 2 * w + k + 1)
                        nc.scalar.activation(fT[:, par, lo:hi], bank[1 + k][:, 0:hi - lo], ACT.Gelu, scale=1.0 / W_SCALE).then_inc(f_g, 1)
                        act.wait_ge(f_g, 2 * w + k + 1)
                        nc.scalar.copy(fT16[:, par, 0, lo:hi], fT[:, par, lo:hi]).then_inc(f_fh, 1)

                with act.Fori(0, L) as l:
                    attn_weights_high(l)
                    copy_xT(l * B, 0, True)
                    high_k(l * B, True)
                    masked_q(l * B, True)
                    copy_xT(l * B + 1, 1, True)
                    for r in range(4):
                        if r % 2 == 0:
                            padding(l * B, r, True)
                        probabilities(l * B, r, True)
                    high_k(l * B + 1, False)
                    masked_q(l * B + 1, False)
                    copy_xT(l * B + 2, 0, False)
                    attention_unit(l, 0, 0, True, 3)
                    with act.Fori(0, B // 2 - 2) as j:
                        attention_unit(l, 2 * j + 1, 1, False, 3)
                        attention_unit(l, 2 * j + 2, 0, False, 3)
                    for u in range(B - 3, B):
                        attention_unit(l, u, u % 2, False, B - 1 - u)
                    ffn_weights_high(l)
                    ffn_copy(l * B, 0)
                    ffn_unit(l, 0, 0, True, False)
                    ffn_unit(l, 1, 1, False, False, second=True)
                    with act.Fori(1, B // 2 - 1) as j:
                        ffn_unit(l, 2 * j, 0, False, False)
                        ffn_unit(l, 2 * j + 1, 1, False, False)
                    ffn_unit(l, B - 2, 0, False, False)
                    ffn_unit(l, B - 1, 1, False, True)

            @block.vector
            def _(dve):
                def attn_weights_low(l):
                    dve.wait_ge(a_high, l + 1)
                    nc.vector.scalar_tensor_tensor(w_qkv[:, 1], w_qkv_raw[:, 0], W_SCALE, w_qkv[:, 0], ALU.mult, ALU.subtract)
                    nc.vector.scalar_tensor_tensor(w_qkv[:, 3], w_qkv_raw[:, 2], W_SCALE, w_qkv_high3[:], ALU.mult, ALU.subtract).then_inc(a_low, 1)

                def x_halves(n, u, buffer, done):
                    nc.vector.tensor_copy(x16[:, buffer, 0, :], H[:, u, :]).then_inc(x_high, 1)
                    dve.wait_ge(s_const, 1)
                    dve.wait_ge(x_high, n + 1)
                    nc.vector.tensor_tensor(x16[:, buffer, 1, :], H[:, u, :], x16[:, buffer, 0, :], ALU.subtract).then_inc(done, 1)

                def low_k(g):
                    dve.wait_ge(s_qkh, 2 * g + 1)
                    nc.vector.scalar_tensor_tensor(k16[:, 1].rearrange("p t s -> p (t s)"), bank[5][:, 0:3 * S], 1.0 / W_SCALE,
                                                   k16[:, 0].rearrange("p t s -> p (t s)"), ALU.mult, ALU.subtract).then_inc(s_ke, 1)

                def halves_q(g, first):
                    dve.wait_ge(s_qkh, 2 * g + 2)
                    if not first:
                        dve.wait_ge(s_sc, 2 * g)
                    nc.vector.scalar_tensor_tensor(q16[:].rearrange("p t s -> p (t s)"), bank[4][:, 0:3 * S], Q_SCALE,
                                                   q_masked[:].rearrange("p t s -> p (t s)"), ALU.mult, ALU.subtract).then_inc(s_qe, 1)

                def copy_v(g, par):
                    for b, pairs in ((bank[5], slice(0, 4)), (bank[4], slice(4, 6))):
                        n = pairs.stop - pairs.start
                        for odd in range(2):
                            last = nc.vector.tensor_scalar(v_sb[:, par, pairs, 2 * DH * odd:2 * DH * odd + DH],
                                                           b[:, 3 * S:3 * S + 2 * DH * n].rearrange("p (n b e) -> p n b e", b=2, e=DH)[:, :, odd, :],
                                                           1.0 / W_SCALE, None, ALU.mult)
                    last.then_inc(s_ve, 1)

                def residual(g, u, par, first):
                    dve.wait_ge(s_wo, g + 1)
                    if not first:
                        dve.wait_ge(s_h, g - 1)
                    nc.vector.tensor_tensor(xres[:, par, :], bank[4][:, 0:D], H[:, u, :], ALU.add).then_inc(s_xadd, 1)

                def residual_stats(g, par):
                    dve.wait_ge(s_xadd, g + 1)
                    nc.vector.bn_stats(stats[:], xres[:, par, :]).then_inc(s_st, 1)
                    dve.wait_ge(s_const, 1)
                    dve.wait_ge(s_st, g + 1)
                    nc.vector.bn_aggr(mv[:, par, :], stats[:]).then_inc(s_ag, 1)
                    dve.wait_ge(s_ag, g + 1)
                    nc.vector.tensor_scalar(var_eps[:, par:par + 1], mv[:, par, 1:2], EPS_TXT, None, ALU.add).then_inc(s_stat, 1)

                def negative_max(g, r, first):
                    dve.wait_ge(s_sc, 2 * g + r // 2 + 1)
                    if not first:
                        dve.wait_ge(s_exp, 4 * g - 3 + r)
                    nc.vector.tensor_reduce(neg_max[:, r, :], bank[r][:, 0:3 * S].rearrange("p (i s) -> p i s", i=3),
                                            AX.X, ALU.max, negate=True).then_inc(s_max, 1)

                def denominators(g, r0, first):
                    at = slice(r0, r0 + 2)
                    dve.wait_ge(s_exp, 4 * g + r0 + 2)
                    nc.vector.scalar_tensor_tensor(den[:, 0, at], pad_exp[:, at], float(N_PAD), sums[:, at], ALU.mult, ALU.add).then_inc(s_den, 1)
                    dve.wait_ge(s_den, 4 * g + r0 + 1)
                    if not first:
                        dve.wait_ge(s_norm, 4 * g - 2 + r0)
                    nc.vector.reciprocal(den[:, 1, at], den[:, 0, at]).then_inc(s_den, 1)

                def copy_pT(g, r, first):
                    dve.wait_ge(s_pTp, 4 * g + r + 1)
                    if not first or r >= 2:
                        dve.wait_ge(s_pv, 2 * g + r // 2)
                    nc.vector.tensor_copy(pT[:, r % 2, :], bank[6 + r % 2][:, 0:3 * S]).then_inc(s_pTe, 1)

                def attention_unit(l, u, par, first, more, few=False):
                    g = l * B + u
                    if more >= 1:
                        for r in (0, 1, 2):
                            negative_max(g + 1, r, False)
                    for r in (0, 1):
                        copy_pT(g, r, first)
                    if more >= 1:
                        negative_max(g + 1, 3, False)
                    if more >= 3:
                        dve.wait_ge(s_hTp, g + 2)
                        x_halves(2 * l * B + u + 3, u + 3, 1 - par, s_xin)
                    if not first:
                        residual(g - 1, u - 1, 1 - par, few)
                    for r in (2, 3):
                        copy_pT(g, r, first)
                    if more >= 2:
                        low_k(g + 2)
                    if more >= 1:
                        denominators(g + 1, 0, False)
                    if more >= 2:
                        halves_q(g + 2, False)
                    if not first:
                        residual_stats(g - 1, 1 - par)
                    if more >= 2:
                        dve.wait_ge(s_pv, 2 * g + 2)
                        copy_v(g + 2, par)
                    if more >= 1:
                        denominators(g + 1, 2, False)

                def ffn_weights_low(l):
                    dve.wait_ge(f_high, 2 * l + 1)
                    nc.vector.scalar_tensor_tensor(w1[:, 1], w1_raw[:, 0], W_SCALE, w1[:, 0], ALU.mult, ALU.subtract)
                    nc.vector.scalar_tensor_tensor(w1[:, 3], w1_raw[:, 2], W_SCALE, w1_high3[:], ALU.mult, ALU.subtract).then_inc(f_low, 1)
                    dve.wait_ge(f_high, 2 * l + 2)
                    nc.vector.scalar_tensor_tensor(w2[:, 1], w2_raw[:], W_SCALE, w2[:, 0], ALU.mult, ALU.subtract).then_inc(f_low, 1)

                def ffn_gelu_low(w, par):
                    for k, (lo, hi) in enumerate(((0, 512), (512, NF * S))):
                        dve.wait_ge(f_fh, 2 * w + k + 1)
                        nc.vector.tensor_tensor(fT16[:, par, 1, lo:hi], fT[:, par, lo:hi], fT16[:, par, 0, lo:hi], ALU.subtract).then_inc(f_fl, 1)

                def ffn_residual(w, u, par, few):
                    dve.wait_ge(f_2, w + 1)
                    if not few:
                        dve.wait_ge(f_h, B + w - 1)
                    nc.vector.scalar_tensor_tensor(xres[:, par, :], bank[3][:, 0:D], 1.0 / W_SCALE, H[:, u, :], ALU.mult, ALU.add).then_inc(f_c, 1)
                    dve.wait_ge(f_c, 2 * w + 1)
                    nc.vector.tensor_tensor(xres[:, par, :], xres[:, par, :], b2_rows[:], ALU.add).then_inc(f_c, 1)
                    dve.wait_ge(f_c, 2 * w + 2)
                    nc.vector.bn_stats(stats[:], xres[:, par, :]).then_inc(f_st, 1)
                    dve.wait_ge(s_const, 1)
                    dve.wait_ge(f_st, w + 1)
                    nc.vector.bn_aggr(mv[:, par, :], stats[:]).then_inc(f_ag, 1)
                    dve.wait_ge(f_ag, w + 1)
                    nc.vector.tensor_scalar(var_eps[:, par:par + 1], mv[:, par, 1:2], EPS_TXT, None, ALU.add).then_inc(f_stat, 1)

                with dve.Fori(0, L) as l:
                    attn_weights_low(l)
                    dve.wait_ge(f_h, B * l + B)
                    dve.wait_ge(w_attn, 16 * N_WA * l + 16 * N_WA)
                    x_halves(2 * l * B, 0, 0, s_xin)
                    x_halves(2 * l * B + 1, 1, 1, s_xin)
                    low_k(l * B)
                    halves_q(l * B, True)
                    copy_v(l * B, 0)
                    dve.wait_ge(s_hTp, B * l + 1)
                    x_halves(2 * l * B + 2, 2, 0, s_xin)
                    for r in range(4):
                        negative_max(l * B, r, True)
                    for r0 in (0, 2):
                        denominators(l * B, r0, True)
                    low_k(l * B + 1)
                    halves_q(l * B + 1, False)
                    copy_v(l * B + 1, 1)
                    attention_unit(l, 0, 0, True, 3)
                    attention_unit(l, 1, 1, False, 3, few=True)
                    attention_unit(l, 2, 0, False, 3, few=True)
                    attention_unit(l, 3, 1, False, 3)
                    with dve.Fori(2, B // 2 - 2) as j:
                        attention_unit(l, 2 * j, 0, False, 3)
                        attention_unit(l, 2 * j + 1, 1, False, 3)
                    for u in range(B - 4, B):
                        attention_unit(l, u, u % 2, False, min(3, B - 1 - u))
                    residual(l * B + B - 1, B - 1, 1, False)
                    residual_stats(l * B + B - 1, 1)
                    ffn_weights_low(l)
                    for u in range(4):
                        if u == 0:
                            dve.wait_ge(s_h, B * l + B)
                        if u >= 2:
                            dve.wait_ge(f_T, B * l + u - 1)
                        x_halves(2 * l * B + B + u, u, u % 2, f_xin)
                        if u == 2:
                            ffn_gelu_low(l * B, 0)
                    ffn_gelu_low(l * B + 1, 1)
                    ffn_residual(l * B, 0, 0, True)
                    with dve.Fori(0, B // 2 - 2) as j:
                        for c in range(2):
                            u = 2 * j + c + 1
                            dve.wait_ge(f_T, l * B + 2 * j + c + 3)
                            x_halves(2 * l * B + B + u + 3, u + 3, c, f_xin)
                            ffn_gelu_low(l * B + u + 1, c)
                            ffn_residual(l * B + u, u, 1 - c, False)
                    for u in range(B - 3, B):
                        if u + 1 < B:
                            ffn_gelu_low(l * B + u + 1, (u + 1) % 2)
                        ffn_residual(l * B + u, u, u % 2, False)

            @block.gpsimd
            def _(pool):
                def attention_norm(g, u, par):
                    pool.wait_ge(s_stat, g + 1)
                    norm_rows(pool, s_pc, 4 * g, xres[:, par, :], mv[:, par, 0:1], var_eps[:, par:par + 1],
                              ln1_s[:], ln1_b[:], H[:, u, :]).then_inc(s_h, 1)

                def ffn_norm(w, u, par):
                    pool.wait_ge(f_stat, w + 1)
                    norm_rows(pool, f_pc, 4 * w, xres[:, par, :], mv[:, par, 0:1], var_eps[:, par:par + 1], ln2_s[:], ln2_b[:], H[:, u, :]).then_inc(f_h, 1)

                def normalise(g):
                    for r in range(4):
                        pool.wait_ge(s_const, 1)
                        pool.wait_ge(s_den, 4 * g + 2 * (r // 2) + 2)
                        nc.gpsimd.tensor_tensor(probs[:, r], probs[:, r], den[:, 1, r].unsqueeze(2).to_broadcast([P, 3, S]),
                                                ALU.mult).then_inc(s_norm, 1)

                with pool.Fori(0, L) as l:
                    normalise(l * B)
                    normalise(l * B + 1)
                    with pool.Fori(1, B // 2) as j:
                        for par in range(2):
                            normalise(l * B + 2 * j + par)
                            attention_norm(l * B + 2 * j + par - 2, 2 * j + par - 2, par)
                    for u in range(B - 2, B):
                        attention_norm(l * B + u, u, u % 2)
                    with pool.Fori(0, B // 2) as j:
                        ffn_norm(l * B + 2 * j, 2 * j, 0)
                        ffn_norm(l * B + 2 * j + 1, 2 * j + 1, 1)


def text_layout(x):
    def with_bias(w, b):
        return np.concatenate([w, b[:, None, :]], axis=1)

    wq = with_bias(x["L0_txt_Wq"], x["L0_txt_bq"])
    wk = with_bias(x["L0_txt_Wk"], x["L0_txt_bk"])
    wv = with_bias(x["L0_txt_Wv"], x["L0_txt_bv"])
    wq_tiles = np.zeros((L, D + 1, 3 * P), np.float32)
    wk_tiles = np.zeros((L, D + 1, 3 * P), np.float32)
    for r in range(4):
        for i, h in enumerate(HEADS_OF_GROUP[r]):
            for a in (i * P + 32 * ROW_GROUP[r], i * P + 32 * ROW_GROUP[r] + DH):
                wq_tiles[:, :, a:a + DH] = wq[:, :, DH * h:DH * h + DH]
                wk_tiles[:, :, a:a + DH] = wk[:, :, DH * h:DH * h + DH]
    wo = with_bias(x["L0_txt_Wo"], x["L0_txt_bo"])
    return dict(
        ids=np.ascontiguousarray(x["x_txt"].T), mask=x["mask_BS_i1_0"].reshape(-1),
        q_scale=np.where(np.arange(P) % 32 < DH, 0.0, Q_SCALE).astype(np.float32)[:, None],
        emb=x["L0_txt_emb_word"], pos=x["L0_txt_emb_pos"][:S],
        emb_ln_s=x["L0_txt_emb_ln_s"], emb_ln_b=x["L0_txt_emb_ln_b"],
        wqkv=np.concatenate([wq_tiles, wk_tiles, wv], axis=2), wo=wo,
        w1=with_bias(x["L0_txt_W1"], x["L0_txt_b1"]), w2=x["L0_txt_W2"], b2=x["L0_txt_b2"],
        ln1_s=x["L0_txt_ln1_s"], ln1_b=x["L0_txt_ln1_b"], ln2_s=x["L0_txt_ln2_s"], ln2_b=x["L0_txt_ln2_b"],
    )


def patch_embedding(nc, io, sem, H, H_img, consts):
    ident, half = consts["ident"], consts["half"]
    NP, WF, CH = 6, 3 * 18 * 18, 108
    NCH = WF // CH
    PD = 16 * 16 * 15
    with ExitStack() as ctx:
        def sb(name, shape, dt=F32):
            return ctx.enter_context(nc.sbuf_tensor(name, shape, dt))

        rows = [P, 6 * B - P]
        xw = [sb(f"tok_x{i}", [P, 3, 18, 98]) for i in range(2)]
        w5 = sb("tok_w5", [CH, 5, NCH, D])
        g5 = sb("tok_g5", [CH, 5, NCH])
        b5 = sb("tok_b5", [CH, 5, NCH])
        w_eff = sb("tok_w_eff", [CH, NCH, D])
        mult = sb("tok_mult", [P, WF])
        ones = sb("tok_ones", [CH, P])
        b_row = sb("tok_b", [1, D])
        ids = sb("ids", [P, B], I32)
        ids_f = sb("ids_f", [P, 3, B])
        rows_of = sb("rows_of", [P, B], I32)
        const_rows = sb("tok_const", [P, D])
        xc = sb("tok_xc", [P, 2, WF])
        xm = sb("tok_xm", [P, 2, WF])
        junk = sb("tok_junk", [P, WF])
        xT = sb("tok_xT", [CH, 2, NCH, P])
        neg_mean = sb("tok_neg_mean", [P, 12])
        var = sb("tok_var", [P, 12])
        var_eps = sb("tok_var_eps", [P, 12])
        rstd = sb("tok_rstd", [P, 12])
        tok_out = sb("tok_out", [P, 2, NP, D])
        tb = [ctx.enter_context(nc.psum_tensor(f"tok_bank{i}", [P, 512], F32)) for i in range(6)]

        s_x, s_w, s_one = sem("tok_x_loaded"), sem("tok_w_loaded"), sem("tok_ones_set")
        s_gw, s_const = sem("tok_w_steps"), sem("tok_const_ready")
        s_ids, s_rows, s_gath = sem("txt_ids_loaded"), sem("txt_row_steps"), sem("txt_rows_gathered")
        s_cp = sem("tok_const_product")
        s_xc, s_xm, s_var, s_rs = sem("tok_centred"), sem("tok_weighted"), sem("tok_var"), sem("tok_rstd")
        s_vp = sem("tok_var_sum")
        s_T, s_xT, s_mm, s_out = sem("tok_T"), sem("tok_xT"), sem("tok_mm"), sem("tok_out")
        s_junk = sem("tok_junk")
        s_scr, s_back = sem("tok_scratch_written"), sem("tok_scratch_read")
        steps = [(t, w) for t in range(2) for w in range(NP)]

        def window(t, w):
            return xw[t][0:rows[t], :, :, 16 * w:16 * w + 18]

        def v3(ap):
            return ap.rearrange("p (c y x) -> p c y x", c=3, y=18)

        with nc.Block() as block:
            @block.sync
            def _(sp):
                sp.dma_start(ids[:], io["ids"]).then_inc(s_ids, 16)
                sp.dma_start(xw[0][:], io["tok_x"][0:P]).then_inc(s_x, 16)
                sp.dma_start(mult[:], io["tok_mult"].partition_broadcast(P)).then_inc(s_x, 16)
                sp.dma_start(xw[1][0:rows[1]], io["tok_x"][P:6 * B]).then_inc(s_x, 16)
                sp.dma_start(g5[:], io["tok_g5"]).then_inc(s_w, 16)
                sp.dma_start(b5[:], io["tok_b5"]).then_inc(s_w, 16)
                sp.dma_start(b_row[:], io["tok_b"]).then_inc(s_w, 16)
                sp.dma_start(w5[:], io["tok_w5"]).then_inc(s_w, 16)
                for t in range(2):
                    sp.wait_ge(s_out, NP * (t + 1))
                    sp.dma_start(io["scratch_tok"][t * P:t * P + rows[t]],
                                 tok_out[0:rows[t], t].rearrange("p w e -> p (w e)")).then_inc(s_scr, 16)
                sp.wait_ge(s_scr, 32)
                sp.dma_start(H_img[:], io["scratch_tok"].rearrange("(b h) n -> b (h n)", h=NP).rearrange(
                    "b (t e) -> t b e", e=D)).then_inc(s_back, 16)
                sp.wait_ge(s_gath, 16 * B)

            @block.vector
            def _(dve):
                nc.vector.memset(ones[:], 1.0).then_inc(s_one, 1)
                V = io["emb"].shape[0]
                dve.wait_ge(s_ids, 16)
                nc.vector.tensor_copy(ids_f[:, 0, :], ids[:]).then_inc(s_rows, 1)
                dve.wait_ge(s_rows, 1)
                nc.vector.tensor_scalar(ids_f[:, 1, :], ids_f[:, 0, :], 0.0, float(V), ALU.is_lt, ALU.mult).then_inc(s_rows, 1)
                dve.wait_ge(s_rows, 2)
                nc.vector.tensor_tensor(ids_f[:, 2, :], ids_f[:, 0, :], ids_f[:, 1, :], ALU.add).then_inc(s_rows, 1)
                dve.wait_ge(s_rows, 3)
                nc.vector.tensor_scalar(rows_of[:], ids_f[:, 2, :], 0.0, float(V - 1), ALU.max, ALU.min).then_inc(s_rows, 1)
                dve.wait_ge(s_x, 48)
                for k, (t, w) in enumerate(steps):
                    if k:
                        dve.wait_ge(s_junk, k)
                    nc.vector.tensor_tensor_reduce(v3(junk[0:rows[t]]), window(t, w), v3(mult[0:rows[t]]), -1.0 / PD, 0.0,
                                                   ALU.mult, ALU.add, neg_mean[0:rows[t], k:k + 1]).then_inc(s_junk, 1)
                dve.wait_ge(s_junk, 12)
                dve.wait_ge(s_w, 64)
                for s in range(5):
                    if s:
                        dve.wait_ge(s_gw, s)
                    for c in range(NCH):
                        if s == 0:
                            last = nc.vector.tensor_scalar(w_eff[:, c, :], w5[:, 0, c, :], g5[:, 0, c:c + 1], None, ALU.mult)
                        else:
                            last = nc.vector.scalar_tensor_tensor(w_eff[:, c, :], w5[:, s, c, :], g5[:, s, c:c + 1], w_eff[:, c, :], ALU.mult, ALU.add)
                    last.then_inc(s_gw, 1)
                dve.wait_ge(s_cp, 1)
                nc.vector.tensor_copy(const_rows[:], tb[5][:, 0:D]).then_inc(s_const, 1)
                for k in range(len(steps) + 1):
                    if k < len(steps):
                        r = rows[steps[k][0]]
                        dve.wait_ge(s_xm, k + 1)
                        if k:
                            dve.wait_ge(s_vp, k)
                        nc.vector.tensor_tensor_reduce(junk[0:r], xc[0:r, k % 2], xm[0:r, k % 2], 1.0 / PD, 0.0,
                                                       ALU.mult, ALU.add, var[0:r, k:k + 1]).then_inc(s_vp, 1)
                        dve.wait_ge(s_vp, k + 1)
                        nc.vector.tensor_scalar(var_eps[0:r, k:k + 1], var[0:r, k:k + 1], EPS, None, ALU.add).then_inc(s_var, 1)
                        if k >= 2:
                            dve.wait_ge(s_mm, k - 1)
                        for q in range(3):
                            c, n = 4 * q, min(4, NCH - 4 * q)
                            dve.wait_ge(s_T, 3 * k + q + 1)
                            nc.vector.tensor_copy(xT[:, k % 2, c:c + n, 0:r],
                                                  tb[q][0:CH, 0:n * P].rearrange("p (c n) -> p c n", c=n)[:, :, 0:r]).then_inc(s_xT, 1)
                    if k:
                        t, w = steps[k - 1]
                        r = rows[t]
                        dve.wait_ge(s_mm, k)
                        dve.wait_ge(s_rs, k)
                        dve.wait_ge(s_const, 1)
                        nc.vector.scalar_tensor_tensor(tok_out[0:r, t, w, :], tb[3 + (k - 1) % 2][0:r, 0:D], rstd[0:r, k - 1:k], const_rows[0:r],
                                                       ALU.mult, ALU.add).then_inc(s_out, 1)

            @block.scalar
            def _(act):
                for k, (t, w) in enumerate(steps):
                    act.wait_ge(s_junk, k + 1)
                    if k >= 2:
                        act.wait_ge(s_vp, k - 1)
                        act.wait_ge(s_T, 3 * k - 3)
                    nc.scalar.activation(v3(xc[0:rows[t], k % 2]), window(t, w), ACT.Identity,
                                         bias=neg_mean[0:rows[t], k:k + 1]).then_inc(s_xc, 1)

            def rstd_of(pool, k):
                r = rows[steps[k][0]]
                pool.wait_ge(s_var, k + 1)
                nc.gpsimd.tensor_tensor(rstd[0:r, k:k + 1], var_eps[0:r, k:k + 1], half[0:r], ALU.pow).then_inc(s_rs, 1)

            @block.gpsimd
            def _(pool):
                pool.wait_ge(s_rows, 4)
                for b in range(B):
                    nc.gpsimd.indirect_dma_start(
                        out=H[:, b, :], out_offset=None, in_=io["emb"],
                        in_offset=bass.IndirectOffsetOnAxis(ap=rows_of[:, b:b + 1], axis=0)).then_inc(s_gath, 16)
                for k, (t, w) in enumerate(steps):
                    r = rows[t]
                    pool.wait_ge(s_xc, k + 1)
                    if k >= 2:
                        pool.wait_ge(s_vp, k - 1)
                    nc.gpsimd.tensor_tensor(xm[0:r, k % 2], xc[0:r, k % 2], mult[0:r], ALU.mult).then_inc(s_xm, 1)
                    if k >= 1:
                        rstd_of(pool, k - 1)
                rstd_of(pool, 11)

            @block.tensor
            def _(pe):
                def transposed(k):
                    r = rows[steps[k][0]]
                    pe.wait_ge(s_xc, k + 1)
                    for c in range(NCH):
                        if c % 4 == 0 and k:
                            pe.wait_ge(s_xT, 3 * (k - 1) + c // 4 + 1)
                        last = nc.tensor.transpose(tb[c // 4][0:CH, (c % 4) * P:(c % 4) * P + r], xc[0:r, k % 2, c * CH:(c + 1) * CH], ident[0:r, 0:r])
                        if c in (3, 7, 8):
                            last.then_inc(s_T, 1)

                transposed(0)
                pe.wait_ge(s_w, 64)
                pe.wait_ge(s_one, 1)
                for i in range(5 * NCH):
                    nc.tensor.matmul(tb[5][:, 0:D], b5[:, i // NCH, i % NCH:i % NCH + 1].to_broadcast([CH, P]), w5[:, i // NCH, i % NCH, :],
                                     start=(i == 0), stop=False)
                nc.tensor.matmul(tb[5][:, 0:D], ones[0:1, :], b_row[:], start=False, stop=True).then_inc(s_cp, 1)
                for k, (t, w) in enumerate(steps):
                    if k + 1 < len(steps):
                        transposed(k + 1)
                    r = rows[t]
                    pe.wait_ge(s_gw, 5)
                    pe.wait_ge(s_xT, 3 * k + 3)
                    if k >= 2:
                        pe.wait_ge(s_out, k - 1)
                    for c in range(NCH):
                        last = nc.tensor.matmul(tb[3 + k % 2][0:r, 0:D], xT[:, k % 2, c, 0:r], w_eff[:, c, :], start=(c == 0), stop=(c == NCH - 1))
                    last.then_inc(s_mm, 1)
    return s_back


def tok_layout(x):
    xp = np.zeros((B, 3, 98, 98), np.float32)
    xp[:, :, 1:97, 1:97] = x["x"]
    tok_x = np.stack([xp[:, :, 16 * h:16 * h + 18, :] for h in range(6)], axis=1).reshape(6 * B, 3, 18, 98)
    shifts = [(1, 1), (1, 0), (1, 2), (0, 1), (2, 1)]

    def spread(a):
        n = a.shape[1]
        a = a.reshape(16, 16, 5, 3, n)
        out = np.zeros((5, 3, 18, 18, n), np.float32)
        for s, (dy, dx) in enumerate(shifts):
            out[s, :, dy:dy + 16, dx:dx + 16] = a[:, :, s].transpose(2, 0, 1, 3)
        return np.ascontiguousarray(out.reshape(5, 9, 108, n).transpose(2, 0, 1, 3))

    mult = np.zeros((3, 18, 18), np.float32)
    for dy, dx in shifts:
        mult[:, dy:dy + 16, dx:dx + 16] += 1
    return dict(tok_x=tok_x, tok_w5=spread(x["L0_tok_W"]), tok_g5=spread(x["L0_tok_gamma"][:, None])[..., 0],
                tok_b5=spread(x["L0_tok_beta"][:, None])[..., 0], tok_b=x["L0_tok_b"][None], tok_mult=mult.reshape(-1))


class Steps:

    def __init__(self, engine, semaphore, per, j):
        self.engine, self.semaphore, self.per, self.j, self.n = engine, semaphore, per, j, 0

    def done(self, instruction):
        self.n += 1
        instruction.then_inc(self.semaphore, 1)
        return self.n

    def wait(self, n=None):
        self.engine.wait_ge(self.semaphore, self.per * self.j + (self.n if n is None else n))


NPAIR = B // 2
W2T = 2 * T
W3T = 3 * T


def ssm_and_slots(nc, io, sem, H, H_img, consts):
    ident, half = consts["ident"], consts["half"]
    with ExitStack() as ctx:
        def sb(name, shape, dt=F32):
            return ctx.enter_context(nc.sbuf_tensor(name, shape, dt))

        wB, wC = (sb(n, [P, 4, NS * D], F16) for n in ("wB", "wC"))
        wi0, wi1 = sb("wi0", [P, 2 * D]), sb("wi1", [D1 + 1, 2 * D])
        wdt0, wdt1 = sb("wdt0", [P, D]), sb("wdt1", [D1 + 1, D])
        wso0, wso1 = sb("wso0", [P, D]), sb("wso1", [D1 + 1, D])
        a_neg = sb("a_neg", [P, 2, NS])
        wconv = sb("wconv", [P, 2, KC + 2])
        slots0, slots1 = sb("slots0", [P, SLOTS]), sb("slots1", [D1, SLOTS])
        xt0, xt1 = sb("xt0", [P, B, SLOTS]), sb("xt1", [D1 + 1, B, SLOTS])
        c16_all = sb("c16_all", [3 * SLOTS, NPAIR, W2T], F16)
        half4 = sb("half4", [P, 2, 4])
        pb = [ctx.enter_context(nc.psum_tensor(f"bank{i}", [P, 512], F32)) for i in range(8)]

        with ExitStack() as tmp:
            def t(name, shape):
                return tmp.enter_context(nc.sbuf_tensor(name, shape, F32))
            a_log = t("a_log", [P, 2, NS])
            raw0, raw1 = t("raw0", [P, SLOTS]), t("raw1", [D1, SLOTS])
            sq = t("sq", [P, 2, SLOTS])
            nrm = t("nrm", [P, 4, 2, NP_])
            scale = t("scale", [P, 1])
            CW = NS * D // 4
            NBUF = 3
            pieces = [(name, w, c) for name, w in (("wB", wB), ("wC", wC)) for c in range(0, NS * D, CW)]
            stage = t("stage", [P, NBUF, 3, CW])
            high = tmp.enter_context(nc.sbuf_tensor("high", [P, NBUF, CW], F16))
            low_scale = t("ssm_low_scale", [P, 1])
            z_st, z_h, z_l = sem("stage_zeroed"), sem("high_ready"), sem("low_ready")
            l_st = [sem(f"stage_loaded{i}") for i in range(NBUF)]
            l_w, l_s = sem("ssm_weights_loaded"), sem("slots_loaded")
            z_v, z_p, z_a, z_set = sem("setup_dve"), sem("setup_pool"), sem("setup_act"), sem("setup_zeroed")
            with nc.Block() as block:
                @block.sync
                def _(sp):
                    for dst, src in ((raw0[:], io["slot_params"][0:P]), (raw1[:], io["slot_params"][P:D]),
                                     (scale[:], io["slot_scale"].partition_broadcast(P)), (a_log[:], io["a_log"])):
                        sp.dma_start(dst, src).then_inc(l_s, 16)
                    sp.wait_ge(z_st, 1)
                    for i, (name, _, c) in enumerate(pieces):
                        if i >= NBUF:
                            sp.wait_ge(z_l, i - NBUF + 1)
                        w, st, k = io[name].rearrange("r n e -> r (n e)")[:, c:c + CW], stage[:, i % NBUF], l_st[i % NBUF]
                        for dst, src in ((st[:, 0], w[0:P]), (st[0:D1, 1], w[P:D]), (st[D1:P, 1], w[P:D]),
                                         (st[0:D1, 2], w[P:D]), (st[D1:D1 + 1, 2], w[D:D + 1]), (st[96:97, 2], w[D:D + 1])):
                            sp.dma_start(dst, src).then_inc(k, 16)
                    for dst, src in ((wconv[:], io["wconv"]), (wi0[:], io["wi"][0:P]), (wi1[:], io["wi"][P:D + 1]),
                                     (wdt0[:], io["wdt"][0:P]), (wdt1[:], io["wdt"][P:D + 1]),
                                     (wso0[:], io["wso"][0:P]), (wso1[:], io["wso"][P:D + 1])):
                        sp.dma_start(dst, src).then_inc(l_w, 16)
                    sp.wait_ge(l_w, 16 * 7)

                @block.scalar
                def _(act):
                    act.wait_ge(l_s, 64)
                    nc.scalar.activation(a_neg[:], a_log[:], ACT.Exp).then_inc(z_a, 1)
                    for i, (_, w, c) in enumerate(pieces):
                        act.wait_ge(z_st, 1)
                        act.wait_ge(l_st[i % NBUF], 96 * (i // NBUF + 1))
                        if i >= NBUF:
                            act.wait_ge(z_l, i - NBUF + 1)
                        nc.scalar.mul(w[:, 0, c:c + CW], stage[:, i % NBUF, 0], W_SCALE)
                        nc.scalar.mul(high[:, i % NBUF], stage[:, i % NBUF, 2], low_scale[:, 0:1]).then_inc(z_h, 1)

                @block.vector
                def _(dve):
                    nc.vector.memset(half4[:, 0, :], -0.5)
                    nc.vector.memset(half4[:, 1, :], 0.5)
                    nc.vector.memset(xt1[:], 1.0)
                    nc.vector.memset(low_scale[:D1], W_SCALE)
                    nc.vector.memset(low_scale[D1:96], 0.0)
                    nc.vector.memset(low_scale[96:], W_SCALE)
                    nc.vector.memset(stage[:, :, 2], 0.0).then_inc(z_st, 1)
                    nc.vector.memset(sq[:], 0.0).then_inc(z_set, 1)
                    dve.wait_ge(z_set, 1)
                    dve.wait_ge(l_s, 64)
                    for c, (raw, r) in enumerate(((raw0, P), (raw1, D1))):
                        nc.vector.tensor_tensor(sq[0:r, c], raw[:], raw[:], ALU.mult).then_inc(z_v, 1)
                    dve.wait_ge(z_v, 2)
                    nc.vector.tensor_reduce(nrm[:, 0], sq[:].rearrange("p c (n q) -> p c q n", n=NE), AX.X, ALU.add).then_inc(z_v, 1)
                    dve.wait_ge(z_a, 1)
                    nc.vector.tensor_scalar(a_neg[:], a_neg[:], -1.0, None, ALU.mult)
                    dve.wait_ge(z_p, 1)
                    nc.vector.tensor_scalar(nrm[:, 2], nrm[:, 1], 1e-6, None, ALU.add).then_inc(z_v, 1)
                    dve.wait_ge(z_v, 4)
                    nc.vector.reciprocal(nrm[:, 3], nrm[:, 2]).then_inc(z_v, 1)
                    dve.wait_ge(z_v, 5)
                    for c, (raw, slots, r) in enumerate(((raw0, slots0, P), (raw1, slots1, D1))):
                        nc.vector.scalar_tensor_tensor(slots[:].rearrange("p (n q) -> p n q", n=NE), raw[:].rearrange("p (n q) -> p n q", n=NE),
                                                       scale[0:r, 0:1], nrm[0:r, 3, c].unsqueeze(1).to_broadcast([r, NE, NP_]), ALU.mult, ALU.mult)
                    for i, (_, w, c) in enumerate(pieces):
                        dve.wait_ge(l_st[i % NBUF], 96 * (i // NBUF + 1))
                        nc.vector.tensor_scalar(w[:, 2, c:c + CW], stage[:, i % NBUF, 1], W_SCALE, None, ALU.mult)
                        dve.wait_ge(z_h, i + 1)
                        nc.vector.scalar_tensor_tensor(w[:, 1, c:c + CW], stage[:, i % NBUF, 0], W_SCALE, w[:, 0, c:c + CW], ALU.mult, ALU.subtract)
                        nc.vector.scalar_tensor_tensor(w[:, 3, c:c + CW], stage[:, i % NBUF, 2], W_SCALE, high[:, i % NBUF],
                                                       ALU.mult, ALU.subtract).then_inc(z_l, 1)

                @block.gpsimd
                def _(pool):
                    pool.wait_ge(z_v, 3)
                    nc.gpsimd.tensor_tensor(nrm[:, 1], nrm[:, 0], half4[:, 1, 0:1].unsqueeze(2).to_broadcast([P, 2, NP_]), ALU.pow).then_inc(z_p, 1)

        with ExitStack() as tmp:
            def t(name, shape):
                return tmp.enter_context(nc.sbuf_tensor(name, shape, F32))
            st4 = t("st4", [P, 4, 6])
            mv_f, ve_f, rs_f = t("mv_f", [P, 4, 2]), t("ve_f", [P, 4]), t("rs_f", [P, 4])
            xn_t, xn_i = t("xn_t", [P, 2, D]), t("xn_i", [N_IMG, 2, D])
            xT0, xT1 = t("xT0", [P, W2T]), t("xT1", [D1 + 1, W2T])
            u_pad = t("u_pad", [P, 3, KC - 1 + T])
            conv = t("conv", [P, 2, 3, T])
            uc_n, uc1_n = t("uc_n", [P, 3, T]), t("uc1_n", [D1 + 1, W2T])
            ev_n = t("ev_n", [P, W3T])
            sp_a, sp_e, sp_l = t("sp_a", [P, W3T]), t("sp_e", [P, W3T]), t("sp_l", [P, W3T])
            dt_n = t("dt_n", [P, W3T])
            y0 = t("y0", [P, 3, T])
            u16, u16_n = (tmp.enter_context(nc.sbuf_tensor(n, [P, 4, W2T], F16)) for n in ("u16", "u16_n"))
            dt, dtu = t("dt", [P, 3, T]), t("dtu", [P, W3T])
            sg = t("sg", [P, 2, W3T])
            decay = t("decay", [P, 2, 3, T])
            inp = t("inp", [P, 2, W3T])
            state = t("state", [P, 2, W3T])
            cstate = t("cstate", [P, 2, W3T])
            y = t("y", [P, 2, W3T])
            yg, yg1 = t("yg", [P, W3T]), t("yg1", [D1 + 1, W2T])
            mv_b, sm = t("mv_b", [P, 4, 2]), t("sm", [P, 8, 4])
            zn_t, zn_i = t("zn_t", [P, 2, D]), t("zn_i", [N_IMG, 2, D])
            zT0, zT1 = t("zT0", [P, W2T]), t("zT1", [D1, W2T])
            cmax, cexp = t("cmax", [P, 3, 4]), t("cexp", [P, 3, 4, SLOTS])
            dmax, dexp = t("dmax", [SLOTS, 3, 2]), t("dexp", [SLOTS, 2, W2T])
            d_tok = t("d_tok", [P, 4, SLOTS])

            names = ("bn bn0 var rs xn T xT U V up v conv uc1 hi lo D l dt y0").split()
            F = {n: sem("front_" + n) for n in names}
            fd, fa = sem("front_dve_steps"), sem("front_act_steps")
            s_uc, s_dt, s_dtu, s_sg = sem("uc_ready"), sem("dt_ready"), sem("dtu_ready"), sem("sigmoid_ready")
            s_B, s_C, s_a, s_in, s_scan, s_cs, s_acc = (sem(n) for n in ("B_done", "C_done", "decay_ready", "input_ready", "scan_done", "cstate_ready", "y_added"))
            names = ("yg yg1 op h2 bn var pw zn T zT L mx e cd T3 ct cl dT x xt").split()
            K = {n: sem("back_" + n) for n in names}
            bd = sem("back_dve_steps")
            s_set = sem("scan_constants")
            FD, BD = 8, 10

            def v3(ap):
                return ap.rearrange("p (a t) -> p a t", a=3)

            with nc.Block() as block:
                @block.tensor
                def _(pe):
                    def mixed(bank, w0, w1, c0, x0, x1, done):
                        nc.tensor.matmul(bank[:, 0:W2T], w0[:, c0:c0 + P], x0, start=True, stop=False)
                        nc.tensor.matmul(bank[:, 0:W2T], w1[:, c0:c0 + P], x1, start=False, stop=True)
                        for k, (w, x) in enumerate(((w0, x0), (w1, x1))):
                            for s in range(2):
                                last = nc.tensor.matmul(bank[D1 * s:D1 * s + D1, W2T:W3T], w[:, c0 + P:c0 + D], x[:, s * T:(s + 1) * T],
                                                        start=(k == 0), stop=(k == 1))
                        last.then_inc(done, 1)

                    def mixed_halves(bank, w, n, done):
                        passes = ((0, 0, P), (1, 0, P), (0, 1, P), (2, 2, P), (3, 3, 97))
                        for k, (a, b, r) in enumerate(passes):
                            nc.tensor.matmul(bank[:, 0:W2T], w[0:r, a, n * D:n * D + P], u16[0:r, b, :], start=(k == 0), stop=(k == 4))
                        for k, (a, b, r) in enumerate(passes):
                            for s in range(2):
                                last = nc.tensor.matmul(bank[D1 * s:D1 * s + D1, W2T:W3T], w[0:r, a, n * D + P:(n + 1) * D],
                                                        u16[0:r, b, s * T:(s + 1) * T], start=(k == 0), stop=(k == 4))
                        last.then_inc(done, 1)

                    def to_channels(b0, b1, z_t, z_i, done):
                        for s in range(2):
                            c = s * T
                            nc.tensor.transpose(b0[:, c + N_IMG:c + T], z_t[:, s, 0:P], ident[:])
                            nc.tensor.transpose(b0[:, c:c + N_IMG], z_i[:, s, 0:P], ident[0:N_IMG, 0:N_IMG])
                            nc.tensor.transpose(b1[0:D1, c:c + N_IMG], z_i[:, s, P:D], ident[0:N_IMG, 0:N_IMG])
                            last = nc.tensor.transpose(b1[0:D1, c + N_IMG:c + T], z_t[:, s, P:D], ident[:])
                        last.then_inc(done, 1)

                    def front_T(j):
                        pe.wait_ge(F["xn"], j + 1)
                        pe.wait_ge(F["dt"], j)
                        pe.wait_ge(F["v"], j)
                        to_channels(pb[6], pb[7], xn_t, xn_i, F["T"])

                    def front_uv(j):
                        pe.wait_ge(F["xT"], j + 1)
                        mixed(pb[6], wi0, wi1, 0, xT0[:], xT1[:], F["U"])
                        mixed(pb[7], wi0, wi1, D, xT0[:], xT1[:], F["V"])

                    def front_dt(j):
                        pe.wait_ge(F["uc1"], j + 1)
                        pe.wait_ge(F["up"], j + 1)
                        mixed(pb[6], wdt0, wdt1, 0, uc_n[:].rearrange("p a t -> p (a t)")[:, 0:W2T], uc1_n[:], F["D"])

                    def back_op(j):
                        pe.wait_ge(K["yg1"], j + 1)
                        pe.wait_ge(K["xt"], j)
                        pe.wait_ge(K["dT"], j)
                        for s in range(2):
                            c = s * T
                            nc.tensor.matmul(pb[4][:, s * D:(s + 1) * D], yg[:, c + N_IMG:c + T], wso0[:], start=True, stop=False)
                            nc.tensor.matmul(pb[4][:, s * D:(s + 1) * D], yg1[:, c + N_IMG:c + T], wso1[:], start=False, stop=True)
                            nc.tensor.matmul(pb[5][0:N_IMG, s * D:(s + 1) * D], yg[:, c:c + N_IMG], wso0[:], start=True, stop=False)
                            last = nc.tensor.matmul(pb[5][0:N_IMG, s * D:(s + 1) * D], yg1[:, c:c + N_IMG], wso1[:], start=False, stop=True)
                        last.then_inc(K["op"], 1)

                    def back_T(j):
                        pe.wait_ge(K["zn"], j + 1)
                        to_channels(pb[4], pb[5], zn_t, zn_i, K["T"])

                    def back_logits(j):
                        pe.wait_ge(K["zT"], j + 1)
                        for i in range(4):
                            s, c = i % 2, (i % 2) * T + (N_IMG if i < 2 else 0)
                            out = pb[4][:, i * SLOTS:(i + 1) * SLOTS]
                            nc.tensor.matmul(out, zT0[:, c:c + P], slots0[:], start=True, stop=False)
                            nc.tensor.matmul(out, zT1[:, c:c + P], slots1[:], start=False, stop=True)
                        nc.tensor.matmul(pb[5][0:SLOTS, 0:W2T], slots0[:], zT0[:], start=True, stop=False)
                        nc.tensor.matmul(pb[5][0:SLOTS, 0:W2T], slots1[:], zT1[:], start=False, stop=True).then_inc(K["L"], 1)

                    def back_T3(j):
                        pe.wait_ge(K["cd"], j + 1)
                        for i in range(4):
                            s, c = i % 2, (i % 2) * T + (N_IMG if i < 2 else 0)
                            r = P if i < 2 else N_IMG
                            nc.tensor.transpose(pb[4][0:SLOTS, c:c + r], cexp[0:r, 2, i, :], ident[0:r, 0:r])
                            last = nc.tensor.transpose(pb[5][:, i * SLOTS:(i + 1) * SLOTS], dexp[:, 1, c:c + P], ident[0:SLOTS, 0:SLOTS])
                        last.then_inc(K["T3"], 1)

                    def back_x(j):
                        pe.wait_ge(K["cl"], j + 1)
                        pe.wait_ge(K["dT"], j + 1)
                        for s in range(2):
                            for m, (lo, hi) in enumerate(((0, P), (P, D))):
                                out = pb[4][0:hi - lo, m * 2 * SLOTS + s * SLOTS:m * 2 * SLOTS + (s + 1) * SLOTS]
                                nc.tensor.matmul(out, zn_t[:, s, lo:hi], d_tok[:, s, :], start=True, stop=False)
                                last = nc.tensor.matmul(out, zn_i[:, s, lo:hi], d_tok[0:N_IMG, 2 + s, :], start=False, stop=True)
                        last.then_inc(K["x"], 1)

                    def scan_steps(j, first, last_pair):
                        pe.wait_ge(s_uc, j + 1)
                        back = {3: back_op, 7: back_T, 9: back_logits, 14: back_T3}
                        front = {4: front_T, 6: front_uv, 10: front_dt}
                        for n in range(NS):
                            m = NS * j + n
                            if n in back and not first:
                                back[n](j - 1)
                            if n in front and not last_pair:
                                front[n](j + 1)
                            if n >= 2 or not first:
                                pe.wait_ge(s_in, m - 1)
                            mixed_halves(pb[n % 2], wB, n, s_B)
                            if n >= 2 or not first:
                                pe.wait_ge(s_cs, m - 1)
                            mixed_halves(pb[2 + n % 2], wC, n, s_C)
                        if not first:
                            back_x(j - 1)

                    front_T(0)
                    front_uv(0)
                    front_dt(0)
                    scan_steps(0, True, False)
                    scan_steps(1, False, False)
                    with pe.Fori(2, NPAIR - 1) as j:
                        scan_steps(j, False, False)
                    scan_steps(NPAIR - 1, False, True)
                    for piece in (back_op, back_T, back_logits, back_T3, back_x):
                        piece(NPAIR - 1)

                @block.scalar
                def _(act):
                    def front_xT(j):
                        act.wait_ge(F["T"], j + 1)
                        act.wait_ge(F["V"], j)
                        nc.scalar.copy(xT0[:], pb[6][:, 0:W2T])
                        nc.scalar.copy(xT1[0:D1, :], pb[7][0:D1, 0:W2T]).then_inc(F["xT"], 1)

                    def front_up(j):
                        act.wait_ge(F["U"], j + 1)
                        act.wait_ge(F["conv"], j)
                        nc.scalar.copy(u_pad[:, :, KC - 1:], v3(pb[6][:, 0:W3T])).then_inc(F["up"], 1)
                        act.wait_ge(F["V"], j + 1)
                        act.wait_ge(s_sg, 2 * j)
                        nc.scalar.activation(ev_n[:], pb[7][:, 0:W3T], ACT.Exp, scale=-1.0).then_inc(F["v"], 1)

                    def front_uc1(j):
                        act.wait_ge(F["conv"], j + 1)
                        act.wait_ge(F["D"], j)
                        nc.scalar.copy(uc1_n[0:D1, 0:T], uc_n[0:D1, 2, :])
                        nc.scalar.copy(uc1_n[0:D1, T:W2T], uc_n[D1:P, 2, :]).then_inc(F["uc1"], 1)
                        act.wait_ge(F["uc1"], j + 1)
                        act.wait_ge(s_uc, j)
                        nc.scalar.copy(u16_n[:, 0, :], uc_n[:, 0:2, :].rearrange("p a t -> p (a t)"))
                        nc.scalar.copy(u16_n[0:D1, 2, :], uc1_n[0:D1, :])
                        nc.scalar.copy(u16_n[0:D1, 3, :], uc1_n[0:D1, :]).then_inc(F["hi"], 1)

                    def front_softplus(j):
                        act.wait_ge(F["D"], j + 1)
                        act.wait_ge(F["dt"], j)
                        nc.scalar.activation(sp_a[:], pb[6][:, 0:W3T], ACT.Abs).then_inc(fa, 1)
                        act.wait_ge(fa, 2 * j + 1)
                        nc.scalar.activation(sp_e[:], sp_a[:], ACT.Exp, scale=-1.0).then_inc(fa, 1)
                        act.wait_ge(fa, 2 * j + 2)
                        nc.scalar.activation(sp_l[:], sp_e[:], ACT.Ln, bias=1.0).then_inc(F["l"], 1)

                    def back_yg1(j):
                        act.wait_ge(K["yg"], j + 1)
                        act.wait_ge(K["op"], j)
                        nc.scalar.copy(yg1[0:D1, 0:T], yg[0:D1, W2T:W3T])
                        nc.scalar.copy(yg1[0:D1, T:W2T], yg[D1:P, W2T:W3T]).then_inc(K["yg1"], 1)

                    def back_zT(j):
                        act.wait_ge(K["T"], j + 1)
                        nc.scalar.copy(zT0[:], pb[4][:, 0:W2T])
                        nc.scalar.copy(zT1[:], pb[5][0:D1, 0:W2T]).then_inc(K["zT"], 1)

                    def back_exp(j):
                        act.wait_ge(K["mx"], j + 1)
                        nc.scalar.activation(cexp[:, 1], cexp[:, 0], ACT.Exp)
                        for s in range(2):
                            last = nc.scalar.activation(dexp[:, 0, s * T:(s + 1) * T], pb[5][0:SLOTS, s * T:(s + 1) * T], ACT.Exp,
                                                        bias=dmax[:, 0, s:s + 1])
                        last.then_inc(K["e"], 1)

                    def back_ct(j):
                        act.wait_ge(K["T3"], j + 1)
                        for part in range(2):
                            last = nc.scalar.copy(c16_all[part * SLOTS:(part + 1) * SLOTS, bass.ds(j, 1), :], pb[4][0:SLOTS, 0:W2T].unsqueeze(1))
                        last.then_inc(K["ct"], 1)

                    def back_xt(j):
                        act.wait_ge(K["x"], j + 1)
                        nc.scalar.copy(xt0[:, bass.ds(2 * j, 2), :], pb[4][:, 0:2 * SLOTS].rearrange("p (s k) -> p s k", s=2))
                        nc.scalar.copy(xt1[0:D1, bass.ds(2 * j, 2), :],
                                       pb[4][0:D1, 2 * SLOTS:4 * SLOTS].rearrange("p (s k) -> p s k", s=2)).then_inc(K["xt"], 1)

                    def scan_steps(j, first, last_pair):
                        act.wait_ge(s_dt, j + 1)
                        back = {2: back_yg1, 8: back_zT, 11: back_exp, 14: back_ct}
                        front = {5: front_xT, 7: front_up, 9: front_uc1, 10: front_softplus}
                        for n in range(NS):
                            m = NS * j + n
                            if n >= 2 or not first:
                                act.wait_ge(s_scan, m - 1)
                            nc.scalar.activation(decay[:, n % 2, 0:2, 1:], dt[:, 0:2, 1:], ACT.Exp, scale=a_neg[:, 0, n:n + 1])
                            nc.scalar.activation(decay[:, n % 2, 2, 1:], dt[:, 2, 1:], ACT.Exp, scale=a_neg[:, 1, n:n + 1]).then_inc(s_a, 1)
                            if n in back and not first:
                                back[n](j - 1)
                            if n in front and not last_pair:
                                front[n](j + 1)
                        if not first:
                            back_xt(j - 1)

                    act.wait_ge(s_set, 1)
                    for piece in (front_xT, front_up, front_uc1, front_softplus):
                        piece(0)
                    scan_steps(0, True, False)
                    scan_steps(1, False, False)
                    with act.Fori(2, NPAIR - 1) as j:
                        scan_steps(j, False, False)
                    scan_steps(NPAIR - 1, False, True)
                    for piece in (back_yg1, back_zT, back_exp, back_ct, back_xt):
                        piece(NPAIR - 1)

                @block.vector
                def _(dve):
                    def rows_of(i, j, arrays):
                        return arrays[i // 2][:, 2 * j + i % 2, :], (P if i < 2 else N_IMG)

                    def statistics(j, bn, count, mv):
                        for i in range(4):
                            x, r = rows_of(i, j, (H, H_img))
                            last = nc.vector.bn_stats(st4[0:r, i, :], x)
                        last.then_inc(bn, 1)
                        dve.wait_ge(s_set, 1)
                        dve.wait_ge(bn, count)
                        for i in range(4):
                            r = P if i < 2 else N_IMG
                            last = nc.vector.bn_aggr(mv[0:r, i, :], st4[0:r, i, :])
                        return last

                    def normalise(j, mv, factor, z_t, z_i):
                        for i in range(4):
                            x, r = rows_of(i, j, (H, H_img))
                            z = (z_t, z_i)[i // 2][:, i % 2, :]
                            last = nc.vector.tensor_scalar(z, x, mv[0:r, i, 0:1], factor[0:r, i:i + 1], ALU.subtract, ALU.mult)
                        return last

                    def front_norm_a(j):
                        st = Steps(dve, fd, FD, j)
                        at_start = isinstance(j, int) and j == 0
                        st.done(statistics(j, F["bn0"] if at_start else F["bn"], 1 if at_start else j, mv_f))
                        st.wait()
                        nc.vector.tensor_scalar(ve_f[:], mv_f[:, :, 1], EPS, None, ALU.add).then_inc(F["var"], 1)

                    def front_norm_b(j):
                        dve.wait_ge(F["rs"], j + 1)
                        dve.wait_ge(F["T"], j)
                        normalise(j, mv_f, rs_f, xn_t, xn_i).then_inc(F["xn"], 1)

                    def front_conv(j):
                        st = Steps(dve, fd, FD, j)
                        st.n = 1
                        dve.wait_ge(F["up"], j + 1)
                        dve.wait_ge(F["hi"], j)
                        dve.wait_ge(F["D"], j)
                        parts = ((slice(0, 2), 0), (slice(2, 3), 1))
                        for k in range(KC):
                            for seg, w in parts:
                                x = u_pad[:, seg, k:k + T]
                                out = uc_n[:, seg] if k == KC - 1 else conv[:, k % 2, seg]
                                if k == 0:
                                    st.done(nc.vector.tensor_scalar(out, x, wconv[:, w, 0:1], wconv[:, w, KC:KC + 1], ALU.mult, ALU.add))
                                else:
                                    st.wait(st.n - 1)
                                    last = nc.vector.scalar_tensor_tensor(out, x, wconv[:, w, k:k + 1], conv[:, (k - 1) % 2, seg],
                                                                          ALU.mult, ALU.add)
                                    if (k, w) == (KC - 1, 1):
                                        last.then_inc(F["conv"], 1)
                                    else:
                                        st.done(last)
                        dve.wait_ge(F["conv"], j + 1)
                        if not (isinstance(j, int) and j == 0):
                            dve.wait_ge(s_acc, NS * j - NS + 1)
                        for seg, w in parts:
                            last = nc.vector.tensor_scalar(y0[:, seg], uc_n[:, seg], wconv[:, w, KC + 1:KC + 2], W_SCALE, ALU.mult, ALU.mult)
                        last.then_inc(F["y0"], 1)

                    def front_dt(j):
                        dve.wait_ge(F["l"], j + 1)
                        nc.vector.scalar_tensor_tensor(dt_n[:], pb[6][:, 0:W3T], 0.0, sp_l[:], ALU.max, ALU.add).then_inc(F["dt"], 1)

                    def front_low(j):
                        dve.wait_ge(F["hi"], j + 1)
                        dve.wait_ge(F["D"], j + 1)
                        nc.vector.tensor_tensor(u16_n[:, 1, :], uc_n[:, 0:2, :].rearrange("p a t -> p (a t)"), u16_n[:, 0, :], ALU.subtract)
                        nc.vector.tensor_tensor(u16_n[D1:P, 2, :], uc1_n[0:D1, :], u16_n[0:D1, 3, :], ALU.subtract).then_inc(F["lo"], 1)

                    def take_dt(j):
                        dve.wait_ge(F["lo"], j + 1)
                        dve.wait_ge(s_C, NS * j)
                        nc.vector.tensor_copy(u16[:].rearrange("p a t -> p (a t)"), u16_n[:].rearrange("p a t -> p (a t)")).then_inc(s_uc, 1)
                        dve.wait_ge(F["dt"], j + 1)
                        dve.wait_ge(F["y0"], j + 1)
                        dve.wait_ge(s_a, NS * j)
                        nc.vector.tensor_copy(dt[:].rearrange("p a t -> p (a t)"), dt_n[:]).then_inc(s_dt, 1)
                        nc.vector.scalar_tensor_tensor(dtu[:], dt_n[:], 1.0 / W_SCALE, uc_n[:].rearrange("p a t -> p (a t)"),
                                                       ALU.mult, ALU.mult).then_inc(s_dtu, 1)

                    def gate(j):
                        dve.wait_ge(F["v"], j + 1)
                        nc.vector.tensor_scalar(sg[:, 0, :], ev_n[:], 1.0, W_SCALE, ALU.add, ALU.mult).then_inc(s_sg, 1)
                        dve.wait_ge(s_sg, 2 * j + 1)
                        nc.vector.reciprocal(sg[:, 1, :], sg[:, 0, :]).then_inc(s_sg, 1)

                    def back_yg(j):
                        dve.wait_ge(s_acc, NS * j + NS)
                        dve.wait_ge(s_sg, 2 * j + 2)
                        dve.wait_ge(K["op"], j)
                        nc.vector.tensor_tensor(yg[:], y[:, 1, :], sg[:, 1, :], ALU.mult).then_inc(K["yg"], 1)

                    def back_residual(j):
                        st = Steps(dve, bd, BD, j)
                        dve.wait_ge(K["op"], j + 1)
                        for i in range(4):
                            x, r = rows_of(i, j, (H, H_img))
                            last = nc.vector.tensor_tensor(x, pb[4 + i // 2][0:r, (i % 2) * D:(i % 2 + 1) * D], x, ALU.add)
                        last.then_inc(K["h2"], 1)
                        dve.wait_ge(s_set, 1)
                        dve.wait_ge(K["h2"], j + 1)
                        st.done(statistics(j, K["bn"], j + 1, mv_b))
                        st.wait()
                        nc.vector.tensor_scalar(sm[:, 0, :], mv_b[:, :, 1], EPS, None, ALU.add)
                        nc.vector.tensor_scalar(sm[:, 1, :], mv_b[:, :, 1], float(D), None, ALU.mult).then_inc(K["var"], 1)

                    def back_norm(j):
                        st = Steps(dve, bd, BD, j)
                        st.n = 1
                        dve.wait_ge(K["pw"], j + 1)
                        st.done(nc.vector.tensor_tensor(sm[:, 4, :], sm[:, 2, :], sm[:, 3, :], ALU.mult))
                        st.wait()
                        st.done(nc.vector.tensor_scalar(sm[:, 5, :], sm[:, 4, :], 1e-6, None, ALU.add))
                        st.wait()
                        st.done(nc.vector.reciprocal(sm[:, 6, :], sm[:, 5, :]))
                        st.wait()
                        st.done(nc.vector.tensor_tensor(sm[:, 7, :], sm[:, 6, :], sm[:, 2, :], ALU.mult))
                        st.wait()
                        dve.wait_ge(K["x"], j)
                        normalise(j, mv_b, sm[:, 7, :], zn_t, zn_i).then_inc(K["zn"], 1)

                    def back_max(j):
                        st = Steps(dve, bd, BD, j)
                        st.n = 5
                        dve.wait_ge(K["L"], j + 1)
                        logits = pb[4][:, 0:4 * SLOTS].rearrange("p (i k) -> p i k", i=4)
                        st.done(nc.vector.tensor_reduce(cmax[:, 0, :], logits, AX.X, ALU.max))
                        nc.vector.tensor_reduce(dmax[:, 0, :], pb[5][0:SLOTS, 0:W2T].rearrange("p (s t) -> p s t", s=2), AX.X, ALU.max, negate=True)
                        st.wait()
                        nc.vector.tensor_tensor(cexp[:, 0], logits, cmax[:, 0, :].unsqueeze(2).to_broadcast([P, 4, SLOTS]),
                                                ALU.subtract).then_inc(K["mx"], 1)

                    def back_softmax(j):
                        st = Steps(dve, bd, BD, j)
                        st.n = 6
                        dve.wait_ge(K["e"], j + 1)
                        dview = dexp[:, 0, :].rearrange("p (s t) -> p s t", s=2)
                        st.done(nc.vector.tensor_reduce(cmax[:, 1, :], cexp[:, 1], AX.X, ALU.add))
                        st.done(nc.vector.tensor_reduce(dmax[:, 1, :], dview, AX.X, ALU.add))
                        st.wait(st.n - 1)
                        st.done(nc.vector.reciprocal(cmax[:, 2, :], cmax[:, 1, :]))
                        st.wait(st.n - 1)
                        st.done(nc.vector.reciprocal(dmax[:, 2, :], dmax[:, 1, :]))
                        st.wait(st.n - 1)
                        dve.wait_ge(K["T3"], j)
                        nc.vector.tensor_tensor(cexp[:, 2], cexp[:, 1], cmax[:, 2, :].unsqueeze(2).to_broadcast([P, 4, SLOTS]), ALU.mult)
                        st.wait()
                        nc.vector.tensor_tensor(dexp[:, 1, :].rearrange("p (s t) -> p s t", s=2), dview,
                                                dmax[:, 2, :].unsqueeze(2).to_broadcast([SLOTS, 2, T]), ALU.mult).then_inc(K["cd"], 1)

                    def back_dtok(j):
                        dve.wait_ge(K["T3"], j + 1)
                        dve.wait_ge(K["x"], j)
                        nc.vector.tensor_copy(d_tok[:].rearrange("p i k -> p (i k)"), pb[5][:, 0:4 * SLOTS]).then_inc(K["dT"], 1)

                    def back_c_low(j):
                        dve.wait_ge(s_set, 1)
                        dve.wait_ge(K["ct"], j + 1)
                        nc.vector.tensor_tensor(c16_all[2 * SLOTS:3 * SLOTS, bass.ds(j, 1), :], pb[4][0:SLOTS, 0:W2T].unsqueeze(1),
                                                c16_all[0:SLOTS, bass.ds(j, 1), :], ALU.subtract).then_inc(K["cl"], 1)

                    def input_of(j, n):
                        m = NS * j + n
                        dve.wait_ge(s_B, m + 1)
                        nc.vector.tensor_tensor(inp[:, n % 2, :], pb[n % 2][:, 0:W3T], dtu[:], ALU.mult).then_inc(s_in, 1)

                    def scan_steps(j, first, last_pair):
                        take_dt(j)
                        dve.wait_ge(s_dtu, j + 1)
                        input_of(j, 0)
                        back = {0: back_yg, 3: back_residual, 4: back_norm, 9: back_max, 11: back_softmax, 13: back_dtok, 14: back_c_low}
                        front = {0: (front_norm_a,), 1: (front_norm_b,), 6: (front_conv,), 12: (front_low, front_dt)}
                        for n in range(NS):
                            m = NS * j + n
                            dve.wait_ge(s_a, m + 1)
                            dve.wait_ge(s_in, m + 1)
                            nc.vector.tensor_tensor_scan(state[:, n % 2, :], decay[:, n % 2].rearrange("p a t -> p (a t)"), inp[:, n % 2, :], 0.0,
                                                         ALU.mult, ALU.add).then_inc(s_scan, 1)
                            if n + 1 < NS:
                                input_of(j, n + 1)
                            dve.wait_ge(s_C, m + 1)
                            dve.wait_ge(s_scan, m + 1)
                            if n >= 2 or not first:
                                dve.wait_ge(s_acc, m - 1)
                            nc.vector.tensor_tensor(cstate[:, n % 2, :], pb[2 + n % 2][:, 0:W3T], state[:, n % 2, :], ALU.mult).then_inc(s_cs, 1)
                            if n in back and not first:
                                back[n](j - 1)
                            if n == 0:
                                gate(j)
                            for piece in front.get(n, ()):
                                if not last_pair:
                                    piece(j + 1)

                    nc.vector.memset(mv_f[:], 1.0)
                    nc.vector.memset(mv_b[:], 1.0)
                    nc.vector.memset(xT1[:], 1.0)
                    nc.vector.memset(uc1_n[:], 1.0)
                    nc.vector.memset(u16_n[:], 1.0)
                    nc.vector.memset(yg1[:], 1.0)
                    nc.vector.memset(u_pad[:], 0.0)
                    nc.vector.memset(decay[:], 0.0).then_inc(s_set, 1)
                    dve.wait_ge(s_set, 1)
                    front_norm_a(0)
                    front_norm_b(0)
                    front_conv(0)
                    front_low(0)
                    front_dt(0)
                    scan_steps(0, True, False)
                    scan_steps(1, False, False)
                    with dve.Fori(2, NPAIR - 1) as j:
                        scan_steps(j, False, False)
                    scan_steps(NPAIR - 1, False, True)
                    for piece in (back_yg, back_residual, back_norm, back_max, back_softmax, back_dtok, back_c_low):
                        piece(NPAIR - 1)

                @block.gpsimd
                def _(pool):
                    def front_rs(j):
                        pool.wait_ge(F["var"], j + 1)
                        pool.wait_ge(F["xn"], j)
                        nc.gpsimd.tensor_tensor(rs_f[:], ve_f[:], half4[:, 0, :], ALU.pow).then_inc(F["rs"], 1)

                    def back_pw(j):
                        pool.wait_ge(K["var"], j + 1)
                        pool.wait_ge(K["zn"], j)
                        nc.gpsimd.tensor_tensor(sm[:, 2, :], sm[:, 0, :], half4[:, 0, :], ALU.pow)
                        nc.gpsimd.tensor_tensor(sm[:, 3, :], sm[:, 1, :], half4[:, 1, :], ALU.pow).then_inc(K["pw"], 1)

                    def scan_steps(j, first, last_pair):
                        for n in range(NS):
                            m = NS * j + n
                            if n == 1 and not last_pair:
                                front_rs(j + 1)
                            if n == 4 and not first:
                                back_pw(j - 1)
                            pool.wait_ge(s_cs, m + 1)
                            if n == 0:
                                pool.wait_ge(F["y0"], j + 1)
                                pool.wait_ge(s_acc, NS * j)
                                src = y0[:].rearrange("p a t -> p (a t)")
                            else:
                                pool.wait_ge(s_acc, m)
                                src = y[:, (n - 1) % 2, :]
                            if n == 1:
                                pool.wait_ge(K["yg"], j)
                            nc.gpsimd.tensor_tensor(y[:, n % 2, :], src, cstate[:, n % 2, :], ALU.add).then_inc(s_acc, 1)

                    front_rs(0)
                    scan_steps(0, True, False)
                    scan_steps(1, False, False)
                    with pool.Fori(2, NPAIR - 1) as j:
                        scan_steps(j, False, False)
                    scan_steps(NPAIR - 1, False, True)
                    back_pw(NPAIR - 1)

        slot_experts(nc, io, sem, H, H_img, xt0, xt1, c16_all, pb)


def slot_experts(nc, io, sem, H, H_img, xt0, xt1, c16_all, pb):
    with ExitStack() as ctx:
        def sb(name, shape, dt=F32):
            return ctx.enter_context(nc.sbuf_tensor(name, shape, dt))

        wd0, wd1 = sb("wd0", [P, NE, HID]), sb("wd1", [D1 + 1, NE, HID])
        wu = sb("wu", [HID + 1, NE, D])
        hid = sb("hid", [HID + 8, NE, P])
        y_rows = sb("y_rows", [P, NE, D])
        y_halves = sb("y_halves", [P, 2, NE, D], F16)
        y_slots = sb("y_slots", [3 * SLOTS, B, D], F16)
        ct = sb("ct", [3 * SLOTS, 2, W2T], F16)
        NO = 4
        out_t, out_i = sb("out_t", [P, NO, 2, D]), sb("out_i", [N_IMG, NO, 2, D])
        x_w, x_one = sem("expert_weights"), sem("expert_ones")
        x_h, x_g, x_y, x_ye = sem("expert_hidden"), sem("expert_gelu"), sem("expert_y"), sem("expert_y_copied")
        x_scr, x_sl = sem("slots_written"), sem("slots_loaded_back")
        o_ct, o_mm, o_sum = sem("out_c_copied"), sem("out_product"), sem("out_summed")
        o_st = [sem(f"out_stored{i}") for i in range(NO)]
        out = io["out"]
        with nc.Block() as block:
            @block.sync
            def _(sp):
                sp.dma_start(wd0[:], io["wd"][0:P]).then_inc(x_w, 16)
                sp.dma_start(wd1[:], io["wd"][P:D + 1]).then_inc(x_w, 16)
                sp.dma_start(wu[:], io["wu"]).then_inc(x_w, 16)
                sp.wait_ge(x_ye, NE // 2 + 2)
                sp.dma_start(io["scratch_y"].rearrange("k e q d -> q (k e) d"), y_halves[:].rearrange("q k e d -> q (k e) d")).then_inc(x_scr, 16)
                sp.wait_ge(x_scr, 16)
                for part, k in enumerate((0, 1, 0)):
                    sp.dma_start(y_slots[part * SLOTS:(part + 1) * SLOTS],
                                 io["scratch_y"][k].rearrange("e (p b) d -> (e p) b d", p=NP_)).then_inc(x_sl, 16)

                def store(j, par):
                    sp.wait_ge(o_sum, j + 1)
                    sp.dma_start(out[bass.ds(2 * j, 2), N_IMG:T, :].rearrange("b t d -> t b d"), out_t[:, par]).then_inc(o_st[par], 16)
                    sp.dma_start(out[bass.ds(2 * j, 2), 0:N_IMG, :].rearrange("b t d -> t b d"), out_i[:, par]).then_inc(o_st[par], 16)

                with sp.Fori(0, NPAIR // NO) as i:
                    for buffer in range(NO):
                        store(NO * i + buffer, buffer)
                for stored in o_st:
                    sp.wait_ge(stored, 32 * NPAIR // NO)

            @block.tensor
            def _(pe):
                pe.wait_ge(x_w, 48)
                for e in range(NE):
                    o = pb[e // 4][0:HID, (e % 4) * P:(e % 4 + 1) * P].rearrange("h (p b) -> h p b", p=NP_)
                    for k, (wd, xt) in enumerate(((wd0, xt0), (wd1, xt1))):
                        last = nc.tensor.matmul(o, wd[:, e, :], xt[:, :, NP_ * e:NP_ * (e + 1)].rearrange("k b p -> k p b"),
                                                start=(k == 0), stop=(k == 1))
                    if e % 4 == 3:
                        last.then_inc(x_h, 1)
                for e in range(NE):
                    if e % 4 == 0:
                        pe.wait_ge(x_g, e // 4 + 1)
                    last = nc.tensor.matmul(pb[2 + e // 2][:, (e % 2) * D:(e % 2 + 1) * D], hid[0:HID + 1, e, :], wu[:, e, :], start=True, stop=True)
                    if e % 2:
                        last.then_inc(x_y, 1)
                pe.wait_ge(x_sl, 16 * 3)
                pe.wait_ge(x_ye, NE // 2)

                def product(j, par):
                    pe.wait_ge(o_ct, j + 1)
                    if not (isinstance(j, int) and j < 2):
                        pe.wait_ge(o_sum, j - 1)
                    for s in range(2):
                        rhs = y_slots[:, bass.ds(2 * j + s, 1), :].rearrange("k b d -> k (b d)")
                        c = s * T
                        nc.tensor.matmul(pb[2 * par][:, s * D:(s + 1) * D], ct[:, par, c + N_IMG:c + T], rhs, start=True, stop=True)
                        last = nc.tensor.matmul(pb[2 * par + 1][:, s * D:(s + 1) * D], ct[:, par, c:c + P], rhs, start=True, stop=True)
                    last.then_inc(o_mm, 1)

                product(0, 0)
                product(1, 1)
                with pe.Fori(1, NPAIR // 2) as i:
                    product(2 * i, 0)
                    product(2 * i + 1, 1)

            @block.scalar
            def _(act):
                act.wait_ge(x_one, 1)
                for i in range(2):
                    act.wait_ge(x_h, i + 1)
                    nc.scalar.activation(hid[0:HID, 4 * i:4 * i + 4, :], pb[i][0:HID, :].rearrange("h (e n) -> h e n", e=4), ACT.Gelu).then_inc(x_g, 1)

                def copy_c(j, par):
                    if not (isinstance(j, int) and j < 2):
                        act.wait_ge(o_mm, j - 1)
                    nc.scalar.copy(ct[:, par, :], c16_all[:, bass.ds(j, 1), :].rearrange("k a t -> k (a t)")).then_inc(o_ct, 1)

                copy_c(0, 0)
                copy_c(1, 1)
                with act.Fori(1, NPAIR // 2) as i:
                    copy_c(2 * i, 0)
                    copy_c(2 * i + 1, 1)

            @block.vector
            def _(dve):
                nc.vector.memset(hid[:], 1.0).then_inc(x_one, 1)
                for i in range(NE // 2):
                    dve.wait_ge(x_y, i + 1)
                    nc.vector.tensor_copy(y_rows[:, 2 * i:2 * i + 2, :], pb[2 + i][:, 0:2 * D].rearrange("p (e d) -> p e d", e=2)).then_inc(x_ye, 1)
                dve.wait_ge(x_ye, NE // 2)
                nc.vector.tensor_copy(y_halves[:, 0], y_rows[:]).then_inc(x_ye, 1)
                dve.wait_ge(x_ye, NE // 2 + 1)
                nc.vector.tensor_tensor(y_halves[:, 1], y_rows[:], y_halves[:, 0], ALU.subtract).then_inc(x_ye, 1)

                def total(i, buffer):
                    j = NO * i + buffer
                    par = buffer % 2
                    dve.wait_ge(o_mm, j + 1)
                    if not (isinstance(i, int) and i == 0):
                        dve.wait_ge(o_st[buffer], 32 * i)
                    nc.vector.tensor_tensor(out_t[:, buffer], pb[2 * par][:, 0:2 * D].rearrange("p (s d) -> p s d", s=2),
                                            H[:, bass.ds(2 * j, 2), :], ALU.add)
                    nc.vector.tensor_tensor(out_i[:, buffer], pb[2 * par + 1][0:N_IMG, 0:2 * D].rearrange("p (s d) -> p s d", s=2),
                                            H_img[:, bass.ds(2 * j, 2), :], ALU.add).then_inc(o_sum, 1)

                for buffer in range(NO):
                    total(0, buffer)
                with dve.Fori(1, NPAIR // NO) as i:
                    for buffer in range(NO):
                        total(i, buffer)


def ssm_layout(x):
    def bias_row(w, b):
        return np.concatenate([w, b[None]], axis=0)

    def mixed(a):
        return np.stack([a[:P], np.concatenate([a[P:], a[P:]])], axis=1)

    def by_state(w, b):
        w = bias_row(w, b)
        return np.ascontiguousarray(w.reshape(D + 1, D, NS).transpose(0, 2, 1))

    wconv = np.concatenate([x["L0_attn_Wconv"], x["L0_attn_bconv"][:, None], x["L0_attn_D"][:, None]], axis=1)
    wd = np.concatenate([x["L0_ffn_W_down"], x["L0_ffn_b_down"][:, None, :]], axis=1).transpose(1, 0, 2)
    wu = np.concatenate([x["L0_ffn_W_up"], x["L0_ffn_b_up"][:, None, :]], axis=1).transpose(1, 0, 2)
    return dict(
        wi=bias_row(x["L0_attn_Wi"], x["L0_attn_bi"]), wdt=bias_row(x["L0_attn_Wdt"], x["L0_attn_bdt"]),
        wso=bias_row(x["L0_attn_Wo"], x["L0_attn_bo"]), wB=by_state(x["L0_attn_WB"], x["L0_attn_bB"]),
        wC=by_state(x["L0_attn_WC"], x["L0_attn_bC"]), a_log=mixed(x["L0_attn_A_log"]), wconv=mixed(wconv),
        slot_params=x["L0_ffn_slot_params"].reshape(D, SLOTS), slot_scale=x["L0_ffn_scale"].reshape(1),
        wd=wd, wu=wu)


def build(nc, io):
    with ExitStack() as ctx:
        def sb(name, shape, dt=F32):
            return ctx.enter_context(nc.sbuf_tensor(name, shape, dt))

        def sem(name):
            return ctx.enter_context(nc.semaphore(name))

        H = sb("H", [P, B, D])
        H_img = sb("H_img", [N_IMG, B, D])
        ident = sb("ident", [P, P])
        ident_bf = sb("ident_bf", [P, P], BF16)
        ident_h = sb("ident_h", [P, P], F16)
        band_f = sb("band_f", [P, P])
        band = sb("band", [P, P], BF16)
        half = sb("half", [P, 1])
        s_id = sem("identity_loaded")
        with nc.Block() as block:
            @block.sync
            def _(sp):
                sp.dma_start(ident[:], io["ident"]).then_inc(s_id, 16)
                sp.dma_start(band_f[:], io["band"]).then_inc(s_id, 16)

            @block.vector
            def _(dve):
                nc.vector.memset(half[:], -0.5)
                dve.wait_ge(s_id, 32)
                nc.vector.tensor_copy(ident_bf[:], ident[:])
                nc.vector.tensor_copy(ident_h[:], ident[:])
                nc.vector.tensor_copy(band[:], band_f[:])
        consts = dict(ident=ident, ident_bf=ident_bf, ident_h=ident_h, band=band, half=half)
        image_loaded = patch_embedding(nc, io, sem, H, H_img, consts)
        text_encoder(nc, io, sem, H, image_loaded, consts)
        ssm_and_slots(nc, io, sem, H, H_img, consts)


def kernel(**inputs):
    import concourse.bacc as _bacc
    from concourse.bass_utils import run_bass_kernel_spmd as _run

    x = {k: np.asarray(v) for k, v in inputs.items()}
    far = np.abs(np.arange(P)[:, None] - np.arange(P)[None, :]) > WIN
    arrays = {**text_layout(x), **tok_layout(x), **ssm_layout(x),
              "ident": np.eye(P, dtype=np.float32), "band": np.where(far, MASKED, 0.0).astype(np.float32)}
    nc = _bacc.Bacc("TRN2", target_bir_lowering=False, num_devices=1)
    io, feeds = {}, {}
    for name, a in arrays.items():
        a = np.ascontiguousarray(a)
        feeds[f"in_{name}"] = a
        io[name] = nc.dram_tensor(f"in_{name}", a.shape, mybir.dt.from_np(a.dtype), kind="ExternalInput").ap()
    io["out"] = nc.dram_tensor("out_h", (B, T, D), F32, kind="ExternalOutput").ap()
    io["scratch_tok"] = nc.dram_tensor("scratch_tok", (6 * B, 6 * D), F32, kind="Internal").ap()
    io["scratch_y"] = nc.dram_tensor("scratch_y", (2, NE, P, D), F16, kind="Internal").ap()
    build(nc, io)
    r = _run(nc, [feeds], core_ids=[0])
    return r.results[0]["out_h"]
```
